# Optimizing a Trainium2 kernel written in Bass

```python
import numpy as np
import jax
import jax.numpy as jnp

def _softmax(x, axis=-1):
    return jax.nn.softmax(x, axis=axis)

def _gelu(x):
    return jax.nn.gelu(x, approximate=True)

def _silu(x):
    return jax.nn.silu(x)

def _sigmoid(x):
    return jax.nn.sigmoid(x)

def _layernorm(x, axis=-1, eps=1e-05):
    m = jnp.mean(x, axis=axis, keepdims=True)
    v = jnp.var(x, axis=axis, keepdims=True)
    return (x - m) / jnp.sqrt(v + eps)

def _scatter_add(tgt, idx, src, axis=0):
    return tgt.at[idx].add(src)

def _segment_sum(src, seg, n):
    return jax.ops.segment_sum(src, seg, n)
kernel_name = 'mk_vit_tower_d2_tok_img256_r4_1a9884'

def setup_inputs(seed: int=0):
    np.random.seed(seed)
    _w = jnp.asarray

    def _rec_inputs():
        import jax
        import jax.numpy as jnp
        _rk = jax.random.key(seed)
        x = -0.00040386 + 0.999972 * jax.random.normal(jax.random.fold_in(_rk, 1), (128, 128, 64, 3), jnp.float32)
        return x
    x = _rec_inputs()

    def _L0_tok_setup():
        import jax, jax.numpy as jnp
        import numpy as np
        B, T, J, LAT = (128, 128, 64, 64)
        EPS = 1e-05

        def layernorm(x, g, b):
            m = jnp.mean(x, axis=-1, keepdims=True)
            v = jnp.var(x, axis=-1, keepdims=True)
            return (x - m) * jax.lax.rsqrt(v + EPS) * g + b

        def conv2d(x, w, b, pad):
            y = jax.lax.conv_general_dilated(x, w, window_strides=(1, 1), padding=pad, dimension_numbers=('NCHW', 'OIHW', 'NCHW'))
            return y + b[None, :, None, None]
        key = jax.random.key(seed)
        ks = jax.random.split(key, 10)
        s = 0.02
        return {'x': jax.random.normal(ks[0], (B, T, J, 3), dtype=jnp.float32), 'ln0_g': jnp.ones((J * 3,), jnp.float32), 'ln0_b': jnp.zeros((J * 3,), jnp.float32), 'ln1_g': jnp.ones((J * 2,), jnp.float32), 'ln1_b': jnp.zeros((J * 2,), jnp.float32), 'conv1_w': jax.random.normal(ks[1], (T, T, 5, 3), jnp.float32) * s, 'conv1_b': jnp.zeros((T,), jnp.float32), 'conv2_w': jax.random.normal(ks[2], (T, T, 5, 2), jnp.float32) * s, 'conv2_b': jnp.zeros((T,), jnp.float32), 'conv3_w': jax.random.normal(ks[3], (2 * T, T, 5, 2), jnp.float32) * s, 'conv3_b': jnp.zeros((2 * T,), jnp.float32), 'out_w': jax.random.normal(ks[4], (2 * J, LAT), jnp.float32) * s, 'out_b': jnp.zeros((LAT,), jnp.float32)}
    _L0_tok_all = _L0_tok_setup()
    _L0_tok_in = {k: v for k, v in _L0_tok_all.items() if k in ('ln0_g', 'ln0_b', 'ln1_g', 'ln1_b', 'conv1_w', 'conv1_b', 'conv2_w', 'conv2_b', 'conv3_w', 'conv3_b', 'out_w', 'out_b')}
    del _L0_tok_all

    def _L0_attn_setup():
        import jax, jax.numpy as jnp
        import numpy as np
        B, S, D, H, K = (8, 256, 64, 8, 5)
        DK = D // H

        def _layernorm(x, w, b, eps=1e-12):
            m = x.mean(-1, keepdims=True)
            v = ((x - m) ** 2).mean(-1, keepdims=True)
            return w * (x - m) / jnp.sqrt(v + eps) + b

        def _forward(x, conv_w, conv_b, sqrt_beta, ln_w, ln_b, q_w, q_b, k_w, k_b, v_w, v_b, out_w, out_b, gammas):
            b, s, d = x.shape
            h = gammas.shape[0]
            dk = d // h
            xc = x.transpose(0, 2, 1)
            low = jax.lax.conv_general_dilated(xc, conv_w, window_strides=(1,), padding=[(K - 1, 0)], dimension_numbers=('NCH', 'OIH', 'NCH'))
            low = low.transpose(0, 2, 1) + conv_b
            high = x - low
            hid = _layernorm(low + sqrt_beta ** 2 * high + x, ln_w, ln_b)

            def proj(w, bb):
                return (hid @ w.T + bb).reshape(b, s, h, dk).transpose(0, 2, 1, 3)
            q, k, v = (proj(q_w, q_b), proj(k_w, k_b), proj(v_w, v_b))
            scores = jnp.einsum('bhqd,bhkd->bhqk', q, k) / jnp.sqrt(jnp.float32(dk))
            mask = jnp.tril(jnp.ones((s, s), bool))
            p_ = jax.nn.softmax(jnp.where(mask, scores, -1e+32), axis=-1) * mask
            distcum = jnp.cumsum(p_, axis=-1)
            disttotal = p_.sum(-1, keepdims=True)
            idx = jnp.arange(s)
            pos = jnp.abs(idx[:, None] - idx[None, :]).astype(jnp.float32)
            dist = jax.lax.stop_gradient(jnp.sqrt(jnp.clip((disttotal - distcum) * pos, 0.0)))
            gamma = -jax.nn.softplus(gammas)[None]
            total_effect = jnp.clip(jnp.exp(dist * gamma), 1e-05, 100000.0)
            scores = jnp.where(mask, scores * total_effect, -1e+32)
            p = jax.nn.softmax(scores, axis=-1)
            p = p.at[:, :, 0, :].set(0.0)
            out = jnp.einsum('bhqk,bhkd->bhqd', p, v)
            out = out.transpose(0, 2, 1, 3).reshape(b, s, d)
            return out @ out_w.T + out_b
        key = jax.random.key(seed)
        ks = jax.random.split(key, 8)
        s = 0.05
        return dict(x=jax.random.normal(ks[0], (B, S, D), jnp.float32), conv_w=jax.random.normal(ks[1], (D, D, K), jnp.float32) * s, conv_b=jnp.zeros((D,), jnp.float32), sqrt_beta=jax.random.normal(ks[2], (1, 1, D), jnp.float32), ln_w=jnp.ones((D,), jnp.float32), ln_b=jnp.zeros((D,), jnp.float32), q_w=jax.random.normal(ks[3], (D, D), jnp.float32) * s, q_b=jnp.zeros((D,), jnp.float32), k_w=jax.random.normal(ks[4], (D, D), jnp.float32) * s, k_b=jnp.zeros((D,), jnp.float32), v_w=jax.random.normal(ks[5], (D, D), jnp.float32) * s, v_b=jnp.zeros((D,), jnp.float32), out_w=jax.random.normal(ks[6], (D, D), jnp.float32) * s, out_b=jnp.zeros((D,), jnp.float32), gammas=jax.random.normal(ks[7], (H, 1, 1), jnp.float32) * 0.1)
    _L0_attn_all = _L0_attn_setup()
    _L0_attn_in = {k: v for k, v in _L0_attn_all.items() if k in ('conv_w', 'conv_b', 'sqrt_beta', 'ln_w', 'ln_b', 'q_w', 'q_b', 'k_w', 'k_b', 'v_w', 'v_b', 'out_w', 'out_b', 'gammas')}
    del _L0_attn_all

    def _L0_ffn_setup():
        import jax, jax.numpy as jnp
        import numpy as np
        NUM_EXPERTS = 8
        TOP_K = 2
        B, S, D = (8, 2048, 64)

        def _moe(tokens, router_w, w1, b1, w2, b2):
            N = tokens.shape[0]
            E = router_w.shape[0]
            logits = tokens.astype(jnp.float32) @ router_w.astype(jnp.float32).T
            probs = jax.nn.softmax(logits, axis=-1)
            rw, re = jax.lax.top_k(probs, TOP_K)
            if TOP_K > 1:
                rw = rw / jnp.maximum(rw.sum(-1, keepdims=True), 1e-12)
            rw = rw.astype(tokens.dtype)
            combine = jnp.zeros((N, E), tokens.dtype).at[jnp.arange(N)[:, None], re].set(rw)
            out = tokens
            for e in range(E):
                h = jax.nn.gelu(tokens @ w1[e] + b1[e], approximate=False)
                y = h @ w2[e] + b2[e]
                out = out + combine[:, e:e + 1] * y
            return out
        key = jax.random.key(seed)
        ks = jax.random.split(key, 4)
        scale = 1.0 / np.sqrt(D).astype(np.float32)
        return {'input_embeddings': jax.random.normal(ks[0], (B, S, D), jnp.float32), 'router_w': jax.random.normal(ks[1], (NUM_EXPERTS, D), jnp.float32) * scale, 'w1': jax.random.normal(ks[2], (NUM_EXPERTS, D, D), jnp.float32) * scale, 'b1': jnp.zeros((NUM_EXPERTS, D), jnp.float32), 'w2': jax.random.normal(ks[3], (NUM_EXPERTS, D, D), jnp.float32) * scale, 'b2': jnp.zeros((NUM_EXPERTS, D), jnp.float32)}
    _L0_ffn_all = _L0_ffn_setup()
    _L0_ffn_in = {k: v for k, v in _L0_ffn_all.items() if k in ('router_w', 'w1', 'b1', 'w2', 'b2')}
    del _L0_ffn_all

    def _L1_attn_setup():
        import math
        import jax, jax.numpy as jnp
        import numpy as np
        ROPE_DIMS = 16
        N_WIN = 16

        def rmsnorm(x, w):
            return x * jax.lax.rsqrt(jnp.mean(x * x, axis=-1, keepdims=True) + 1e-08) * w

        def apply_rope(x, negate=False):
            T = x.shape[2]
            x_pass, x_rope = (x[..., :-ROPE_DIMS], x[..., -ROPE_DIMS:])
            t = jnp.arange(T, dtype=x.dtype)
            if negate:
                t = -t
            k = jnp.arange(ROPE_DIMS // 2, dtype=x.dtype)
            theta = 10000.0 ** (-2.0 * k / ROPE_DIMS)
            freqs = t[:, None] * theta[None, :]
            cos, sin = (jnp.cos(freqs), jnp.sin(freqs))
            x1, x2 = (x_rope[..., 0::2], x_rope[..., 1::2])
            rx1 = x1 * cos - x2 * sin
            rx2 = x1 * sin + x2 * cos
            rx = jnp.stack([rx1, rx2], axis=-1).reshape(x_rope.shape)
            return jnp.concatenate([x_pass, rx], axis=-1)
        key = jax.random.key(seed)
        ks = jax.random.split(key, 14)
        B, T, d, c, nh = (4, 512, 64, 64, 4)
        s = 0.02
        return {'H': jax.random.normal(ks[0], (B, T, d), jnp.float32), 'W_Q': jax.random.normal(ks[1], (nh * c, d), jnp.float32) * s, 'W_K': jax.random.normal(ks[2], (c, d), jnp.float32) * s, 'W_V': jax.random.normal(ks[3], (c, d), jnp.float32) * s, 'wq': 1.0 + 0.1 * jax.random.normal(ks[4], (nh, c), jnp.float32), 'wk': 1.0 + 0.1 * jax.random.normal(ks[5], (c,), jnp.float32), 'wv': 1.0 + 0.1 * jax.random.normal(ks[6], (c,), jnp.float32), 'Wg0': jax.random.normal(ks[7], (64, 2 * c), jnp.float32) * s, 'bg0': jnp.zeros((64,), jnp.float32), 'Wg1': jax.random.normal(ks[8], (64, 2 * c), jnp.float32) * s, 'bg1': jnp.zeros((64,), jnp.float32), 'Wout': jax.random.normal(ks[9], (d, 128), jnp.float32) * s, 'bout': jnp.zeros((d,), jnp.float32)}
    _L1_attn_all = _L1_attn_setup()
    _L1_attn_in = {k: v for k, v in _L1_attn_all.items() if k in ('W_Q', 'W_K', 'W_V', 'wq', 'wk', 'wv', 'Wg0', 'bg0', 'Wg1', 'bg1', 'Wout', 'bout')}
    del _L1_attn_all

    def _L1_ffn_setup():
        import jax, jax.numpy as jnp
        import numpy as np
        B, T, IN_DIM = (64, 64, 64)
        HID, OUT_DIM = (128, 64)
        N_LAYERS, N_EXPERTS, N_SHARED = (2, 16, 1)
        key = jax.random.key(seed)
        ks = jax.random.split(key, 10)
        s = 0.02
        x = jax.random.normal(ks[0], (B, T, IN_DIM), dtype=jnp.float32)
        route_id = jax.random.randint(ks[1], (B,), 0, N_EXPERTS)
        Wi = jax.random.normal(ks[2], (HID, IN_DIM), dtype=jnp.float32) * s
        bi = jnp.zeros((HID,), dtype=jnp.float32)
        Wr = jax.random.normal(ks[3], (N_LAYERS, N_EXPERTS, HID, HID), dtype=jnp.float32) * s
        br = jax.random.normal(ks[4], (N_LAYERS, N_EXPERTS, HID), dtype=jnp.float32) * s
        Ws = jax.random.normal(ks[5], (N_LAYERS, N_SHARED, HID, HID), dtype=jnp.float32) * s
        bs = jax.random.normal(ks[6], (N_LAYERS, N_SHARED, HID), dtype=jnp.float32) * s
        Wo = jax.random.normal(ks[7], (OUT_DIM, HID), dtype=jnp.float32) * s
        bo = jnp.zeros((OUT_DIM,), dtype=jnp.float32)
        return {'x': x, 'route_id': route_id, 'Wi': Wi, 'bi': bi, 'Wr': Wr, 'br': br, 'Ws': Ws, 'bs': bs, 'Wo': Wo, 'bo': bo}
    _L1_ffn_all = _L1_ffn_setup()
    _L1_ffn_in = {k: v for k, v in _L1_ffn_all.items() if k in ('route_id', 'Wi', 'bi', 'Wr', 'br', 'Ws', 'bs', 'Wo', 'bo')}
    del _L1_ffn_all
    return {'x': x, 'L0_tok_ln0_g': _L0_tok_in['ln0_g'], 'L0_tok_ln0_b': _L0_tok_in['ln0_b'], 'L0_tok_ln1_g': _L0_tok_in['ln1_g'], 'L0_tok_ln1_b': _L0_tok_in['ln1_b'], 'L0_tok_conv1_w': _L0_tok_in['conv1_w'], 'L0_tok_conv1_b': _L0_tok_in['conv1_b'], 'L0_tok_conv2_w': _L0_tok_in['conv2_w'], 'L0_tok_conv2_b': _L0_tok_in['conv2_b'], 'L0_tok_conv3_w': _L0_tok_in['conv3_w'], 'L0_tok_conv3_b': _L0_tok_in['conv3_b'], 'L0_tok_out_w': _L0_tok_in['out_w'], 'L0_tok_out_b': _L0_tok_in['out_b'], 'L0_attn_conv_w': _L0_attn_in['conv_w'], 'L0_attn_conv_b': _L0_attn_in['conv_b'], 'L0_attn_sqrt_beta': _L0_attn_in['sqrt_beta'], 'L0_attn_ln_w': _L0_attn_in['ln_w'], 'L0_attn_ln_b': _L0_attn_in['ln_b'], 'L0_attn_q_w': _L0_attn_in['q_w'], 'L0_attn_q_b': _L0_attn_in['q_b'], 'L0_attn_k_w': _L0_attn_in['k_w'], 'L0_attn_k_b': _L0_attn_in['k_b'], 'L0_attn_v_w': _L0_attn_in['v_w'], 'L0_attn_v_b': _L0_attn_in['v_b'], 'L0_attn_out_w': _L0_attn_in['out_w'], 'L0_attn_out_b': _L0_attn_in['out_b'], 'L0_attn_gammas': _L0_attn_in['gammas'], 'L0_ffn_router_w': _L0_ffn_in['router_w'], 'L0_ffn_w1': _L0_ffn_in['w1'], 'L0_ffn_b1': _L0_ffn_in['b1'], 'L0_ffn_w2': _L0_ffn_in['w2'], 'L0_ffn_b2': _L0_ffn_in['b2'], 'L1_attn_W_Q': _L1_attn_in['W_Q'], 'L1_attn_W_K': _L1_attn_in['W_K'], 'L1_attn_W_V': _L1_attn_in['W_V'], 'L1_attn_wq': _L1_attn_in['wq'], 'L1_attn_wk': _L1_attn_in['wk'], 'L1_attn_wv': _L1_attn_in['wv'], 'L1_attn_Wg0': _L1_attn_in['Wg0'], 'L1_attn_bg0': _L1_attn_in['bg0'], 'L1_attn_Wg1': _L1_attn_in['Wg1'], 'L1_attn_bg1': _L1_attn_in['bg1'], 'L1_attn_Wout': _L1_attn_in['Wout'], 'L1_attn_bout': _L1_attn_in['bout'], 'L1_ffn_route_id': _L1_ffn_in['route_id'], 'L1_ffn_Wi': _L1_ffn_in['Wi'], 'L1_ffn_bi': _L1_ffn_in['bi'], 'L1_ffn_Wr': _L1_ffn_in['Wr'], 'L1_ffn_br': _L1_ffn_in['br'], 'L1_ffn_Ws': _L1_ffn_in['Ws'], 'L1_ffn_bs': _L1_ffn_in['bs'], 'L1_ffn_Wo': _L1_ffn_in['Wo'], 'L1_ffn_bo': _L1_ffn_in['bo']}

def reference(x, L0_tok_ln0_g, L0_tok_ln0_b, L0_tok_ln1_g, L0_tok_ln1_b, L0_tok_conv1_w, L0_tok_conv1_b, L0_tok_conv2_w, L0_tok_conv2_b, L0_tok_conv3_w, L0_tok_conv3_b, L0_tok_out_w, L0_tok_out_b, L0_attn_conv_w, L0_attn_conv_b, L0_attn_sqrt_beta, L0_attn_ln_w, L0_attn_ln_b, L0_attn_q_w, L0_attn_q_b, L0_attn_k_w, L0_attn_k_b, L0_attn_v_w, L0_attn_v_b, L0_attn_out_w, L0_attn_out_b, L0_attn_gammas, L0_ffn_router_w, L0_ffn_w1, L0_ffn_b1, L0_ffn_w2, L0_ffn_b2, L1_attn_W_Q, L1_attn_W_K, L1_attn_W_V, L1_attn_wq, L1_attn_wk, L1_attn_wv, L1_attn_Wg0, L1_attn_bg0, L1_attn_Wg1, L1_attn_bg1, L1_attn_Wout, L1_attn_bout, L1_ffn_route_id, L1_ffn_Wi, L1_ffn_bi, L1_ffn_Wr, L1_ffn_br, L1_ffn_Ws, L1_ffn_bs, L1_ffn_Wo, L1_ffn_bo):
    import jax
    import jax.numpy as jnp

    def _L0_tok_ref(x, ln0_g, ln0_b, ln1_g, ln1_b, conv1_w, conv1_b, conv2_w, conv2_b, conv3_w, conv3_b, out_w, out_b):
        import jax, jax.numpy as jnp
        import numpy as np
        B, T, J, LAT = (128, 128, 64, 64)
        EPS = 1e-05

        def layernorm(x, g, b):
            m = jnp.mean(x, axis=-1, keepdims=True)
            v = jnp.var(x, axis=-1, keepdims=True)
            return (x - m) * jax.lax.rsqrt(v + EPS) * g + b

        def conv2d(x, w, b, pad):
            y = jax.lax.conv_general_dilated(x, w, window_strides=(1, 1), padding=pad, dimension_numbers=('NCHW', 'OIHW', 'NCHW'))
            return y + b[None, :, None, None]
        b, t, j, d = x.shape
        h = layernorm(x.reshape(b, t, j * 3), ln0_g, ln0_b).reshape(b, t, j, 3)
        h = jax.nn.relu(conv2d(h, conv1_w, conv1_b, ((2, 2), (1, 1))))
        h = layernorm(h.reshape(b, t, j * 3), ln0_g, ln0_b).reshape(b, t, j, 3)
        h = jax.nn.relu(conv2d(h, conv2_w, conv2_b, ((2, 2), (0, 0))))
        h = layernorm(h.reshape(b, t, j * 2), ln1_g, ln1_b).reshape(b, t, j, 2)
        h = jax.nn.relu(conv2d(h, conv3_w, conv3_b, ((2, 2), (0, 0))))
        h = h.reshape(b, 2 * t, j)
        res = jnp.concatenate([h[:, :t, :], h[:, t:, :]], axis=2)
        res = layernorm(res, ln1_g, ln1_b)
        return res @ out_w + out_b

    def _L0_attn_ref(x, conv_w, conv_b, sqrt_beta, ln_w, ln_b, q_w, q_b, k_w, k_b, v_w, v_b, out_w, out_b, gammas):
        import jax, jax.numpy as jnp
        import numpy as np
        B, S, D, H, K = (8, 256, 64, 8, 5)
        DK = D // H

        def _layernorm(x, w, b, eps=1e-12):
            m = x.mean(-1, keepdims=True)
            v = ((x - m) ** 2).mean(-1, keepdims=True)
            return w * (x - m) / jnp.sqrt(v + eps) + b

        def _forward(x, conv_w, conv_b, sqrt_beta, ln_w, ln_b, q_w, q_b, k_w, k_b, v_w, v_b, out_w, out_b, gammas):
            b, s, d = x.shape
            h = gammas.shape[0]
            dk = d // h
            xc = x.transpose(0, 2, 1)
            low = jax.lax.conv_general_dilated(xc, conv_w, window_strides=(1,), padding=[(K - 1, 0)], dimension_numbers=('NCH', 'OIH', 'NCH'))
            low = low.transpose(0, 2, 1) + conv_b
            high = x - low
            hid = _layernorm(low + sqrt_beta ** 2 * high + x, ln_w, ln_b)

            def proj(w, bb):
                return (hid @ w.T + bb).reshape(b, s, h, dk).transpose(0, 2, 1, 3)
            q, k, v = (proj(q_w, q_b), proj(k_w, k_b), proj(v_w, v_b))
            scores = jnp.einsum('bhqd,bhkd->bhqk', q, k) / jnp.sqrt(jnp.float32(dk))
            mask = jnp.tril(jnp.ones((s, s), bool))
            p_ = jax.nn.softmax(jnp.where(mask, scores, -1e+32), axis=-1) * mask
            distcum = jnp.cumsum(p_, axis=-1)
            disttotal = p_.sum(-1, keepdims=True)
            idx = jnp.arange(s)
            pos = jnp.abs(idx[:, None] - idx[None, :]).astype(jnp.float32)
            dist = jax.lax.stop_gradient(jnp.sqrt(jnp.clip((disttotal - distcum) * pos, 0.0)))
            gamma = -jax.nn.softplus(gammas)[None]
            total_effect = jnp.clip(jnp.exp(dist * gamma), 1e-05, 100000.0)
            scores = jnp.where(mask, scores * total_effect, -1e+32)
            p = jax.nn.softmax(scores, axis=-1)
            p = p.at[:, :, 0, :].set(0.0)
            out = jnp.einsum('bhqk,bhkd->bhqd', p, v)
            out = out.transpose(0, 2, 1, 3).reshape(b, s, d)
            return out @ out_w.T + out_b
        return _forward(x, conv_w, conv_b, sqrt_beta, ln_w, ln_b, q_w, q_b, k_w, k_b, v_w, v_b, out_w, out_b, gammas)

    def _L0_ffn_ref(input_embeddings, router_w, w1, b1, w2, b2):
        import jax, jax.numpy as jnp
        import numpy as np
        NUM_EXPERTS = 8
        TOP_K = 2
        B, S, D = (8, 2048, 64)

        def _moe(tokens, router_w, w1, b1, w2, b2):
            N = tokens.shape[0]
            E = router_w.shape[0]
            logits = tokens.astype(jnp.float32) @ router_w.astype(jnp.float32).T
            probs = jax.nn.softmax(logits, axis=-1)
            rw, re = jax.lax.top_k(probs, TOP_K)
            if TOP_K > 1:
                rw = rw / jnp.maximum(rw.sum(-1, keepdims=True), 1e-12)
            rw = rw.astype(tokens.dtype)
            combine = jnp.zeros((N, E), tokens.dtype).at[jnp.arange(N)[:, None], re].set(rw)
            out = tokens
            for e in range(E):
                h = jax.nn.gelu(tokens @ w1[e] + b1[e], approximate=False)
                y = h @ w2[e] + b2[e]
                out = out + combine[:, e:e + 1] * y
            return out
        b, s, d = input_embeddings.shape
        tokens = input_embeddings.reshape(b * s, d)
        return _moe(tokens, router_w, w1, b1, w2, b2).reshape(b, s, d)

    def _L1_attn_ref(H, W_Q, W_K, W_V, wq, wk, wv, Wg0, bg0, Wg1, bg1, Wout, bout):
        import math
        import jax, jax.numpy as jnp
        import numpy as np
        ROPE_DIMS = 16
        N_WIN = 16

        def rmsnorm(x, w):
            return x * jax.lax.rsqrt(jnp.mean(x * x, axis=-1, keepdims=True) + 1e-08) * w

        def apply_rope(x, negate=False):
            T = x.shape[2]
            x_pass, x_rope = (x[..., :-ROPE_DIMS], x[..., -ROPE_DIMS:])
            t = jnp.arange(T, dtype=x.dtype)
            if negate:
                t = -t
            k = jnp.arange(ROPE_DIMS // 2, dtype=x.dtype)
            theta = 10000.0 ** (-2.0 * k / ROPE_DIMS)
            freqs = t[:, None] * theta[None, :]
            cos, sin = (jnp.cos(freqs), jnp.sin(freqs))
            x1, x2 = (x_rope[..., 0::2], x_rope[..., 1::2])
            rx1 = x1 * cos - x2 * sin
            rx2 = x1 * sin + x2 * cos
            rx = jnp.stack([rx1, rx2], axis=-1).reshape(x_rope.shape)
            return jnp.concatenate([x_pass, rx], axis=-1)
        B, T, d = H.shape
        nh, c = wq.shape
        Q = (H @ W_Q.T).reshape(B, T, nh, c).transpose(0, 2, 1, 3)
        K = (H @ W_K.T)[:, None]
        V = (H @ W_V.T)[:, None]
        Q = rmsnorm(Q, wq[None, :, None, :])
        K = rmsnorm(K, wk)
        V = rmsnorm(V, wv)
        Q = apply_rope(Q)
        K = apply_rope(K)[:, 0]
        V = apply_rope(V)[:, 0]
        S = jnp.einsum('bhtc,bsc->bhts', Q, K) / math.sqrt(c)
        i = jnp.arange(T)[:, None]
        j = jnp.arange(T)[None, :]
        allowed = (j <= i) & (j >= i - (N_WIN - 1))
        S = jnp.where(allowed, S, -jnp.inf)
        P = jax.nn.softmax(S, axis=-1)
        O = jnp.einsum('bhts,bsc->bhtc', P, V)
        O = apply_rope(O, negate=True)
        O_g0 = O[:, :2].transpose(0, 2, 1, 3).reshape(B, T, 2 * c)
        O_g1 = O[:, 2:].transpose(0, 2, 1, 3).reshape(B, T, 2 * c)
        p0 = O_g0 @ Wg0.T + bg0
        p1 = O_g1 @ Wg1.T + bg1
        p_all = jnp.concatenate([p0, p1], axis=-1)
        return p_all @ Wout.T + bout

    def _L1_ffn_ref(x, route_id, Wi, bi, Wr, br, Ws, bs, Wo, bo):
        import jax, jax.numpy as jnp
        import numpy as np
        B, T, IN_DIM = (64, 64, 64)
        HID, OUT_DIM = (128, 64)
        N_LAYERS, N_EXPERTS, N_SHARED = (2, 16, 1)
        flat = x.reshape(-1, x.shape[-1])
        n_tok = flat.shape[0]
        route = jnp.repeat(route_id, n_tok // route_id.shape[0])
        h = jax.nn.relu(flat @ Wi.T + bi)
        n_layers, n_experts = (Wr.shape[0], Wr.shape[1])
        for l in range(n_layers):
            shared = (jnp.einsum('nd,shd->snh', h, Ws[l]) + bs[l][:, None, :]).mean(axis=0)
            routed = jnp.zeros_like(h)
            for e in range(n_experts):
                ye = h @ Wr[l, e].T + br[l, e]
                routed = routed + jnp.where((route == e)[:, None], ye, 0.0)
            h = jax.nn.relu(shared + routed + h)
        out = h @ Wo.T + bo
        return out.reshape(*x.shape[:-1], out.shape[-1])
    h = _L0_tok_ref(x, L0_tok_ln0_g, L0_tok_ln0_b, L0_tok_ln1_g, L0_tok_ln1_b, L0_tok_conv1_w, L0_tok_conv1_b, L0_tok_conv2_w, L0_tok_conv2_b, L0_tok_conv3_w, L0_tok_conv3_b, L0_tok_out_w, L0_tok_out_b)
    h = h + _L0_attn_ref(_layernorm(h, axis=-1), L0_attn_conv_w, L0_attn_conv_b, L0_attn_sqrt_beta, L0_attn_ln_w, L0_attn_ln_b, L0_attn_q_w, L0_attn_q_b, L0_attn_k_w, L0_attn_k_b, L0_attn_v_w, L0_attn_v_b, L0_attn_out_w, L0_attn_out_b, L0_attn_gammas)
    h = h + _L0_ffn_ref(_layernorm(h, axis=-1), L0_ffn_router_w, L0_ffn_w1, L0_ffn_b1, L0_ffn_w2, L0_ffn_b2)
    h = h + _L1_attn_ref(_layernorm(h, axis=-1), L1_attn_W_Q, L1_attn_W_K, L1_attn_W_V, L1_attn_wq, L1_attn_wk, L1_attn_wv, L1_attn_Wg0, L1_attn_bg0, L1_attn_Wg1, L1_attn_bg1, L1_attn_Wout, L1_attn_bout)
    h = h + _L1_ffn_ref(_layernorm(h, axis=-1), L1_ffn_route_id, L1_ffn_Wi, L1_ffn_bi, L1_ffn_Wr, L1_ffn_br, L1_ffn_Ws, L1_ffn_bs, L1_ffn_Wo, L1_ffn_bo)
    return h

_drawn_inputs = setup_inputs


def setup_inputs(seed=0):
    import zlib

    import numpy as np

    out = dict(_drawn_inputs(seed))
    spreads = {'L0_tok_ln0_g': (1.0, 0.2),
     'L0_tok_ln0_b': (0.0, 0.1),
     'L0_tok_ln1_g': (1.0, 0.2),
     'L0_tok_ln1_b': (0.0, 0.1),
     'L0_tok_conv1_b': (0.0, 0.1),
     'L0_tok_conv2_b': (0.0, 0.1),
     'L0_tok_conv3_b': (0.0, 0.1),
     'L0_tok_out_b': (0.0, 0.1),
     'L0_attn_conv_b': (0.0, 0.1),
     'L0_attn_ln_w': (1.0, 0.2),
     'L0_attn_ln_b': (0.0, 0.1),
     'L0_attn_q_b': (0.0, 0.78),
     'L0_attn_k_b': (0.0, 0.8),
     'L0_attn_v_b': (0.0, 0.1),
     'L0_attn_out_b': (0.0, 0.1),
     'L0_ffn_b1': (0.0, 0.1),
     'L0_ffn_b2': (0.0, 0.1),
     'L1_attn_bg0': (0.0, 0.787),
     'L1_attn_bg1': (0.0, 0.781),
     'L1_attn_bout': (0.0, 0.1),
     'L1_ffn_bi': (0.0, 0.8),
     'L1_ffn_bo': (0.0, 0.1)}
    factors = {'L0_attn_gammas': 8.0,
     'L1_attn_W_Q': 6.701,
     'L1_attn_W_K': 6.77,
     'L1_attn_wq': 8.0,
     'L1_attn_wk': 8.0,
     'L1_attn_wv': 8.0,
     'L1_attn_Wg0': 3.779,
     'L1_attn_Wg1': 3.619,
     'L1_ffn_Wi': 3.62,
     'L1_ffn_Wr': 8.0,
     'L1_ffn_br': 8.0,
     'L1_ffn_Ws': 8.0,
     'L1_ffn_bs': 8.0}
    for name, (base, spread) in spreads.items():
        noise = np.random.default_rng([zlib.crc32(name.encode()), seed]).standard_normal(out[name].shape)
        drawn = base * np.exp(spread * noise) if base else spread * noise
        out[name] = jnp.asarray(drawn.astype(out[name].dtype))
    for name, factor in factors.items():
        out[name] = (out[name] * factor).astype(out[name].dtype)
    return out
```

```python
from contextlib import ExitStack

import concourse.bass as bass
import numpy as np
from concourse import mybir

F32 = mybir.dt.float32
BF16 = mybir.dt.bfloat16
I32 = mybir.dt.int32
ALU = mybir.AluOpType
ACT = mybir.ActivationFunctionType
AX_X = mybir.AxisListType.X

B, T, J, D = 128, 128, 64, 64
PAIRS = B // 2
HALF = T // 2
H0, DK = 8, 8
SL, SH = H0 * HALF, H0 * T
SA = SL + SH
NEXP = 8
NH1, C1, WIN, ROT = 4, 64, 16, 16
QB = 32
NBLK = 2 * T // QB
KW = QB + WIN
HID, NRT = 128, 16
EPS = 1e-5


def after(eng, sem, count):
    if isinstance(count, int) and count <= 0:
        return
    eng.wait_ge(sem, count)


def after_all(eng, carrier, *waits):
    for sem, n in waits:
        after(eng, sem, n)
    if any(not isinstance(n, int) for _, n in waits):
        carrier()


def each_pair(eng, depth, body):
    peel = max(2, depth + depth % 2)
    for t in range(peel):
        body(t, t % 2, lambda d, t=t: 0 <= t - d)
    with eng.Fori(peel, PAIRS - 1, 2) as i:
        body(i, 0, lambda d: True)
        body(i + 1, 1, lambda d: True)
    for t in range(PAIRS, PAIRS + depth):
        body(t, t % 2, lambda d, t=t: t - d < PAIRS)


def tower(nc, a, out):
    ctx = ExitStack()
    with ctx:
        def sb(name, shape, dt=F32, c=ctx):
            return c.enter_context(nc.sbuf_tensor(name, shape, dt))

        stage_sems = []

        def sem(name):
            stage_sems.append(nc.alloc_semaphore(name))
            return stage_sems[-1]

        def end_stage():
            nc.clear_and_free_semaphores(list(stage_sems))
            stage_sems.clear()
            nc.all_engine_barrier()

        psum = ctx.enter_context(nc.psum_tensor("psum", [128, 8, 512], F32))
        h_all = sb("h_all", [128, PAIRS, 2, D])
        ident = sb("ident", [128, 128])
        setup = sem("setup")
        st = Stage(nc, a, out, sb, sem, psum, h_all, ident)
        with nc.Block() as block:
            @block.sync
            def _(sp):
                sp.dma_start(ident[:], a["c_ident"]).then_inc(setup, 16)
                sp.wait_ge(setup, 16)
        with ExitStack() as c:
            token_stage(st, c)
        end_stage()
        with ExitStack() as c:
            distance_attention_stage(st, c)
        end_stage()
        with ExitStack() as c:
            mixture_stage(st, c)
        end_stage()
        with ExitStack() as c:
            window_attention_stage(st, c)
        end_stage()
        with ExitStack() as c:
            routed_stage(st, c)


class Stage:
    def __init__(self, nc, a, out, sb, sem, psum, h_all, ident):
        self.nc, self.a, self.out, self.sb, self.sem = nc, a, out, sb, sem
        self.psum, self.h_all, self.ident = psum, h_all, ident


def token_stage(st, c):
    nc, a, psum, h_all, ident = st.nc, st.a, st.psum, st.h_all, st.ident

    def sb(n, s, dt=F32):
        return st.sb(n, s, dt, c)

    def sem(n):
        return st.sem(n)

    w1 = sb("w1", [128, 15, 128])
    w2 = sb("w2", [128, 10, 128])
    w3 = sb("w3", [128, 10, 256])
    bias = sb("conv_bias", [128, 4])
    ln0 = sb("ln0", [128, 2, 3, J])
    ln1 = sb("ln1", [128, 2, 2, J])
    ln1c = sb("ln1c", [128, 2])
    wout = sb("wout", [128, D])
    woutg = sb("woutg", [128, D])
    beta_rep = sb("beta_rep", [128, 128])
    bias_out = sb("bias_out", [128, D])
    ones = sb("ones_t", [128, 128])
    xin = sb("xin", [128, 2, 2, J * 3])
    cin1 = sb("cin1", [128, 2, 3, 2, J + 4])
    cin2 = sb("cin2", [128, 2, 3, 2, J + 4])
    cin3 = sb("cin3", [128, 2, 2, 2, J + 4])
    y1 = sb("y1", [128, 2, 3, 2, J])
    y2 = sb("y2", [128, 2, 2, 2, J])
    y3 = sb("y3", [128, 2, 2, 2, J])
    s0 = sb("s0", [128, 3, 2, J])
    s1 = sb("s1", [128, 3, 2, J])
    s2 = sb("s2", [128, 2, 2, J])
    resn = sb("resn", [128, 2, 2, 128])
    resT = sb("resT", [128, 2, 256])
    scrap = sb("scrap_t", [128, 1])
    stats = sb("stats_t", [128, 8, 6])
    mv = sb("mv_t", [128, 8, 2])
    lnv = sb("lnv_t", [128, 8])
    rstd = sb("rstd_t", [128, 8])
    p1, p2, p3, pT, pO = (psum[:, k] for k in range(5))
    c1 = p1[:, 0:384].rearrange("p (w g j) -> p w g j", w=3, g=2)
    c2 = p2[:, 0:256].rearrange("p (w g j) -> p w g j", w=2, g=2)
    c3 = p3[:, 0:256].rearrange("p (h g j) -> p h g j", h=2, g=2)

    loaded, zeroed = sem("tok_loaded"), sem("tok_zeroed")
    folded, bias_mm = sem("tok_folded"), sem("tok_bias_mm")
    x_loaded = [sem("x_loaded0"), sem("x_loaded1")]
    stats_done, var_ready, ln_done, rstd_ready = sem("stats_done"), sem("var_ready"), sem("ln_done"), sem("rstd_ready")
    scaled, normed = sem("scaled"), sem("normed")
    conv1_done, conv2_done, conv3_done = sem("conv1_done"), sem("conv2_done"), sem("conv3_done")
    act1, act2, act3 = sem("act1"), sem("act2"), sem("act3")
    res_turned, resT_ready, projected, h_written = sem("res_turned"), sem("resT_ready"), sem("projected"), sem("h_written")
    consts = [(w1[:], a["w1"]), (w2[:], a["w2"]), (w3[:], a["w3"]), (bias[:], a["conv_bias"]),
              (ln0[:], a["ln0"].partition_broadcast(128)), (ln1[:], a["ln1"].partition_broadcast(128)),
              (ln1c[:], a["ln1c"]), (wout[:], a["out_w"]),
              (bias_out[:], a["out_b"].partition_broadcast(128))]

    with nc.Block() as block:
        @block.sync
        def _(sp):
            for dst, src in consts:
                sp.dma_start(dst, src).then_inc(loaded, 16)

            def body(t, par, live):
                if live(0) and not (isinstance(t, int) and t >= PAIRS):
                    after(sp, scaled, t - 1)
                    sp.dma_start(xin[:, par], a["x"][bass.ds(2 * t, 2)].rearrange("g t k -> t g k")).then_inc(x_loaded[par], 16)
            each_pair(sp, 0, body)

        @block.gpsimd
        def _(pool):
            for buf in (cin1, cin2, cin3):
                pool.memset(buf[:], 0.0).then_inc(zeroed, 1)
            pool.memset(mv[:], 1.0).then_inc(zeroed, 1)
            pool.memset(ones[:], 1.0).then_inc(zeroed, 1)

        @block.vector
        def _(dve):
            def carry():
                dve.tensor_copy(scrap[:], ident[:, 0:1])

            dve.wait_ge(loaded, 16 * len(consts))
            dve.wait_ge(zeroed, 5)
            dve.tensor_scalar(woutg[:], wout[:], ln1c[:, 0:1], None, ALU.mult).then_inc(folded, 1)
            dve.tensor_scalar(beta_rep[:], ones[:], ln1c[:, 1:2], None, ALU.mult).then_inc(folded, 1)
            dve.wait_ge(bias_mm, 1)
            dve.tensor_tensor(bias_out[:], pO[:, 0:D], bias_out[:], ALU.add).then_inc(folded, 1)
            dve.wait_ge(folded, 3)

            def body(t, par, live):
                q = 1 - par
                last = None
                if live(0) and not (isinstance(t, int) and t >= PAIRS):
                    after(dve, x_loaded[par], (t // 2 + 1) * 16 if isinstance(t, int) else (t + (2 - par)) * 8)
                    for g in range(2):
                        last = dve.bn_stats(stats[:, g], xin[:, par, g])
                if live(2):
                    after(dve, act1, t - 1)
                    for g in range(2):
                        last = dve.bn_stats(stats[:, 2 + g], y1[:, par, :, g])
                if live(4):
                    after(dve, act2, t - 3)
                    for g in range(2):
                        last = dve.bn_stats(stats[:, 4 + g], y2[:, par, :, g])
                if live(6):
                    after(dve, act3, t - 5)
                    for g in range(2):
                        last = dve.bn_stats(stats[:, 6 + g], y3[:, par, g])
                if last is not None:
                    last.then_inc(stats_done, 1)
                    after_all(dve, carry, (stats_done, t + 1))
                    slots = [k for k in range(4) if live(2 * k) and not (k == 0 and isinstance(t, int) and t >= PAIRS)]
                    for k in slots:
                        for g in (2 * k, 2 * k + 1):
                            last = dve.bn_aggr(mv[:, g], stats[:, g])
                    last.then_inc(var_ready, 1)
                    dve.wait_ge(var_ready, t + 1)
                    last = None
                    for k, (src, dst, gam) in enumerate(((xin[:, par].rearrange("p g (j w) -> p w g j", w=3), s0, ln0),
                                                         (y1[:, par], s1, ln0), (y2[:, par], s2, ln1))):
                        if k in slots:
                            for g in range(2):
                                last = dve.scalar_tensor_tensor(out=dst[:, :, g], in0=src[:, :, g], scalar=mv[:, 2 * k + g, 0:1],
                                                                in1=gam[:, 0], op0=ALU.subtract, op1=ALU.mult)
                    if last is not None:
                        last.then_inc(scaled, 1)
                        dve.wait_ge(scaled, t + 1)
                    dve.wait_ge(rstd_ready, t + 1)
                    if 0 in slots:
                        after(dve, conv1_done, t - 1)
                    if 1 in slots:
                        after(dve, conv2_done, t - 3)
                    if 2 in slots:
                        after(dve, conv3_done, t - 5)
                    for k, (src, dst, gam) in enumerate(((s0, cin1, ln0), (s1, cin2, ln0), (s2, cin3, ln1))):
                        if k in slots:
                            for g in range(2):
                                last = dve.scalar_tensor_tensor(out=dst[:, par, :, g, 2:2 + J], in0=src[:, :, g], scalar=rstd[:, 2 * k + g:2 * k + g + 1],
                                                                in1=gam[:, 1], op0=ALU.mult, op1=ALU.add)
                    if 3 in slots:
                        after(dve, res_turned, t - 7)
                        for g in range(2):
                            last = dve.tensor_scalar(resn[:, par, g], y3[:, par, g].rearrange("p h j -> p (h j)"), mv[:, 6 + g, 0:1], rstd[:, 6 + g:7 + g],
                                                     ALU.subtract, ALU.mult)
                    last.then_inc(normed, 1)
                if live(7):
                    after(dve, projected, t - 6)
                    dve.tensor_tensor(h_all[:, bass.ds(t - 7, 1)].rearrange("p u s d -> p (u s) d"),
                                      pO[:, 0:128].rearrange("p (s d) -> p s d", s=2),
                                      bias_out[:].unsqueeze(1).to_broadcast([128, 2, D]), ALU.add).then_inc(h_written, 1)
            each_pair(dve, 8, body)

        @block.scalar
        def _(act):
            act.preload_act_table_set("natural_log_exp_and_others")
            act.wait_ge(loaded, 16 * len(consts))

            def body(t, par, live):
                q = 1 - par
                if live(6) if isinstance(t, int) and t >= PAIRS else True:
                    act.wait_ge(var_ready, t + 1)
                    act.activation(lnv[:], mv[:, :, 1], ACT.Ln, bias=EPS).then_inc(ln_done, 1)
                    act.wait_ge(ln_done, t + 1)
                    act.activation(rstd[:], lnv[:], ACT.Exp, scale=-0.5).then_inc(rstd_ready, 1)
                if live(1):
                    after(act, conv1_done, t)
                    after(act, normed, t - 0)
                    act.activation(y1[:, q], c1, ACT.Relu, bias=bias[:, 0:1]).then_inc(act1, 1)
                if live(3):
                    after(act, conv2_done, t - 2)
                    act.activation(y2[:, q], c2, ACT.Relu, bias=bias[:, 1:2]).then_inc(act2, 1)
                if live(7):
                    after(act, res_turned, t - 6)
                    after(act, projected, t - 8)
                    act.activation(resT[:, q].rearrange("p (s g t) -> p g s t", s=2, g=2),
                                   pT[:, 0:256].rearrange("p (g s t) -> p g s t", g=2, s=2), ACT.Copy).then_inc(resT_ready, 1)
                if live(5):
                    after(act, conv3_done, t - 4)
                    act.activation(y3[:, q, :, 0], c3[:, 0], ACT.Relu, bias=bias[:, 2:3])
                    act.activation(y3[:, q, :, 1], c3[:, 1], ACT.Relu, bias=bias[:, 3:4]).then_inc(act3, 1)
            each_pair(act, 8, body)

        @block.tensor
        def _(pe):
            pe.wait_ge(loaded, 16 * len(consts))
            pe.wait_ge(folded, 2)
            pe.matmul(pO[:, 0:D], beta_rep[:], wout[:], start=True, stop=True).then_inc(bias_mm, 1)
            pe.wait_ge(folded, 3)
            taps1 = [(kh, kw) for kw in (1, 0, 2) for kh in range(5)]
            taps2 = [(kh, kw) for kw in range(2) for kh in range(5)]

            def body(t, par, live):
                q = 1 - par
                if live(1):
                    pe.wait_ge(normed, t)
                    after(pe, act1, t - 1)
                    for n, (kh, kw) in enumerate(taps1):
                        lo, hi = max(0, 1 - kw), min(3, 4 - kw)
                        mm = pe.matmul(c1[:, lo:hi], w1[:, kh * 3 + kw], cin1[:, q, lo + kw - 1:hi + kw - 1, :, kh:kh + J],
                                       start=n == 0, stop=n == len(taps1) - 1)
                    mm.then_inc(conv1_done, 1)
                if live(3):
                    pe.wait_ge(normed, t)
                    after(pe, act2, t - 3)
                    for n, (kh, kw) in enumerate(taps2):
                        mm = pe.matmul(c2, w2[:, kh * 2 + kw], cin2[:, q, kw:kw + 2, :, kh:kh + J], start=n == 0, stop=n == len(taps2) - 1)
                    mm.then_inc(conv2_done, 1)
                if live(7):
                    pe.wait_ge(normed, t)
                    after(pe, resT_ready, t - 7)
                    for g in range(2):
                        mm = pe.transpose(pT[:, g * 128:(g + 1) * 128], resn[:, q, g], ident[:])
                    mm.then_inc(res_turned, 1)
                if live(5):
                    pe.wait_ge(normed, t)
                    after(pe, act3, t - 5)
                    for m in range(2):
                        for n, (kh, kw) in enumerate(taps2):
                            mm = pe.matmul(c3[:, m], w3[:, kh * 2 + kw, m * 128:(m + 1) * 128], cin3[:, q, kw, :, kh:kh + J],
                                           start=n == 0, stop=n == len(taps2) - 1)
                    mm.then_inc(conv3_done, 1)
                if live(7):
                    after(pe, resT_ready, t - 6)
                    after(pe, h_written, t - 7)
                    for s in range(2):
                        mm = pe.matmul(pO[:, s * D:(s + 1) * D], resT[:, q, s * 128:(s + 1) * 128], woutg[:], start=True, stop=True)
                    mm.then_inc(projected, 1)
            each_pair(pe, 8, body)


def distance_attention_stage(st, c):
    nc, a, psum, h_all, ident = st.nc, st.a, st.psum, st.h_all, st.ident

    def sb(n, s, dt=F32):
        return st.sb("at_" + n, s, dt, c)

    def sem(n):
        return st.sem("at_" + n)

    convw = sb("convw", [65, 5, D])
    beta, bsq, omb, opb = sb("beta", [65, D]), sb("bsq", [65, D]), sb("omb", [65, D]), sb("opb", [65, D])
    diag = sb("diag", [64, D])
    wraw, waug = sb("wraw", [65, 576]), sb("waug", [65, 576])
    lnw, lnb_sel = sb("lnw", [65, 1]), sb("lnb_sel", [64, 65])
    wo = sb("wo", [65, D])
    gam, gtmp, gsq = sb("gam", [128, H0]), sb("gtmp", [128, H0]), sb("gsq", [128, H0])
    posg = sb("posg", [128, SA])
    cont = sb("cont", [128, SA])
    maskl, maskh = sb("maskl", [128, SL], BF16), sb("maskh", [128, 512], BF16)
    identb = sb("identb", [128, 128], BF16)
    rowm = sb("rowm", [128, 16])
    hcur = sb("hcur", [128, 2, D])
    xh = sb("xh", [128, 2, D])
    xT = sb("xT", [65, 2, 4 + T])
    hidn = sb("hidn", [128, 2, D])
    hT = sb("hT", [65, 2, T])
    QT = sb("QT", [128, 2, 2 * T])
    KT = sb("KT", [128, 2, 4, 2 * T])
    V9 = sb("V9", [128, 2, 2, H0, DK + 1])
    E = sb("E", [128, 2, SA])
    R = sb("R", [128, SA + 1])
    mx = sb("mx", [128, 2, 16])
    rT = sb("rT", [128, 16])
    PTL, PTH = sb("PTL", [64, H0, 128]), sb("PTH", [128, H0, 128])
    rs = sb("rs", [128, 16])
    att = sb("att", [128, 2, D])
    aT = sb("aT", [65, 2, 128])
    scrap = sb("scrap", [128, 1])
    stats, mv, lnv, rstd = sb("stats", [128, 4, 6]), sb("mv", [128, 4, 2]), sb("lnv", [128, 4]), sb("rstd", [128, 4])

    S = psum[:, 0:3].rearrange("p b n -> p (b n)")
    X, Y = psum[:, 3], psum[:, 4]
    O = X[:, 0:288].rearrange("p (n g e) -> p n g e", g=2, e=DK + 1)

    loaded, zeroed, g_step, fold, fold_mm = (sem(n) for n in ("loaded", "zeroed", "g_step", "fold", "fold_mm"))
    names = """h_copied stats1 var1 ln1 rstd1 x_ready x_turned xT_ready conv_done stats2 var2 ln2 rstd2 hid_ready
               hid_turned hT_ready q_done q_ready k_done k_ready v_done v_ready s_done max1 x1_ready e1_ready
               scan_done recip1 dist1 d_ready ln_d exp_d eff_ready s2_done max2 x2_ready p_ready pt_turned pt_ready pv_done
               recip2 rs_ready att_ready a_turned aT_ready out_done h_written""".split()
    s = {n: sem(n) for n in names}
    consts = [(convw[:], a["a_conv"]), (beta[:], a["a_beta"].partition_broadcast(65)), (wraw[:], a["a_w"]), (lnw[:], a["a_lnw"]),
              (lnb_sel[:], a["a_lnb"]), (wo[:], a["a_wo"]), (gam[:], a["a_gam"].partition_broadcast(128)), (posg[:], a["c_pos"]),
              (cont[:], a["c_cont"].partition_broadcast(128)), (E[:, 0, 0:512], a["c_maskl"]), (E[:, 0, 512:1024], a["c_maskh"]),
              (rowm[:], a["c_rowm"])]

    def parts(ap):
        return (ap[:, 0:SL].rearrange("p (h k) -> p h k", h=H0), ap[:, SL:SA].rearrange("p (h k) -> p h k", h=H0))

    def spread(col, k):
        return col.unsqueeze(2).to_broadcast([128, H0, k])

    with nc.Block() as block:
        @block.sync
        def _(sp):
            for dst, src in consts:
                sp.dma_start(dst, src).then_inc(loaded, 16)

        @block.gpsimd
        def _(pool):
            pool.memset(xT[:], 0.0).then_inc(zeroed, 1)
            pool.wait_ge(zeroed, 1)
            for k, (buf, v) in enumerate(((xT[64:65], 1.0), (hT[64:65], 1.0), (aT[64:65], 1.0), (KT[:], 0.0), (V9[:], 1.0),
                                          (R[:, SA:SA + 1], 0.0), (mv[:], 1.0))):
                pool.memset(buf, v).then_inc(zeroed, 1)
                pool.wait_ge(zeroed, k + 2)

        @block.vector
        def _(dve):
            def carry():
                dve.tensor_copy(scrap[:], ident[:, 0:1])

            dve.wait_ge(loaded, 16 * len(consts))
            dve.wait_ge(zeroed, 8)
            n = [0]

            def link(ins):
                n[0] += 1
                ins.then_inc(fold, 1)
                dve.wait_ge(fold, n[0])
            link(dve.tensor_copy(maskl[:], E[:, 0, 0:512]))
            link(dve.tensor_copy(maskh[:], E[:, 0, 512:1024]))
            link(dve.tensor_copy(identb[:], ident[:]))
            link(dve.tensor_tensor(bsq[:], beta[:], beta[:], ALU.mult))
            link(dve.tensor_scalar(omb[:], bsq[:], -1.0, 1.0, ALU.mult, ALU.add))
            link(dve.tensor_scalar(opb[:], bsq[:], 1.0, None, ALU.add))
            link(dve.tensor_tensor(convw[:], convw[:], omb[:].unsqueeze(1).to_broadcast([65, 5, D]), ALU.mult))
            link(dve.tensor_tensor(diag[:], ident[0:64, 0:64], opb[0:64], ALU.mult))
            link(dve.tensor_tensor(convw[0:64, 4], convw[0:64, 4], diag[:], ALU.add))
            dve.wait_ge(fold_mm, 1)
            link(dve.scalar_tensor_tensor(out=waug[:, 0:512], in0=wraw[:, 0:512], scalar=lnw[:, 0:1], in1=X[0:65, 0:512],
                                          op0=ALU.mult, op1=ALU.add))
            link(dve.scalar_tensor_tensor(out=waug[:, 512:576], in0=wraw[:, 512:576], scalar=lnw[:, 0:1], in1=Y[0:65, 0:64],
                                          op0=ALU.mult, op1=ALU.add))
            link(dve.tensor_scalar(waug[:, 0:256], waug[:, 0:256], float(DK) ** -0.5, None, ALU.mult))
            dve.wait_ge(g_step, 3)
            link(dve.scalar_tensor_tensor(out=gsq[:], in0=gam[:], scalar=0.0, in1=gtmp[:], op0=ALU.max, op1=ALU.add))
            link(dve.tensor_tensor(gsq[:], gsq[:], gsq[:], ALU.mult))
            for ap, k in zip(parts(posg[:]), (HALF, T)):
                link(dve.tensor_tensor(ap, ap, spread(gsq[:], k), ALU.mult))

            def body(t, par, live):
                q = 1 - par
                if live(2):
                    after(dve, s["pv_done"], t - 1)
                    for g in range(2):
                        r = slice(64 * g, 64 * g + 64)
                        i = dve.reciprocal(rs[r], O[r, :, g, DK])
                    i.then_inc(s["recip2"], 1)
                    after(dve, s["recip2"], t - 1)
                    dve.tensor_tensor(rs[:], rs[:], rowm[:], ALU.mult).then_inc(s["rs_ready"], 1)
                    after(dve, s["rs_ready"], t - 1)
                    for g in range(2):
                        r = slice(64 * g, 64 * g + 64)
                        i = dve.tensor_tensor(att[r].rearrange("p s (h e) -> p (s h) e", h=H0), O[r, :, g, 0:DK],
                                              rs[r].unsqueeze(2).to_broadcast([64, 16, DK]), ALU.mult)
                    i.then_inc(s["att_ready"], 1)
                if live(1):
                    after(dve, s["s_done"], t)
                    for k, ap in enumerate(parts(S)):
                        i = dve.tensor_reduce(mx[:, 0, 8 * k:8 * k + 8], ap, AX_X, ALU.max)
                    i.then_inc(s["max1"], 1)
                    after(dve, s["max1"], t)
                    after(dve, s["pt_turned"], t - 2)
                    for k, (ap, e, w) in enumerate(zip(parts(S), parts(E[:, q]), (HALF, T))):
                        i = dve.tensor_tensor(e, ap, spread(mx[:, 0, 8 * k:8 * k + 8], w), ALU.subtract)
                    i.then_inc(s["x1_ready"], 1)
                if live(0):
                    dve.tensor_copy(hcur[:], h_all[:, bass.ds(t, 1)].rearrange("p u s d -> p (u s) d")).then_inc(s["h_copied"], 1)
                    after(dve, s["h_copied"], t + 1)
                    for k in range(2):
                        i = dve.bn_stats(stats[:, k], hcur[:, k])
                    i.then_inc(s["stats1"], 1)
                    after_all(dve, carry, (s["stats1"], t + 1))
                    for k in range(2):
                        i = dve.bn_aggr(mv[:, k], stats[:, k])
                    i.then_inc(s["var1"], 1)
                    after(dve, s["rstd1"], t + 1)
                    for k in range(2):
                        i = dve.tensor_scalar(xh[:, k], hcur[:, k], mv[:, k, 0:1], rstd[:, k:k + 1], ALU.subtract, ALU.mult)
                    i.then_inc(s["x_ready"], 1)
                if live(1):
                    after(dve, s["e1_ready"], t)
                    dve.tensor_tensor_scan(R[:, 0:SA][:, ::-1], cont[:, ::-1], E[:, q, ::-1], 0.0, ALU.mult, ALU.add).then_inc(s["scan_done"], 1)
                    after(dve, s["scan_done"], t)
                    for k, ap in enumerate(parts(R)):
                        i = dve.reciprocal(rT[:, 8 * k:8 * k + 8], ap[:, :, 0])
                    i.then_inc(s["recip1"], 1)
                    dve.tensor_tensor(E[:, q], R[:, 1:SA + 1], posg[:], ALU.mult).then_inc(s["dist1"], 1)
                    after(dve, s["recip1"], t)
                    after(dve, s["dist1"], t)
                    for k, (e, w) in enumerate(zip(parts(E[:, q]), (HALF, T))):
                        i = dve.scalar_tensor_tensor(out=e, in0=e, scalar=1e-16, in1=spread(rT[:, 8 * k:8 * k + 8], w), op0=ALU.max, op1=ALU.mult)
                    i.then_inc(s["d_ready"], 1)
                if live(0):
                    after(dve, s["conv_done"], t + 1)
                    for k in range(2):
                        i = dve.bn_stats(stats[:, 2 + k], X[:, 64 * k:64 * k + 64])
                    i.then_inc(s["stats2"], 1)
                    after_all(dve, carry, (s["stats2"], t + 1))
                    for k in range(2):
                        i = dve.bn_aggr(mv[:, 2 + k], stats[:, 2 + k])
                    i.then_inc(s["var2"], 1)
                    after(dve, s["rstd2"], t + 1)
                    for k in range(2):
                        i = dve.tensor_scalar(hidn[:, k], X[:, 64 * k:64 * k + 64], mv[:, 2 + k, 0:1], rstd[:, 2 + k:3 + k], ALU.subtract, ALU.mult)
                    i.then_inc(s["hid_ready"], 1)
                if live(2):
                    after(dve, s["out_done"], t - 1)
                    hv = h_all[:, bass.ds(t - 2, 1)].rearrange("p u s d -> p (u s) d")
                    dve.tensor_tensor(hv, X[:, 0:128].rearrange("p (s d) -> p s d", s=2), hv, ALU.add).then_inc(s["h_written"], 1)
                if live(1):
                    after(dve, s["eff_ready"], t)
                    dve.scalar_tensor_tensor(out=E[:, q], in0=E[:, q], scalar=1e-5, in1=S, op0=ALU.max, op1=ALU.mult).then_inc(s["s2_done"], 1)
                    after(dve, s["s2_done"], t)
                    for k, e in enumerate(parts(E[:, q])):
                        i = dve.tensor_reduce(mx[:, 1, 8 * k:8 * k + 8], e, AX_X, ALU.max)
                    i.then_inc(s["max2"], 1)
                    after(dve, s["max2"], t)
                    for k, (e, w) in enumerate(zip(parts(E[:, q]), (HALF, T))):
                        i = dve.tensor_tensor(e, e, spread(mx[:, 1, 8 * k:8 * k + 8], w), ALU.subtract)
                    i.then_inc(s["x2_ready"], 1)
            each_pair(dve, 2, body)

        @block.scalar
        def _(act):
            act.preload_act_table_set("natural_log_exp_and_others")
            act.wait_ge(loaded, 16 * len(consts))
            act.wait_ge(zeroed, 8)
            act.activation(gtmp[:], gam[:], ACT.Abs).then_inc(g_step, 1)
            act.wait_ge(g_step, 1)
            act.activation(gtmp[:], gtmp[:], ACT.Exp, scale=-1.0).then_inc(g_step, 1)
            act.wait_ge(g_step, 2)
            act.activation(gtmp[:], gtmp[:], ACT.Ln, bias=1.0).then_inc(g_step, 1)

            def body(t, par, live):
                q = 1 - par
                if live(1):
                    after(act, s["x1_ready"], t)
                    act.activation(E[:, q], E[:, q], ACT.Exp).then_inc(s["e1_ready"], 1)
                if live(0):
                    after(act, s["var1"], t + 1)
                    act.activation(lnv[:, 0:2], mv[:, 0:2, 1], ACT.Ln, bias=EPS).then_inc(s["ln1"], 1)
                    after(act, s["ln1"], t + 1)
                    act.activation(rstd[:, 0:2], lnv[:, 0:2], ACT.Exp, scale=-0.5).then_inc(s["rstd1"], 1)
                    after(act, s["x_turned"], t + 1)
                    act.activation(xT[0:64, :, 4:4 + T].rearrange("p g (s t) -> p s g t", s=2),
                                   X[0:64, 0:256].rearrange("p (s g t) -> p s g t", s=2, g=2), ACT.Copy).then_inc(s["xT_ready"], 1)
                if live(2):
                    after(act, s["a_turned"], t - 1)
                    act.activation(aT[0:64].rearrange("p s n -> p (s n)"), X[0:64, 0:256], ACT.Copy).then_inc(s["aT_ready"], 1)
                if live(1):
                    after(act, s["d_ready"], t)
                    act.activation(E[:, q], E[:, q], ACT.Ln).then_inc(s["ln_d"], 1)
                if live(0):
                    after(act, s["var2"], t + 1)
                    act.activation(lnv[:, 2:4], mv[:, 2:4, 1], ACT.Ln, bias=1e-12).then_inc(s["ln2"], 1)
                    after(act, s["ln2"], t + 1)
                    act.activation(rstd[:, 2:4], lnv[:, 2:4], ACT.Exp, scale=-0.5).then_inc(s["rstd2"], 1)
                if live(1):
                    after(act, s["ln_d"], t)
                    act.activation(E[:, q], E[:, q], ACT.Exp, scale=0.5).then_inc(s["exp_d"], 1)
                    after(act, s["exp_d"], t)
                    act.activation(E[:, q], E[:, q], ACT.Exp, scale=-1.0).then_inc(s["eff_ready"], 1)
                if live(0):
                    after(act, s["hid_turned"], t + 1)
                    act.activation(hT[0:64].rearrange("p g (s t) -> p s g t", s=2),
                                   X[0:64, 0:256].rearrange("p (s g t) -> p s g t", s=2, g=2), ACT.Copy).then_inc(s["hT_ready"], 1)
                    after(act, s["q_done"], t + 1)
                    act.activation(QT[:].rearrange("p s n -> p (s n)"), Y, ACT.Copy).then_inc(s["q_ready"], 1)
                    after(act, s["k_done"], t + 1)
                    for i in range(4):
                        r = slice(32 * i, 32 * i + 32)
                        ins = act.activation(KT[r, :, i], Y[r].rearrange("p (s n) -> p s n", s=2), ACT.Copy)
                    ins.then_inc(s["k_ready"], 1)
                    after(act, s["v_done"], t + 1)
                    after(act, s["pv_done"], t - 1)
                    act.activation(V9[:, par, :, :, 0:DK], X[:, 0:128].rearrange("p (g h e) -> p g h e", g=2, h=H0), ACT.Copy)\
                       .then_inc(s["v_ready"], 1)
                if live(1):
                    after(act, s["x2_ready"], t)
                    act.activation(E[:, q], E[:, q], ACT.Exp).then_inc(s["p_ready"], 1)
                    for r in range(4):
                        after(act, s["pt_turned"], (t - 1) * 4 + r + 1)
                        if r == 0:
                            after(act, s["pv_done"], t - 1)
                        if r < 2:
                            act.activation(PTL[:, 4 * r:4 * r + 4].rearrange("p h n -> p (h n)"), Y[0:64], ACT.Copy).then_inc(s["pt_ready"], 1)
                        else:
                            act.activation(PTH[:, 4 * r - 8:4 * r - 4].rearrange("p h n -> p (h n)"), Y, ACT.Copy).then_inc(s["pt_ready"], 1)
            each_pair(act, 2, body)

        @block.tensor
        def _(pe):
            def carry(bank=X):
                pe.matmul(bank[:, 511:512], identb[:], identb[:, 0:1], start=True, stop=True)

            pe.wait_ge(loaded, 16 * len(consts))
            pe.wait_ge(zeroed, 8)
            pe.matmul(X[0:65, 0:512], lnb_sel[:], wraw[0:64, 0:512], start=True, stop=True)
            pe.matmul(Y[0:65, 0:64], lnb_sel[:], wraw[0:64, 512:576], start=True, stop=True).then_inc(fold_mm, 1)
            pe.wait_ge(fold, 16)

            def body(t, par, live):
                q = 1 - par
                if live(1):
                    after(pe, s["k_ready"], t)
                    after(pe, s["s2_done"], t - 1)
                    pe.matmul(S[:, 0:512], identb[:], maskl[:], start=True, stop=False, skip_group_check=True)
                    for b in (1, 2):
                        pe.matmul(S[:, 512 * b:512 * b + 512], identb[:], maskh[:], start=True, stop=False, skip_group_check=True)
                    for h in range(H0):
                        for k, base, w in ((0, HALF * h, HALF), (1, SL + T * h, T)):
                            for g in range(2):
                                i = pe.matmul(S[64 * g:64 * g + 64, base:base + w], QT[:, h // 4, T * g + HALF * k:T * g + HALF * k + HALF],
                                              KT[:, h // 4, h % 4, T * g:T * g + w], start=False, stop=True, skip_group_check=True)
                    i.then_inc(s["s_done"], 1)
                if live(0):
                    after_all(pe, carry, (s["x_ready"], t + 1), (s["att_ready"], t - 1))
                    for k in range(2):
                        i = pe.transpose(X[0:64, 128 * k:128 * k + 128], xh[:, k], ident[:])
                    i.then_inc(s["x_turned"], 1)
                if live(2):
                    after_all(pe, carry, (s["att_ready"], t - 1), (s["xT_ready"], t + 1 if not (isinstance(t, int) and t >= PAIRS) else PAIRS))
                    for k in range(2):
                        i = pe.transpose(X[0:64, 128 * k:128 * k + 128], att[:, k], ident[:])
                    i.then_inc(s["a_turned"], 1)
                if live(0):
                    after(pe, s["xT_ready"], t + 1)
                    after(pe, s["aT_ready"], t - 1)
                    for k in range(2):
                        for g in range(2):
                            for tap in range(5):
                                i = pe.matmul(X[64 * g:64 * g + 64, 64 * k:64 * k + 64], xT[:, g, HALF * k + tap:HALF * k + tap + HALF],
                                              convw[:, tap], start=tap == 0, stop=tap == 4)
                    i.then_inc(s["conv_done"], 1)
                if live(2):
                    after(pe, s["aT_ready"], t - 1)
                    after(pe, s["hid_ready"], t + 1 if not (isinstance(t, int) and t >= PAIRS) else PAIRS)
                    for k in range(2):
                        i = pe.matmul(X[:, 64 * k:64 * k + 64], aT[:, k], wo[:], start=True, stop=True)
                    i.then_inc(s["out_done"], 1)
                if live(0):
                    after_all(pe, carry, (s["hid_ready"], t + 1), (s["h_written"], t - 1))
                    for k in range(2):
                        i = pe.transpose(X[0:64, 128 * k:128 * k + 128], hidn[:, k], ident[:])
                    i.then_inc(s["hid_turned"], 1)
                    after(pe, s["hT_ready"], t + 1)
                    if not isinstance(t, int) or t >= 1:
                        after(pe, s["pt_ready"], (t - 1) * 4)
                    hTf = hT[:].rearrange("p g n -> p (g n)")
                    for k in range(2):
                        i = pe.matmul(Y[:, 256 * k:256 * k + 256], waug[:, 128 * k:128 * k + 128], hTf, start=True, stop=True)
                    i.then_inc(s["q_done"], 1)
                    for g in range(2):
                        i = pe.matmul(X[:, 64 * g:64 * g + 64], hT[:, g], waug[:, 512:576], start=True, stop=True)
                    i.then_inc(s["v_done"], 1)
                    after(pe, s["q_ready"], t + 1)
                    for k in range(2):
                        i = pe.matmul(Y[:, 256 * k:256 * k + 256], waug[:, 256 + 128 * k:384 + 128 * k], hTf, start=True, stop=True)
                    i.then_inc(s["k_done"], 1)
                if live(1):
                    dead = isinstance(t, int) and t >= PAIRS
                    after_all(pe, lambda: carry(Y), (s["p_ready"], t), (s["k_ready"], PAIRS if dead else t + 1), (s["v_ready"], PAIRS if dead else t + 1))
                    for r in range(4):
                        if r:
                            after_all(pe, lambda: carry(Y), (s["pt_ready"], (t - 1) * 4 + r))
                        for n in range(4):
                            h = 4 * (r % 2) + n
                            if r < 2:
                                i = pe.transpose(Y[0:64, 128 * n:128 * n + 128], E[:, q, HALF * h:HALF * h + HALF], ident[:])
                            else:
                                i = pe.transpose(Y[:, 128 * n:128 * n + 128], E[:, q, SL + T * h:SL + T * h + T], ident[:])
                        i.then_inc(s["pt_turned"], 1)
                    after(pe, s["pt_ready"], (t - 1) * 4 + 4)
                    for h in range(H0):
                        pe.matmul(O[:, h].rearrange("p g e -> p (g e)"), PTL[:, h], V9[0:64, q, :, h], start=True, stop=True)
                    for h in range(H0):
                        i = pe.matmul(O[:, H0 + h].rearrange("p g e -> p (g e)"), PTH[:, h], V9[:, q, :, h], start=True, stop=True)
                    i.then_inc(s["pv_done"], 1)
            each_pair(pe, 2, body)


def mixture_stage(st, c):
    nc, a, psum, h_all, ident = st.nc, st.a, st.psum, st.h_all, st.ident

    def sb(n, s, dt=F32):
        return st.sb("moe_" + n, s, dt, c)

    def sem(n):
        return st.sem("moe_" + n)

    NP = NEXP // 2
    w1, sel, w2 = sb("w1", [128, NP, 128]), sb("sel", [128, NP, 128]), sb("w2", [128, NP, D])
    b2, router, iota = sb("b2", [128, D]), sb("router", [128, NEXP]), sb("iota", [128, 2, NEXP])
    hcur, hnew = sb("hcur", [128, 2, D]), sb("hnew", [128, 2, D])
    tok = sb("tok", [128, 2, 128])
    tokT, xT = sb("tokT", [128, 2, 2 * T]), sb("xT", [128, 2 * T])
    lg, m8, i8, fi = sb("lg", [128, 2, NEXP]), sb("m8", [128, 2, 8]), sb("i8", [128, 2, 8], mybir.dt.uint32), sb("fi", [128, 2, 8])
    d12, e12, w12 = sb("d12", [128, 2]), sb("e12", [128, 2]), sb("w12", [128, 2, 2])
    den = sb("den", [128, 2])
    eq = sb("eq", [128, 2, 2, NEXP])
    G = sb("G", [128, NP, 2 * T])
    stats, mv, lnv, rstd = sb("stats", [128, 2, 6]), sb("mv", [128, 2, 2]), sb("lnv", [128, 2]), sb("rstd", [128, 2])
    scrap = sb("scrap", [128, 1])
    pX, pW, pH, pC, pY = psum[:, 0], psum[:, 1], psum[:, 2:4], psum[:, 4:6], psum[:, 6]

    names = """h_copied stats1 var1 ln1 rstd1 t_ready t_turned xT_ready logits lg_ready max_done idx_done fi_done d_done e_done
               lg_ready2 den_done w1_done w2_done eq_done c_done w_turned tokT_ready up_done gelu_done cb_done g_ready down_done h_written x_added""".split()
    s = {n: sem(n) for n in names}
    loaded, zeroed = sem("loaded"), sem("zeroed")
    consts = [(w1[:], a["m_w1"]), (sel[:], a["c_sel"]), (w2[:], a["m_w2"]), (b2[:], a["m_b2"]), (router[:], a["m_router"]), (iota[:], a["c_iota"]), (tok[:], a["c_tok"])]

    with nc.Block() as block:
        @block.sync
        def _(sp):
            for dst, src in consts:
                sp.dma_start(dst, src).then_inc(loaded, 16)

        @block.vector
        def _(dve):
            def carry():
                dve.tensor_copy(scrap[:], ident[:, 0:1])

            dve.wait_ge(loaded, 16 * len(consts))

            def body(t, par, live):
                q = 1 - par
                if live(0):
                    dve.tensor_copy(hcur[:], h_all[:, bass.ds(t, 1)].rearrange("p u s d -> p (u s) d")).then_inc(s["h_copied"], 1)
                    after(dve, s["h_copied"], t + 1)
                    for k in range(2):
                        i = dve.bn_stats(stats[:, k], hcur[:, k])
                    i.then_inc(s["stats1"], 1)
                    after_all(dve, carry, (s["stats1"], t + 1))
                    for k in range(2):
                        i = dve.bn_aggr(mv[:, k], stats[:, k])
                    i.then_inc(s["var1"], 1)
                if live(1):
                    after(dve, s["gelu_done"], t)
                    after(dve, s["cb_done"], t)
                    for k in range(2):
                        g = G[:, 2 * k:2 * k + 2].rearrange("p e n -> p (e n)")
                        i = dve.tensor_tensor(g, g, pC[:, k], ALU.mult)
                    i.then_inc(s["g_ready"], 1)
                if live(0):
                    after(dve, s["rstd1"], t + 1)
                    for k in range(2):
                        i = dve.tensor_scalar(tok[:, k, 0:D], hcur[:, k], mv[:, k, 0:1], rstd[:, k:k + 1], ALU.subtract, ALU.mult)
                    i.then_inc(s["t_ready"], 1)
                    after(dve, s["t_ready"], t + 1)
                    dve.tensor_tensor(h_all[:, bass.ds(t, 1)].rearrange("p u s d -> p (u s) d"), hcur[:], tok[:, :, 0:D], ALU.add)\
                       .then_inc(s["x_added"], 1)
                    after(dve, s["logits"], t + 1)
                    dve.tensor_copy(lg[:].rearrange("p k e -> p (k e)"), pX[:, 0:16]).then_inc(s["lg_ready"], 1)
                    after_all(dve, carry, (s["lg_ready"], t + 1))
                    for k in range(2):
                        i = dve.max(m8[:, k], lg[:, k])
                    i.then_inc(s["max_done"], 1)
                    after_all(dve, carry, (s["max_done"], t + 1))
                    for k in range(2):
                        i = dve.max_index(i8[:, k], m8[:, k], lg[:, k])
                    i.then_inc(s["idx_done"], 1)
                    dve.tensor_tensor(d12[:], m8[:, :, 1], m8[:, :, 0], ALU.subtract).then_inc(s["d_done"], 1)
                    after(dve, s["idx_done"], t + 1)
                    dve.tensor_copy(fi[:], i8[:]).then_inc(s["fi_done"], 1)
                    after(dve, s["fi_done"], t + 1)
                    for n in range(2):
                        i = dve.tensor_tensor(eq[:, n], iota[:], fi[:, :, n:n + 1].to_broadcast([128, 2, NEXP]), ALU.is_equal)
                    i.then_inc(s["eq_done"], 1)
                    after(dve, s["e_done"], t + 1)
                    dve.tensor_scalar(den[:], e12[:], 1.0, None, ALU.add).then_inc(s["den_done"], 1)
                    after(dve, s["den_done"], t + 1)
                    dve.reciprocal(w12[:, 0], den[:]).then_inc(s["w1_done"], 1)
                    after(dve, s["w1_done"], t + 1)
                    dve.tensor_tensor(w12[:, 1], w12[:, 0], e12[:], ALU.mult).then_inc(s["w2_done"], 1)
                    after(dve, s["w2_done"], t + 1)
                    after(dve, s["eq_done"], t + 1)
                    for n in range(2):
                        i = dve.tensor_tensor(eq[:, n], eq[:, n], w12[:, n].unsqueeze(2).to_broadcast([128, 2, NEXP]), ALU.mult)
                    i.then_inc(s["c_done"], 1)
                    after(dve, s["c_done"], t + 1)
                    dve.tensor_tensor(tok[:, :, 96:96 + NEXP], eq[:, 0], eq[:, 1], ALU.add).then_inc(s["lg_ready2"], 1)
                if live(1):
                    after(dve, s["down_done"], t)
                    hv = h_all[:, bass.ds(t - 1, 1)].rearrange("p u s d -> p (u s) d")
                    dve.tensor_tensor(hv, pY[:, 0:128].rearrange("p (s d) -> p s d", s=2), hv, ALU.add).then_inc(s["h_written"], 1)
            each_pair(dve, 1, body)

        @block.scalar
        def _(act):
            act.wait_ge(loaded, 16 * len(consts))

            def body(t, par, live):
                q = 1 - par
                if live(0):
                    act.preload_act_table_set("natural_log_exp_and_others")
                    after(act, s["var1"], t + 1)
                    act.activation(lnv[:], mv[:, :, 1], ACT.Ln, bias=EPS).then_inc(s["ln1"], 1)
                    after(act, s["ln1"], t + 1)
                    act.activation(rstd[:], lnv[:], ACT.Exp, scale=-0.5).then_inc(s["rstd1"], 1)
                    after(act, s["t_turned"], t + 1)
                    act.activation(xT[:], pX[:, 0:256], ACT.Copy).then_inc(s["xT_ready"], 1)
                    after(act, s["d_done"], t + 1)
                    act.activation(e12[:], d12[:], ACT.Exp).then_inc(s["e_done"], 1)
                    after(act, s["w_turned"], t + 1)
                    act.activation(tokT[:, par], pW[:, 0:256], ACT.Copy).then_inc(s["tokT_ready"], 1)
                    after(act, s["up_done"], t + 1)
                    after(act, s["down_done"], t)
                    for k in range(2):
                        i = act.activation(G[:, 2 * k:2 * k + 2].rearrange("p e n -> p (e n)"), pH[:, k], ACT.Gelu)
                    i.then_inc(s["gelu_done"], 1)
            each_pair(act, 1, body)

        @block.tensor
        def _(pe):
            pe.wait_ge(loaded, 16 * len(consts))

            def body(t, par, live):
                q = 1 - par
                if live(0):
                    after(pe, s["t_ready"], t + 1)
                    after(pe, s["lg_ready"], t)
                    for k in range(2):
                        i = pe.transpose(pX[:, 128 * k:128 * k + 128], tok[:, k], ident[:])
                    i.then_inc(s["t_turned"], 1)
                if live(1):
                    after(pe, s["g_ready"], t)
                    after(pe, s["h_written"], t - 1)
                    for k in range(2):
                        n = slice(128 * k, 128 * k + 128)
                        pe.matmul(pY[:, 64 * k:64 * k + 64], tokT[:, q, n], b2[:], start=True, stop=False)
                        for e in range(NP):
                            i = pe.matmul(pY[:, 64 * k:64 * k + 64], G[:, e, n], w2[:, e], start=False, stop=e == NP - 1)
                    i.then_inc(s["down_done"], 1)
                if live(0):
                    after(pe, s["xT_ready"], t + 1)
                    for k in range(2):
                        i = pe.matmul(pX[:, 8 * k:8 * k + 8], xT[:, 128 * k:128 * k + 128], router[:], start=True, stop=True)
                    i.then_inc(s["logits"], 1)
                    after(pe, s["lg_ready2"], t + 1)
                    after(pe, s["tokT_ready"], t)
                    for k in range(2):
                        i = pe.transpose(pW[:, 128 * k:128 * k + 128], tok[:, k], ident[:])
                    i.then_inc(s["w_turned"], 1)
                    after(pe, s["tokT_ready"], t + 1)
                    after(pe, s["gelu_done"], t)
                    for e in range(NP):
                        i = pe.matmul(pH[:, e // 2, 256 * (e % 2):256 * (e % 2) + 256], w1[:, e], tokT[:, par], start=True, stop=True)
                    i.then_inc(s["up_done"], 1)
                    for e in range(NP):
                        i = pe.matmul(pC[:, e // 2, 256 * (e % 2):256 * (e % 2) + 256], sel[:, e], tokT[:, par], start=True, stop=True)
                    i.then_inc(s["cb_done"], 1)
            each_pair(pe, 1, body)


def window_attention_stage(st, c):
    nc, a, psum, h_all, ident = st.nc, st.a, st.psum, st.h_all, st.ident

    def sb(n, s, dt=F32):
        return st.sb("wa_" + n, s, dt, c)

    def sem(n):
        return st.sem("wa_" + n)

    NG = NH1 + 2
    W = NG * C1
    PIECES = [(0, 0, 16, 0, 32), (1, 0, 0, 16, 48), (2, 0, 0, 48, 16), (2, 1, 16, 0, 32), (3, 1, 0, 16, 48)]
    wqkv, wn = sb("wqkv", [D, W]), sb("wn", [128, W])
    cosq, sinq = sb("cosq", [128, 2 * NG, 8]), sb("sinq", [128, 2 * NG, 8])
    coso, sino = sb("coso", [128, NBLK, 8]), sb("sino", [128, NBLK, 8])
    mask, identb = sb("mask", [128, NBLK * KW], BF16), sb("identb", [128, 128], BF16)
    wg, wo4 = sb("wg", [C1, NH1, 65]), sb("wo4", [64, 2, D])
    mrow, mw = sb("mrow", [65, NH1, D]), sb("mw", [65, NH1, D])
    hcur, x, xT = sb("hcur", [128, 2, D]), sb("x", [128, 2, 128]), sb("xT", [D, 2 * T])
    sq, ms, lnms, rn = sb("sq", [128, 2, W]), sb("ms", [128, 2 * NG]), sb("lnms", [128, 2 * NG]), sb("rn", [128, 2 * NG])
    qkv = sb("qkv", [128, 2, 2, W + 1])
    rt = [sb(f"rt{i}", [128, 2 * NG, 8]) for i in range(4)]
    ro = [sb(f"ro{i}", [128, NBLK, 8]) for i in range(4)]
    QT, KT = sb("QT", [C1, NBLK, NH1, QB]), sb("KT", [C1, 2, WIN + T])
    mx, P0 = sb("mx", [128, NBLK]), sb("P0", [128, NBLK, KW])
    PZ, PT = sb("PZ", [128, len(PIECES), 2, 192]), sb("PT", [128, len(PIECES) * 2, 128])
    rs, os = sb("rs", [128, NBLK]), sb("os", [128, NBLK * C1 + 64])
    OT = sb("OT", [65, 2, NH1, 128])
    stats, mv, lnv, rstd = sb("stats", [128, 2, 6]), sb("mv", [128, 2, 2]), sb("lnv", [128, 2]), sb("rstd", [128, 2])
    scrap = sb("scrap", [128, 1])
    p0, pQ, p3, pP, pO = psum[:, 0], psum[:, 1:3], psum[:, 3], psum[:, 4:6], psum[:, 6:8]
    osb = os[:, 0:NBLK * C1].rearrange("p (n c) -> p n c", n=NBLK)

    names = """h_copied stats1 var1 ln1 rstd1 x_ready x_turned xT_ready qkv_done sq_done ms_done lnms_done rn_done n_done w_done
               r_done rope_ready q_turned k_turned q_ready k_ready s_done max_done p0_ready pz_ready p_turned p_ready pv_done
               rs_done os_done ro_done os_ready o_turned OT_ready out_done h_written""".split()
    s = {n: sem(n) for n in names}
    loaded, zeroed, fold, fold_mm = sem("loaded"), sem("zeroed"), sem("fold"), sem("fold_mm")
    consts = [(wqkv[:], a["w_qkv"]), (wn[:], a["w_norm"].partition_broadcast(128)), (cosq[:], a["c_cosq"]), (sinq[:], a["c_sinq"]),
              (coso[:], a["c_coso"]), (sino[:], a["c_sino"]), (sq[:, 0], a["c_maskw"]),
              (wg[:], a["w_g"]), (wo4[:], a["w_o"]), (mrow[:], a["w_bout"])]

    with nc.Block() as block:
        @block.sync
        def _(sp):
            for dst, src in consts:
                sp.dma_start(dst, src).then_inc(loaded, 16)

        @block.gpsimd
        def _(pool):
            for k, (buf, v) in enumerate(((x[:], 0.0), (qkv[:, :, :, W:W + 1], 1.0), (KT[:], 0.0), (PZ[:], 0.0), (os[:], 0.0), (OT[64:65], 1.0))):
                pool.memset(buf, v).then_inc(zeroed, 1)
                pool.wait_ge(zeroed, k + 1)

        @block.vector
        def _(dve):
            def carry():
                dve.tensor_copy(scrap[:], ident[:, 0:1])

            dve.wait_ge(loaded, 16 * len(consts))
            dve.wait_ge(zeroed, 6)
            dve.tensor_copy(mask[:], sq[:, 0]).then_inc(fold, 1)
            dve.tensor_copy(identb[:], ident[:]).then_inc(fold, 1)
            dve.wait_ge(fold_mm, 1)
            dve.tensor_tensor(mw[:], p0[0:65, 0:256].rearrange("p (h d) -> p h d", h=NH1), mrow[:], ALU.add).then_inc(fold, 1)

            def rotate(v, cos, sin, tmp, sign, sem_mul, sem_out, n):
                x1, x2 = v[:, :, C1 - ROT:C1:2], v[:, :, C1 - ROT + 1:C1:2]
                for o, (u, w) in zip(tmp, ((x1, cos), (x2, sin), (x1, sin), (x2, cos))):
                    i = dve.tensor_tensor(o[:], u, w[:], ALU.mult)
                i.then_inc(sem_mul, 1)
                after(dve, sem_mul, n)
                dve.tensor_tensor(x1, tmp[0][:], tmp[1][:], ALU.subtract if sign > 0 else ALU.add)
                i = dve.tensor_tensor(x2, tmp[3][:], tmp[2][:], ALU.add if sign > 0 else ALU.subtract)
                i.then_inc(sem_out, 1)

            def body(t, par, live):
                q = 1 - par
                if live(2):
                    after(dve, s["pv_done"], t - 1)
                    for k in range(2):
                        i = dve.reciprocal(rs[:, 4 * k:4 * k + 4], pO[:, k, 0:260].rearrange("p (n e) -> p n e", e=65)[:, :, 64])
                    i.then_inc(s["rs_done"], 1)
                    after(dve, s["rs_done"], t - 1)
                    after(dve, s["o_turned"], t - 2)
                    for k in range(2):
                        i = dve.tensor_tensor(osb[:, 4 * k:4 * k + 4], pO[:, k, 0:260].rearrange("p (n e) -> p n e", e=65)[:, :, 0:64],
                                              rs[:, 4 * k:4 * k + 4].unsqueeze(2).to_broadcast([128, 4, C1]), ALU.mult)
                    i.then_inc(s["os_done"], 1)
                    after(dve, s["os_done"], t - 1)
                    rotate(osb, coso, sino, ro, -1, s["ro_done"], s["os_ready"], t - 1)
                if live(0):
                    dve.tensor_copy(hcur[:], h_all[:, bass.ds(t, 1)].rearrange("p u s d -> p (u s) d")).then_inc(s["h_copied"], 1)
                    after(dve, s["h_copied"], t + 1)
                    for k in range(2):
                        i = dve.bn_stats(stats[:, k], hcur[:, k])
                    i.then_inc(s["stats1"], 1)
                    after_all(dve, carry, (s["stats1"], t + 1))
                    for k in range(2):
                        i = dve.bn_aggr(mv[:, k], stats[:, k])
                    i.then_inc(s["var1"], 1)
                if live(1):
                    after(dve, s["s_done"], t)
                    sc = p3[:, 0:NBLK * KW].rearrange("p (n k) -> p n k", n=NBLK)
                    dve.tensor_reduce(mx[:], sc, AX_X, ALU.max).then_inc(s["max_done"], 1)
                    after(dve, s["max_done"], t)
                    after(dve, s["pz_ready"], t - 1)
                    dve.tensor_tensor(P0[:], sc, mx[:].unsqueeze(2).to_broadcast([128, NBLK, KW]), ALU.subtract).then_inc(s["p0_ready"], 1)
                if live(0):
                    after(dve, s["rstd1"], t + 1)
                    after(dve, s["x_turned"], t)
                    for k in range(2):
                        i = dve.tensor_scalar(x[:, k, 0:D], hcur[:, k], mv[:, k, 0:1], rstd[:, k:k + 1], ALU.subtract, ALU.mult)
                    i.then_inc(s["x_ready"], 1)
                    after(dve, s["sq_done"], t + 1)
                    dve.tensor_reduce(ms[:], sq[:].rearrange("p k (g c) -> p (k g) c", c=C1), AX_X, ALU.add).then_inc(s["ms_done"], 1)
                if live(2):
                    after(dve, s["out_done"], t - 1)
                    hv = h_all[:, bass.ds(t - 2, 1)].rearrange("p u s d -> p (u s) d")
                    dve.tensor_tensor(hv, p0[:, 0:128].rearrange("p (s d) -> p s d", s=2), hv, ALU.add).then_inc(s["h_written"], 1)
                if live(0):
                    after(dve, s["rn_done"], t + 1)
                    after(dve, s["pv_done"], t - 1)
                    v = qkv[:, par]
                    for k in range(2):
                        i = dve.tensor_tensor(v[:, k, 0:W].rearrange("p (g c) -> p g c", g=NG), pQ[:, k, 0:W].rearrange("p (g c) -> p g c", g=NG),
                                              rn[:, NG * k:NG * k + NG].unsqueeze(2).to_broadcast([128, NG, C1]), ALU.mult)
                    i.then_inc(s["n_done"], 1)
                    after(dve, s["n_done"], t + 1)
                    for k in range(2):
                        i = dve.tensor_tensor(v[:, k, 0:W], v[:, k, 0:W], wn[:], ALU.mult)
                    i.then_inc(s["w_done"], 1)
                    after(dve, s["w_done"], t + 1)
                    for k in range(2):
                        g = slice(NG * k, NG * k + NG)
                        vk = v[:, k, 0:W].rearrange("p (g c) -> p g c", g=NG)
                        x1, x2 = vk[:, :, C1 - ROT:C1:2], vk[:, :, C1 - ROT + 1:C1:2]
                        for o, (u, w) in zip(rt, ((x1, cosq), (x2, sinq), (x1, sinq), (x2, cosq))):
                            i = dve.tensor_tensor(o[:, g], u, w[:, g], ALU.mult)
                    i.then_inc(s["r_done"], 1)
                    after(dve, s["r_done"], t + 1)
                    for k in range(2):
                        g = slice(NG * k, NG * k + NG)
                        vk = v[:, k, 0:W].rearrange("p (g c) -> p g c", g=NG)
                        dve.tensor_tensor(vk[:, :, C1 - ROT:C1:2], rt[0][:, g], rt[1][:, g], ALU.subtract)
                        i = dve.tensor_tensor(vk[:, :, C1 - ROT + 1:C1:2], rt[2][:, g], rt[3][:, g], ALU.add)
                    i.then_inc(s["rope_ready"], 1)
            each_pair(dve, 2, body)

        @block.scalar
        def _(act):
            act.preload_act_table_set("natural_log_exp_and_others")
            act.wait_ge(loaded, 16 * len(consts))
            act.wait_ge(zeroed, 6)
            act.wait_ge(fold, 2)

            def body(t, par, live):
                if live(0):
                    after(act, s["var1"], t + 1)
                    act.activation(lnv[:], mv[:, :, 1], ACT.Ln, bias=EPS).then_inc(s["ln1"], 1)
                    after(act, s["ln1"], t + 1)
                    act.activation(rstd[:], lnv[:], ACT.Exp, scale=-0.5).then_inc(s["rstd1"], 1)
                if live(1):
                    after(act, s["p0_ready"], t)
                    after(act, s["p_turned"], (t - 1) * 3)
                    for n, (kind, _, w0, k0, w) in enumerate(PIECES):
                        b = 4 * (kind // 2) + kind % 2
                        i = act.activation(PZ[:, n, :, k0:k0 + w], P0[:, b:b + 3:2, w0:w0 + w], ACT.Exp, scale=C1 ** -0.5)
                    i.then_inc(s["pz_ready"], 1)
                if live(0):
                    after(act, s["x_turned"], t + 1)
                    act.activation(xT[:], p0[0:64, 0:256], ACT.Copy).then_inc(s["xT_ready"], 1)
                if live(2):
                    after(act, s["o_turned"], t - 1)
                    for k in range(2):
                        i = act.activation(OT[0:64, k].rearrange("p h (n q) -> p n h q", n=4), pP[0:64, k].rearrange("p (n h q) -> p n h q", n=4, h=NH1), ACT.Copy)
                    i.then_inc(s["OT_ready"], 1)
                if live(0):
                    after(act, s["qkv_done"], t + 1)
                    for k in range(2):
                        i = act.activation(sq[:, k], pQ[:, k, 0:W], ACT.Square)
                    i.then_inc(s["sq_done"], 1)
                    after(act, s["ms_done"], t + 1)
                    act.activation(lnms[:], ms[:], ACT.Ln, bias=1e-8, scale=1.0 / C1).then_inc(s["lnms_done"], 1)
                    after(act, s["lnms_done"], t + 1)
                    act.activation(rn[:], lnms[:], ACT.Exp, scale=-0.5).then_inc(s["rn_done"], 1)
                    after(act, s["q_turned"], t + 1)
                    for k in range(2):
                        i = act.activation(QT[:, 4 * k:4 * k + 4].rearrange("p n h q -> p h n q"), pQ[0:64, k].rearrange("p (h n q) -> p h n q", h=NH1, n=4), ACT.Copy)
                    i.then_inc(s["q_ready"], 1)
                    after(act, s["k_turned"], t + 1)
                    act.activation(KT[:, :, WIN:].rearrange("p g (k t) -> p k g t", k=2), p3[0:64, 0:256].rearrange("p (k g t) -> p k g t", k=2, g=2), ACT.Copy)\
                       .then_inc(s["k_ready"], 1)
                if live(1):
                    for r in range(3):
                        after(act, s["p_turned"], (t - 1) * 3 + r + 1)
                        w = 4 if r < 2 else 2
                        act.activation(PT[:, 4 * r:4 * r + w].rearrange("p m n -> p (m n)"), pP[:, r % 2, 0:128 * w], ACT.Copy).then_inc(s["p_ready"], 1)
            each_pair(act, 2, body)

        @block.tensor
        def _(pe):
            pe.wait_ge(loaded, 16 * len(consts))
            pe.wait_ge(zeroed, 6)
            for h in range(NH1):
                i = pe.matmul(p0[0:65, 64 * h:64 * h + 64], wg[:, h], wo4[:, h // 2], start=True, stop=True)
            i.then_inc(fold_mm, 1)
            pe.wait_ge(fold, 3)

            def body(t, par, live):
                q = 1 - par
                if live(1):
                    after(pe, s["q_ready"], t)
                    after(pe, s["k_ready"], t)
                    pe.matmul(p3[:, 0:NBLK * KW], identb[:], mask[:], start=True, stop=False, skip_group_check=True)
                    for n in range(NBLK):
                        k, g, b = n // 4, n // 2 % 2, n % 2
                        i = pe.matmul(p3[:, KW * n:KW * n + KW], QT[:, n].rearrange("p h q -> p (h q)"), KT[:, g, 64 * k + 32 * b:64 * k + 32 * b + KW],
                                      start=False, stop=True, skip_group_check=True)
                    i.then_inc(s["s_done"], 1)
                if live(0):
                    after(pe, s["x_ready"], t + 1)
                    after(pe, s["h_written"], t - 2)
                    for k in range(2):
                        i = pe.transpose(p0[:, 128 * k:128 * k + 128], x[:, k], ident[:])
                    i.then_inc(s["x_turned"], 1)
                if live(2):
                    after(pe, s["os_ready"], t - 1)
                    after(pe, s["p_ready"], (t - 2) * 3 + 3)
                    for n in range(NBLK):
                        i = pe.transpose(pP[:, n // 4, 128 * (n % 4):128 * (n % 4) + 128], os[:, C1 * n:C1 * n + 128], ident[:])
                    i.then_inc(s["o_turned"], 1)
                if live(0):
                    after(pe, s["xT_ready"], t + 1)
                    after(pe, s["q_ready"], t)
                    for k in range(2):
                        i = pe.matmul(pQ[:, k, 0:W], xT[:, 128 * k:128 * k + 128], wqkv[:], start=True, stop=True)
                    i.then_inc(s["qkv_done"], 1)
                if live(2):
                    after(pe, s["OT_ready"], t - 1)
                    for k in range(2):
                        for h in range(NH1):
                            i = pe.matmul(p0[:, 64 * k:64 * k + 64], OT[:, k, h], mw[:, h], start=h == 0, stop=h == NH1 - 1)
                    i.then_inc(s["out_done"], 1)
                if live(0):
                    after(pe, s["rope_ready"], t + 1)
                    for k in range(2):
                        for h in range(NH1):
                            i = pe.transpose(pQ[:, k, 128 * h:128 * h + 128], qkv[:, par, k, 64 * h:64 * h + 128], ident[:])
                    i.then_inc(s["q_turned"], 1)
                    after(pe, s["p0_ready"], t)
                    for k in range(2):
                        i = pe.transpose(p3[:, 128 * k:128 * k + 128], qkv[:, par, k, 256:384], ident[:])
                    i.then_inc(s["k_turned"], 1)
                if live(1):
                    after(pe, s["pz_ready"], t)
                    if live(2):
                        after(pe, s["OT_ready"], t - 1)
                    for r in range(3):
                        if r == 2:
                            after(pe, s["p_ready"], (t - 1) * 3 + 1)
                        for m in range(4 * r, min(4 * r + 4, 10)):
                            i = pe.transpose(pP[:, r % 2, 128 * (m % 4):128 * (m % 4) + 128], PZ[:, m // 2].rearrange("p g n -> p (g n)")[:, 128 * (m % 2):128 * (m % 2) + 128], ident[:])
                        i.then_inc(s["p_turned"], 1)
                    after(pe, s["p_ready"], (t - 1) * 3 + 3)
                    for n in range(NBLK):
                        kind, g = 2 * (n // 4) + n % 2, n // 2 % 2
                        mine = [(m, p[1]) for m, p in enumerate(PIECES) if p[0] == kind]
                        for j, (m, k) in enumerate(mine):
                            i = pe.matmul(pO[:, n // 4, 65 * (n % 4):65 * (n % 4) + 65], PT[:, 2 * m + g], qkv[:, q, k, 320:385],
                                          start=j == 0, stop=j == len(mine) - 1)
                    i.then_inc(s["pv_done"], 1)
            each_pair(pe, 2, body)


def routed_stage(st, c):
    nc, a, psum, h_all, ident, out = st.nc, st.a, st.psum, st.h_all, st.ident, st.out

    def sb(n, s, dt=F32):
        return st.sb("rf_" + n, s, dt, c)

    def sem(n):
        return st.sem("rf_" + n)

    wi, ws, wo = sb("wi", [D, HID]), sb("ws", [128, 2, HID + 1]), sb("wo", [HID, D])
    bi, bo, ones = sb("bi", [HID, 1]), sb("bo", [1, D]), sb("ones", [1, 128])
    eye = sb("eye", [128, 2, HID + 1])
    ri, rf, rv, rw, rx = sb("ri", [1, PAIRS], I32), sb("rf", [1, PAIRS]), sb("rv", [1, PAIRS]), sb("rw", [1, PAIRS]), sb("rx", [1, PAIRS], I32)
    wsel, weff = sb("wsel", [128, 2, 2, HID + 1]), sb("weff", [128, 2, 2, HID + 1])
    hcur, x, xT = sb("hcur", [128, 2, D]), sb("x", [128, 2, 128]), sb("xT", [D, 2 * T])
    H1, H2, H3 = sb("H1", [HID, 2, 2 * T]), sb("H2", [HID, 2 * T]), sb("H3", [HID, 2 * T])
    fin = sb("fin", [128, 2, 2, D])
    stats, mv, lnv, rstd = sb("stats", [128, 2, 6]), sb("mv", [128, 2, 2]), sb("lnv", [128, 2]), sb("rstd", [128, 2])
    scrap = sb("scrap", [128, 1])
    pX, pA, pB, pC, pO = (psum[:, k] for k in range(5))

    names = """h_copied stats1 var1 ln1 rstd1 x_ready x_turned xT_ready in_done H1_ready l1_done H2_ready l2_done H3_ready
               out_done fin_ready weff_ready""".split()
    s = {n: sem(n) for n in names}
    loaded, zeroed, fold = sem("loaded"), sem("zeroed"), sem("fold")
    w_loaded, stored = [sem("w_loaded0"), sem("w_loaded1")], [sem("stored0"), sem("stored1")]
    consts = [(wi[:], a["r_wi"]), (ws[:], a["r_ws"]), (wo[:], a["r_wo"]), (bi[:], a["r_bi"]), (bo[:], a["r_bo"]), (eye[:], a["c_eye"]), (ri[:], a["r_route"])]

    def count16(t, par):
        return (t // 2 + 1) * 16 if isinstance(t, int) else (t + (2 - par)) * 8

    with nc.Block() as block:
        @block.sync
        def _(sp):
            for dst, src in consts:
                sp.dma_start(dst, src).then_inc(loaded, 16)
            sp.wait_ge(fold, 6)

            def body(t, par, live):
                q = 1 - par
                if live(0):
                    after(sp, s["weff_ready"], t - 1)
                    n = sp.value_load(rx[0:1, bass.ds(t, 1)], min_val=0, max_val=NRT)
                    sp.dma_start(wsel[:, par].rearrange("p l n -> p (l n)"), a["r_wr"][bass.ds(n, 1)].rearrange("e p n -> (e p) n")).then_inc(w_loaded[par], 16)
            each_pair(sp, 0, body)

        @block.gpsimd
        def _(pool):
            for k, (buf, v) in enumerate(((x[:], 0.0), (ones[:], 1.0))):
                pool.memset(buf, v).then_inc(zeroed, 1)
                pool.wait_ge(zeroed, k + 1)
            pool.wait_ge(fold, 7)

            def body(t, par, live):
                after(pool, s["fin_ready"], t + 1)
                for g in range(2):
                    pool.dma_start(out[bass.ds(2 * t + g, 1)].rearrange("b (s t) d -> t (b s) d", s=2), fin[64 * g:64 * g + 64, par]).then_inc(stored[par], 16)
            each_pair(pool, 0, body)
            for k in range(2):
                pool.wait_ge(stored[k], 32 * PAIRS // 2)

        @block.vector
        def _(dve):
            def carry():
                dve.tensor_copy(scrap[:], ident[:, 0:1])

            dve.wait_ge(loaded, 16 * len(consts))
            dve.wait_ge(zeroed, 2)
            n = [0]

            def link(ins):
                n[0] += 1
                ins.then_inc(fold, 1)
                dve.wait_ge(fold, n[0])
            link(dve.tensor_copy(rf[:], ri[:]))
            link(dve.tensor_scalar(rv[:], rf[:], 0.0, None, ALU.is_ge))
            link(dve.tensor_scalar(rw[:], rf[:], float(NRT - 1), None, ALU.is_le))
            link(dve.tensor_tensor(rv[:], rv[:], rw[:], ALU.mult))
            link(dve.scalar_tensor_tensor(out=rf[:], in0=rf[:], scalar=float(-NRT), in1=rv[:], op0=ALU.add, op1=ALU.mult))
            link(dve.tensor_scalar(rx[:], rf[:], float(NRT), None, ALU.add))
            link(dve.tensor_tensor(ws[:], ws[:], eye[:], ALU.add))

            def body(t, par, live):
                q = 1 - par
                if live(0):
                    after(dve, w_loaded[par], count16(t, par))
                    after(dve, s["H3_ready"], t - 1)
                    dve.tensor_tensor(weff[:, par], wsel[:, par], ws[:], ALU.add).then_inc(s["weff_ready"], 1)
                    after(dve, s["x_ready"], t)
                    dve.tensor_copy(hcur[:], h_all[:, bass.ds(t, 1)].rearrange("p u s d -> p (u s) d")).then_inc(s["h_copied"], 1)
                    after(dve, s["h_copied"], t + 1)
                    for k in range(2):
                        i = dve.bn_stats(stats[:, k], hcur[:, k])
                    i.then_inc(s["stats1"], 1)
                    after_all(dve, carry, (s["stats1"], t + 1))
                    for k in range(2):
                        i = dve.bn_aggr(mv[:, k], stats[:, k])
                    i.then_inc(s["var1"], 1)
                    after(dve, s["rstd1"], t + 1)
                    after(dve, s["x_turned"], t)
                    for k in range(2):
                        i = dve.tensor_scalar(x[:, k, 0:D], hcur[:, k], mv[:, k, 0:1], rstd[:, k:k + 1], ALU.subtract, ALU.mult)
                    i.then_inc(s["x_ready"], 1)
                if live(2):
                    after(dve, s["out_done"], t - 1)
                    if not isinstance(t, int) or t >= 4:
                        after(dve, stored[par], count16(t - 4, par) * 2)
                    dve.tensor_tensor(fin[:, par], pO[:, 0:128].rearrange("p (s d) -> p s d", s=2),
                                      h_all[:, bass.ds(t - 2, 1)].rearrange("p u s d -> p (u s) d"), ALU.add).then_inc(s["fin_ready"], 1)
            each_pair(dve, 2, body)

        @block.scalar
        def _(act):
            act.preload_act_table_set("natural_log_exp_and_others")
            act.wait_ge(loaded, 16 * len(consts))

            def body(t, par, live):
                q = 1 - par
                if live(0):
                    after(act, s["var1"], t + 1)
                    act.activation(lnv[:], mv[:, :, 1], ACT.Ln, bias=EPS).then_inc(s["ln1"], 1)
                    after(act, s["ln1"], t + 1)
                    act.activation(rstd[:], lnv[:], ACT.Exp, scale=-0.5).then_inc(s["rstd1"], 1)
                if live(1):
                    after(act, s["l1_done"], t)
                    act.activation(H2[:], pB[:, 0:256], ACT.Relu, bias=weff[:, q, 0, HID:HID + 1]).then_inc(s["H2_ready"], 1)
                if live(0):
                    after(act, s["x_turned"], t + 1)
                    act.activation(xT[:], pX[0:64, 0:256], ACT.Copy).then_inc(s["xT_ready"], 1)
                if live(1):
                    after(act, s["l2_done"], t)
                    after(act, s["out_done"], t - 1)
                    act.activation(H3[:], pC[:, 0:256], ACT.Relu, bias=weff[:, q, 1, HID:HID + 1]).then_inc(s["H3_ready"], 1)
                if live(0):
                    after(act, s["in_done"], t + 1)
                    act.activation(H1[:, par], pA[:, 0:256], ACT.Relu, bias=bi[:]).then_inc(s["H1_ready"], 1)
            each_pair(act, 2, body)

        @block.tensor
        def _(pe):
            pe.wait_ge(loaded, 16 * len(consts))
            pe.wait_ge(zeroed, 2)

            def body(t, par, live):
                q = 1 - par
                if live(1):
                    after(pe, s["H1_ready"], t)
                    after(pe, s["weff_ready"], t)
                    pe.matmul(pB[:, 0:256], weff[:, q, 0, 0:HID], H1[:, q], start=True, stop=True).then_inc(s["l1_done"], 1)
                if live(0):
                    after(pe, s["x_ready"], t + 1)
                    for k in range(2):
                        i = pe.transpose(pX[:, 128 * k:128 * k + 128], x[:, k], ident[:])
                    i.then_inc(s["x_turned"], 1)
                if live(1):
                    after(pe, s["H2_ready"], t)
                    pe.matmul(pC[:, 0:256], weff[:, q, 1, 0:HID], H2[:], start=True, stop=True).then_inc(s["l2_done"], 1)
                if live(0):
                    after(pe, s["xT_ready"], t + 1)
                    pe.matmul(pA[:, 0:256], wi[:], xT[:], start=True, stop=True).then_inc(s["in_done"], 1)
                if live(1):
                    after(pe, s["H3_ready"], t)
                    after(pe, s["fin_ready"], t - 1)
                    for k in range(2):
                        pe.matmul(pO[:, 64 * k:64 * k + 64], H3[:, 128 * k:128 * k + 128], wo[:], start=True, stop=False)
                        i = pe.matmul(pO[:, 64 * k:64 * k + 64], ones[:], bo[:], start=False, stop=True)
                    i.then_inc(s["out_done"], 1)
            each_pair(pe, 2, body)


def _host_constants(i):
    f = {k: np.asarray(v) for k, v in i.items()}
    r = {}
    r["x"] = np.ascontiguousarray(f["x"].reshape(B, T, J * 3))
    r["w1"] = np.ascontiguousarray(f["L0_tok_conv1_w"].transpose(1, 2, 3, 0).reshape(T, 15, T))
    r["w2"] = np.ascontiguousarray(f["L0_tok_conv2_w"].transpose(1, 2, 3, 0).reshape(T, 10, T))
    r["w3"] = np.ascontiguousarray(f["L0_tok_conv3_w"].transpose(1, 2, 3, 0).reshape(T, 10, 2 * T))
    r["conv_bias"] = np.stack([f["L0_tok_conv1_b"], f["L0_tok_conv2_b"], f["L0_tok_conv3_b"][:T], f["L0_tok_conv3_b"][T:]], axis=1)
    r["ln0"] = np.stack([f[k].reshape(J, 3).T for k in ("L0_tok_ln0_g", "L0_tok_ln0_b")])
    r["ln1"] = np.stack([f[k].reshape(J, 2).T for k in ("L0_tok_ln1_g", "L0_tok_ln1_b")])
    r["ln1c"] = np.stack([f["L0_tok_ln1_g"], f["L0_tok_ln1_b"]], axis=1)
    r["out_w"], r["out_b"] = f["L0_tok_out_w"], f["L0_tok_out_b"]
    cw = np.zeros((65, 5, D), np.float32)
    cw[:64] = f["L0_attn_conv_w"].transpose(1, 2, 0)
    cw[64, 4] = f["L0_attn_conv_b"]
    r["a_conv"], r["a_beta"] = cw, f["L0_attn_sqrt_beta"].reshape(D)
    w = np.zeros((65, 576), np.float32)
    for n, k in enumerate("qk"):
        for h in range(H0):
            at = 256 * n + 128 * (h // 4) + 32 * (h % 4)
            w[:64, at:at + DK] = f[f"L0_attn_{k}_w"].T[:, DK * h:DK * h + DK]
            w[64, at:at + DK] = f[f"L0_attn_{k}_b"][DK * h:DK * h + DK]
    w[:64, 512:], w[64, 512:] = f["L0_attn_v_w"].T, f["L0_attn_v_b"]
    r["a_w"] = w
    r["a_lnw"] = np.concatenate([f["L0_attn_ln_w"], np.ones(1, np.float32)])[:, None]
    r["a_lnb"] = np.concatenate([np.zeros((64, 64), np.float32), f["L0_attn_ln_b"][:, None]], axis=1)
    r["a_wo"] = np.concatenate([f["L0_attn_out_w"].T, f["L0_attn_out_b"][None]], axis=0)
    r["a_gam"] = f["L0_attn_gammas"].reshape(H0)
    qh, kk = np.arange(HALF)[:, None], np.arange(T)[None]
    low = np.where(kk[:, :HALF] <= qh, qh - kk[:, :HALF], -1)
    high = np.where(kk <= qh + HALF, qh + HALF - kk, -1)
    both = np.concatenate([np.tile(low, (2, H0)), np.tile(high, (2, H0))], axis=1)
    r["c_pos"] = np.maximum(both, 0).astype(np.float32)
    masked = np.where(both < 0, -1e30, 0.0).astype(np.float32)
    r["c_maskl"], r["c_maskh"] = masked[:, :SL], masked[:, SL:SL + 512]
    cont = np.ones(SA, np.float32)
    cont[HALF - 1:SL:HALF] = 0
    cont[SL + T - 1::T] = 0
    r["c_cont"] = cont
    rowm = np.ones((128, 16), np.float32)
    rowm[0::64, 0:8] = 0
    r["c_rowm"] = rowm
    w1 = np.zeros((128, NEXP // 2, 128), np.float32)
    w2 = np.zeros((128, NEXP // 2, D), np.float32)
    sel = np.zeros((128, NEXP // 2, 128), np.float32)
    for e in range(NEXP):
        w1[:64, e // 2, 64 * (e % 2):64 * (e % 2) + 64] = f["L0_ffn_w1"][e]
        w1[64, e // 2, 64 * (e % 2):64 * (e % 2) + 64] = f["L0_ffn_b1"][e]
        w2[64 * (e % 2):64 * (e % 2) + 64, e // 2] = f["L0_ffn_w2"][e]
        sel[96 + e, e // 2, 64 * (e % 2):64 * (e % 2) + 64] = 1
    r["m_w1"], r["m_w2"], r["c_sel"] = w1, w2, sel
    b2 = np.zeros((128, D), np.float32)
    b2[96:96 + NEXP] = f["L0_ffn_b2"]
    router = np.zeros((128, NEXP), np.float32)
    router[:64] = f["L0_ffn_router_w"].T
    r["m_b2"], r["m_router"] = b2, router
    r["c_iota"] = np.broadcast_to(np.arange(NEXP, dtype=np.float32), (128, 2, NEXP))
    tok = np.zeros((128, 2, 128), np.float32)
    tok[:, :, 64] = 1
    r["c_tok"] = tok
    r["w_qkv"] = np.concatenate([f["L1_attn_W_Q"].T, f["L1_attn_W_K"].T, f["L1_attn_W_V"].T], axis=1)
    r["w_norm"] = np.concatenate([f["L1_attn_wq"].reshape(-1), f["L1_attn_wk"], f["L1_attn_wv"]])
    p = np.arange(128)
    theta = 10000.0 ** (-2.0 * np.arange(ROT // 2) / ROT)
    tq = (p % 64)[:, None] + 64 * np.repeat(np.arange(2), NH1 + 2)[None]
    n = np.arange(NBLK)
    to = (p % QB)[:, None] + (64 * (n // 4) + QB * (n % 2))[None]
    for name, tt in (("q", tq), ("o", to)):
        ang = (tt[:, :, None].astype(np.float32) * theta[None, None].astype(np.float32)).astype(np.float32)
        r["c_cos" + name], r["c_sin" + name] = np.cos(ang).astype(np.float32), np.sin(ang).astype(np.float32)
    key = to[:, :, None] - (p % QB)[:, None, None] - WIN + np.arange(KW)[None, None]
    ok = (key <= to[:, :, None]) & (key >= to[:, :, None] - (WIN - 1)) & (key >= 0)
    r["c_maskw"] = np.where(ok, 0.0, -1e30).reshape(128, NBLK * KW).astype(np.float32)
    wg = np.zeros((C1, NH1, 65), np.float32)
    for h in range(NH1):
        w = f[f"L1_attn_Wg{h // 2}"]
        wg[:, h, :64] = w[:, 64 * (h % 2):64 * (h % 2) + 64]
        if h % 2 == 0:
            wg[:, h, 64] = f[f"L1_attn_bg{h // 2}"]
    r["w_g"] = wg
    r["w_o"] = f["L1_attn_Wout"].T.reshape(2, 64, D).transpose(1, 0, 2)
    bout = np.zeros((65, NH1, D), np.float32)
    bout[64, 0] = f["L1_attn_bout"]
    r["w_bout"] = bout
    wr = np.zeros((NRT + 1, 128, 2, HID + 1), np.float32)
    wr[:NRT, :, :, :HID] = f["L1_ffn_Wr"].transpose(1, 3, 0, 2)
    wr[:NRT, :, :, HID] = f["L1_ffn_br"].transpose(1, 2, 0)
    r["r_wr"] = wr.reshape(NRT + 1, 128, 2 * (HID + 1))
    r["r_ws"] = np.concatenate([f["L1_ffn_Ws"][:, 0].transpose(2, 0, 1), f["L1_ffn_bs"][:, 0].T[:, :, None]], axis=2)
    eye = np.zeros((128, 2, HID + 1), np.float32)
    eye[:, :, :HID] = np.eye(HID)[:, None]
    r["c_eye"] = eye
    r["r_wi"], r["r_bi"] = f["L1_ffn_Wi"].T, f["L1_ffn_bi"][:, None]
    r["r_wo"], r["r_bo"] = f["L1_ffn_Wo"].T, f["L1_ffn_bo"][None]
    r["r_route"] = f["L1_ffn_route_id"][None]
    r["c_ident"] = np.eye(128, dtype=np.float32)
    return {k: np.ascontiguousarray(v) for k, v in r.items()}


def kernel(**inputs):
    import numpy as _np
    import concourse.bacc as _bacc
    from concourse import mybir as _mybir
    from concourse.bass_utils import run_bass_kernel_spmd as _run

    nc = _bacc.Bacc("TRN2", target_bir_lowering=False, num_devices=1)
    host = _host_constants(inputs)
    arrays, args = {}, {}
    for name, v in host.items():
        arrays[f"in_{name}_dram"] = v
        args[name] = nc.dram_tensor(f"in_{name}_dram", v.shape, _mybir.dt.from_np(v.dtype), kind="ExternalInput").ap()
    out = nc.dram_tensor("out_0_dram", (B, T, D), F32, kind="ExternalOutput").ap()
    tower(nc, args, out)
    r = _run(nc, [arrays], core_ids=[0])
    return r.results[0]["out_0_dram"]
```

```python
from contextlib import ExitStack

import concourse.bass as bass
import numpy as np
from concourse import mybir

F32 = mybir.dt.float32
BF16 = mybir.dt.bfloat16
I32 = mybir.dt.int32
ALU = mybir.AluOpType
ACT = mybir.ActivationFunctionType
AX_X = mybir.AxisListType.X

B, T, J, D = 128, 128, 64, 64
PAIRS = B // 2
HALF = T // 2
H0, DK = 8, 8
SL, SH = H0 * HALF, H0 * T
SA = SL + SH
NEXP = 8
NH1, C1, WIN, ROT = 4, 64, 16, 16
QB = 32
NBLK = 2 * T // QB
KW = QB + WIN
HID, NRT = 128, 16
EPS = 1e-5


def after(eng, sem, count):
    if isinstance(count, int) and count <= 0:
        return
    eng.wait_ge(sem, count)


def after_all(eng, carrier, *waits):
    for sem, n in waits:
        after(eng, sem, n)
    if any(not isinstance(n, int) for _, n in waits):
        carrier()


def each_pair(eng, depth, body, unroll=2):
    peel = max(unroll, -(-depth // unroll) * unroll)
    for t in range(peel):
        body(t, t % unroll, lambda d, t=t: 0 <= t - d)
    with eng.Fori(peel, PAIRS - unroll + 1, unroll) as i:
        for k in range(unroll):
            body(i + k if k else i, k, lambda d: True)
    for t in range(PAIRS, PAIRS + depth):
        body(t, t % unroll, lambda d, t=t: t - d < PAIRS)


def last(count):
    return min(count, PAIRS) if isinstance(count, int) else count


def tower(nc, a, out):
    ctx = ExitStack()
    with ctx:
        def sb(name, shape, dt=F32, c=ctx):
            return c.enter_context(nc.sbuf_tensor(name, shape, dt))

        stage_sems = []

        def sem(name):
            stage_sems.append(nc.alloc_semaphore(name))
            return stage_sems[-1]

        def end_stage():
            nc.clear_and_free_semaphores(list(stage_sems))
            stage_sems.clear()
            nc.all_engine_barrier()

        psum = ctx.enter_context(nc.psum_tensor("psum", [128, 8, 512], F32))
        h_all = sb("h_all", [128, PAIRS, 2, D])
        ident = sb("ident", [128, 128])
        setup = sem("setup")
        st = Stage(nc, a, out, sb, sem, psum, h_all, ident)
        with nc.Block() as block:
            @block.sync
            def _(sp):
                sp.dma_start(ident[:], a["c_ident"]).then_inc(setup, 16)
                sp.wait_ge(setup, 16)
        with ExitStack() as c:
            token_stage(st, c)
        end_stage()
        with ExitStack() as c:
            distance_attention_stage(st, c)
        end_stage()
        with ExitStack() as c:
            mixture_stage(st, c)
        end_stage()
        with ExitStack() as c:
            window_attention_stage(st, c)
        end_stage()
        with ExitStack() as c:
            routed_stage(st, c)


class Stage:
    def __init__(self, nc, a, out, sb, sem, psum, h_all, ident):
        self.nc, self.a, self.out, self.sb, self.sem = nc, a, out, sb, sem
        self.psum, self.h_all, self.ident = psum, h_all, ident


def token_stage(st, c):
    nc, a, psum, h_all, ident = st.nc, st.a, st.psum, st.h_all, st.ident

    def sb(n, s, dt=F32):
        return st.sb(n, s, dt, c)

    def sem(n):
        return st.sem(n)

    w1 = sb("w1", [128, 15, 128])
    w2 = sb("w2", [128, 10, 128])
    w3 = sb("w3", [128, 10, 256])
    bias = sb("conv_bias", [128, 4])
    ln0 = sb("ln0", [128, 2, 3, J])
    ln1 = sb("ln1", [128, 2, 2, J])
    ln1c = sb("ln1c", [128, 2])
    wout = sb("wout", [128, D])
    woutg = sb("woutg", [128, D])
    beta_rep = sb("beta_rep", [128, 128])
    bias_out = sb("bias_out", [128, D])
    ones = sb("ones_t", [128, 128])
    xin = sb("xin", [128, 2, 2, J * 3])
    cin1 = sb("cin1", [128, 2, 3, 2, J + 4])
    cin2 = sb("cin2", [128, 2, 3, 2, J + 4])
    cin3 = sb("cin3", [128, 2, 2, 2, J + 4])
    y1 = sb("y1", [128, 2, 3, 2, J])
    y2 = sb("y2", [128, 2, 2, 2, J])
    y3 = sb("y3", [128, 2, 2, 2, J])
    s0 = sb("s0", [128, 3, 2, J])
    s1 = sb("s1", [128, 3, 2, J])
    s2 = sb("s2", [128, 2, 2, J])
    resn = sb("resn", [128, 2, 2, 128])
    resT = sb("resT", [128, 2, 256])
    scrap = sb("scrap_t", [128, 1])
    stats = sb("stats_t", [128, 8, 6])
    mv = sb("mv_t", [128, 8, 2])
    lnv = sb("lnv_t", [128, 8])
    rstd = sb("rstd_t", [128, 8])
    p1, p2, p3, pT, pO = (psum[:, k] for k in range(5))
    c1 = p1[:, 0:384].rearrange("p (w g j) -> p w g j", w=3, g=2)
    c2 = p2[:, 0:256].rearrange("p (w g j) -> p w g j", w=2, g=2)
    c3 = p3[:, 0:256].rearrange("p (h g j) -> p h g j", h=2, g=2)

    loaded, zeroed = sem("tok_loaded"), sem("tok_zeroed")
    folded, bias_mm = sem("tok_folded"), sem("tok_bias_mm")
    x_loaded = [sem("x_loaded0"), sem("x_loaded1")]
    stats_done, var_ready, ln_done, rstd_ready = sem("stats_done"), sem("var_ready"), sem("ln_done"), sem("rstd_ready")
    scaled, normed = sem("scaled"), sem("normed")
    conv1_done, conv2_done, conv3_done = sem("conv1_done"), sem("conv2_done"), sem("conv3_done")
    act1, act2, act3 = sem("act1"), sem("act2"), sem("act3")
    res_turned, resT_ready, projected, h_written = sem("res_turned"), sem("resT_ready"), sem("projected"), sem("h_written")
    consts = [(w1[:], a["w1"]), (w2[:], a["w2"]), (w3[:], a["w3"]), (bias[:], a["conv_bias"]),
              (ln0[:], a["ln0"].partition_broadcast(128)), (ln1[:], a["ln1"].partition_broadcast(128)),
              (ln1c[:], a["ln1c"]), (wout[:], a["out_w"]),
              (bias_out[:], a["out_b"].partition_broadcast(128))]

    with nc.Block() as block:
        @block.sync
        def _(sp):
            for dst, src in consts:
                sp.dma_start(dst, src).then_inc(loaded, 16)

            def body(t, par, live):
                if live(0) and not (isinstance(t, int) and t >= PAIRS):
                    after(sp, scaled, t - 1)
                    sp.dma_start(xin[:, par], a["x"][bass.ds(2 * t, 2)].rearrange("g t k -> t g k")).then_inc(x_loaded[par], 16)
            each_pair(sp, 0, body)

        @block.gpsimd
        def _(pool):
            for buf in (cin1, cin2, cin3):
                pool.memset(buf[:], 0.0).then_inc(zeroed, 1)
            pool.memset(mv[:], 1.0).then_inc(zeroed, 1)
            pool.memset(ones[:], 1.0).then_inc(zeroed, 1)

        @block.vector
        def _(dve):
            def carry():
                dve.tensor_copy(scrap[:], ident[:, 0:1])

            dve.wait_ge(loaded, 16 * len(consts))
            dve.wait_ge(zeroed, 5)
            dve.tensor_scalar(woutg[:], wout[:], ln1c[:, 0:1], None, ALU.mult).then_inc(folded, 1)
            dve.tensor_scalar(beta_rep[:], ones[:], ln1c[:, 1:2], None, ALU.mult).then_inc(folded, 1)
            dve.wait_ge(bias_mm, 1)
            dve.tensor_tensor(bias_out[:], pO[:, 0:D], bias_out[:], ALU.add).then_inc(folded, 1)
            dve.wait_ge(folded, 3)

            def body(t, par, live):
                q = 1 - par
                last = None
                if live(0) and not (isinstance(t, int) and t >= PAIRS):
                    after(dve, x_loaded[par], (t // 2 + 1) * 16 if isinstance(t, int) else (t + (2 - par)) * 8)
                    for g in range(2):
                        last = dve.bn_stats(stats[:, g], xin[:, par, g])
                if live(2):
                    after(dve, act1, t - 1)
                    for g in range(2):
                        last = dve.bn_stats(stats[:, 2 + g], y1[:, par, :, g])
                if live(4):
                    after(dve, act2, t - 3)
                    for g in range(2):
                        last = dve.bn_stats(stats[:, 4 + g], y2[:, par, :, g])
                if live(6):
                    after(dve, act3, t - 5)
                    for g in range(2):
                        last = dve.bn_stats(stats[:, 6 + g], y3[:, par, g])
                if last is not None:
                    last.then_inc(stats_done, 1)
                    after_all(dve, carry, (stats_done, t + 1))
                    slots = [k for k in range(4) if live(2 * k) and not (k == 0 and isinstance(t, int) and t >= PAIRS)]
                    for k in slots:
                        for g in (2 * k, 2 * k + 1):
                            last = dve.bn_aggr(mv[:, g], stats[:, g])
                    last.then_inc(var_ready, 1)
                    dve.wait_ge(var_ready, t + 1)
                    last = None
                    for k, (src, dst, gam) in enumerate(((xin[:, par].rearrange("p g (j w) -> p w g j", w=3), s0, ln0),
                                                         (y1[:, par], s1, ln0), (y2[:, par], s2, ln1))):
                        if k in slots:
                            for g in range(2):
                                last = dve.scalar_tensor_tensor(out=dst[:, :, g], in0=src[:, :, g], scalar=mv[:, 2 * k + g, 0:1],
                                                                in1=gam[:, 0], op0=ALU.subtract, op1=ALU.mult)
                    if last is not None:
                        last.then_inc(scaled, 1)
                        dve.wait_ge(scaled, t + 1)
                    dve.wait_ge(rstd_ready, t + 1)
                    if 0 in slots:
                        after(dve, conv1_done, t - 1)
                    if 1 in slots:
                        after(dve, conv2_done, t - 3)
                    if 2 in slots:
                        after(dve, conv3_done, t - 5)
                    for k, (src, dst, gam) in enumerate(((s0, cin1, ln0), (s1, cin2, ln0), (s2, cin3, ln1))):
                        if k in slots:
                            for g in range(2):
                                last = dve.scalar_tensor_tensor(out=dst[:, par, :, g, 2:2 + J], in0=src[:, :, g], scalar=rstd[:, 2 * k + g:2 * k + g + 1],
                                                                in1=gam[:, 1], op0=ALU.mult, op1=ALU.add)
                    if 3 in slots:
                        after(dve, res_turned, t - 7)
                        for g in range(2):
                            last = dve.tensor_scalar(resn[:, par, g], y3[:, par, g].rearrange("p h j -> p (h j)"), mv[:, 6 + g, 0:1], rstd[:, 6 + g:7 + g],
                                                     ALU.subtract, ALU.mult)
                    last.then_inc(normed, 1)
                if live(7):
                    after(dve, projected, t - 6)
                    dve.tensor_tensor(h_all[:, bass.ds(t - 7, 1)].rearrange("p u s d -> p (u s) d"),
                                      pO[:, 0:128].rearrange("p (s d) -> p s d", s=2),
                                      bias_out[:].unsqueeze(1).to_broadcast([128, 2, D]), ALU.add).then_inc(h_written, 1)
            each_pair(dve, 8, body)

        @block.scalar
        def _(act):
            act.preload_act_table_set("natural_log_exp_and_others")
            act.wait_ge(loaded, 16 * len(consts))

            def body(t, par, live):
                q = 1 - par
                if live(6) if isinstance(t, int) and t >= PAIRS else True:
                    act.wait_ge(var_ready, t + 1)
                    act.activation(lnv[:], mv[:, :, 1], ACT.Ln, bias=EPS).then_inc(ln_done, 1)
                    act.wait_ge(ln_done, t + 1)
                    act.activation(rstd[:], lnv[:], ACT.Exp, scale=-0.5).then_inc(rstd_ready, 1)
                if live(1):
                    after(act, conv1_done, t)
                    after(act, normed, t - 0)
                    act.activation(y1[:, q], c1, ACT.Relu, bias=bias[:, 0:1]).then_inc(act1, 1)
                if live(3):
                    after(act, conv2_done, t - 2)
                    act.activation(y2[:, q], c2, ACT.Relu, bias=bias[:, 1:2]).then_inc(act2, 1)
                if live(7):
                    after(act, res_turned, t - 6)
                    after(act, projected, t - 8)
                    act.activation(resT[:, q].rearrange("p (s g t) -> p g s t", s=2, g=2),
                                   pT[:, 0:256].rearrange("p (g s t) -> p g s t", g=2, s=2), ACT.Copy).then_inc(resT_ready, 1)
                if live(5):
                    after(act, conv3_done, t - 4)
                    act.activation(y3[:, q, :, 0], c3[:, 0], ACT.Relu, bias=bias[:, 2:3])
                    act.activation(y3[:, q, :, 1], c3[:, 1], ACT.Relu, bias=bias[:, 3:4]).then_inc(act3, 1)
            each_pair(act, 8, body)

        @block.tensor
        def _(pe):
            pe.wait_ge(loaded, 16 * len(consts))
            pe.wait_ge(folded, 2)
            pe.matmul(pO[:, 0:D], beta_rep[:], wout[:], start=True, stop=True).then_inc(bias_mm, 1)
            pe.wait_ge(folded, 3)
            taps1 = [(kh, kw) for kw in (1, 0, 2) for kh in range(5)]
            taps2 = [(kh, kw) for kw in range(2) for kh in range(5)]

            def body(t, par, live):
                q = 1 - par
                if live(1):
                    pe.wait_ge(normed, t)
                    after(pe, act1, t - 1)
                    for n, (kh, kw) in enumerate(taps1):
                        lo, hi = max(0, 1 - kw), min(3, 4 - kw)
                        mm = pe.matmul(c1[:, lo:hi], w1[:, kh * 3 + kw], cin1[:, q, lo + kw - 1:hi + kw - 1, :, kh:kh + J],
                                       start=n == 0, stop=n == len(taps1) - 1)
                    mm.then_inc(conv1_done, 1)
                if live(3):
                    pe.wait_ge(normed, t)
                    after(pe, act2, t - 3)
                    for n, (kh, kw) in enumerate(taps2):
                        mm = pe.matmul(c2, w2[:, kh * 2 + kw], cin2[:, q, kw:kw + 2, :, kh:kh + J], start=n == 0, stop=n == len(taps2) - 1)
                    mm.then_inc(conv2_done, 1)
                if live(7):
                    pe.wait_ge(normed, t)
                    after(pe, resT_ready, t - 7)
                    for g in range(2):
                        mm = pe.transpose(pT[:, g * 128:(g + 1) * 128], resn[:, q, g], ident[:])
                    mm.then_inc(res_turned, 1)
                if live(5):
                    pe.wait_ge(normed, t)
                    after(pe, act3, t - 5)
                    for m in range(2):
                        for n, (kh, kw) in enumerate(taps2):
                            mm = pe.matmul(c3[:, m], w3[:, kh * 2 + kw, m * 128:(m + 1) * 128], cin3[:, q, kw, :, kh:kh + J],
                                           start=n == 0, stop=n == len(taps2) - 1)
                    mm.then_inc(conv3_done, 1)
                if live(7):
                    after(pe, resT_ready, t - 6)
                    after(pe, h_written, t - 7)
                    for s in range(2):
                        mm = pe.matmul(pO[:, s * D:(s + 1) * D], resT[:, q, s * 128:(s + 1) * 128], woutg[:], start=True, stop=True)
                    mm.then_inc(projected, 1)
            each_pair(pe, 8, body)


def distance_attention_stage(st, c):
    nc, a, psum, h_all, ident = st.nc, st.a, st.psum, st.h_all, st.ident

    def sb(n, s, dt=F32):
        return st.sb("at_" + n, s, dt, c)

    def sem(n):
        return st.sem("at_" + n)

    convw = sb("convw", [65, 5, D])
    beta, bsq, omb, opb = sb("beta", [65, D]), sb("bsq", [65, D]), sb("omb", [65, D]), sb("opb", [65, D])
    diag = sb("diag", [64, D])
    wraw, waug = sb("wraw", [65, 576]), sb("waug", [65, 576])
    lnw, lnb_sel = sb("lnw", [65, 1]), sb("lnb_sel", [64, 65])
    wo = sb("wo", [65, D])
    gam, gtmp, gsq = sb("gam", [128, H0]), sb("gtmp", [128, H0]), sb("gsq", [128, H0])
    posg = sb("posg", [128, SA])
    cont = sb("cont", [128, SA])
    maskl, maskh = sb("maskl", [128, SL], BF16), sb("maskh", [128, 512], BF16)
    identb = sb("identb", [128, 128], BF16)
    rowm = sb("rowm", [128, 16])
    hcur = sb("hcur", [128, 2, D])
    xh = sb("xh", [128, 2, 128])
    xT = sb("xT", [65, 2, 4 + T])
    hidn = sb("hidn", [128, 2, 128])
    hT = sb("hT", [65, 2, T])
    QT = sb("QT", [128, 2, 2 * T])
    KT = sb("KT", [128, 2, 4, 2 * T])
    V9 = sb("V9", [128, 4, 2, H0, DK + 1])
    P = sb("P", [128, SA])
    E = sb("E", [128, 2, SA])
    R = sb("R", [128, SA + 1])
    mx = sb("mx", [128, 2, 16])
    rT = sb("rT", [128, 16])
    PTL, PTH = sb("PTL", [64, H0, 128]), sb("PTH", [128, H0, 128])
    rs = sb("rs", [128, 16])
    att = sb("att", [128, 2, 128])
    aT = sb("aT", [65, 2, 128])
    scrap = sb("scrap", [128, 1])
    stats, mv, lnv, rstd = sb("stats", [128, 4, 6]), sb("mv", [128, 4, 2]), sb("lnv", [128, 4]), sb("rstd", [128, 4])

    S2 = [psum[:, 3 * p:3 * p + 3].rearrange("p b n -> p (b n)") for p in range(2)]
    X, Y = psum[:, 6], psum[:, 7]
    O = X[:, 0:288].rearrange("p (n g e) -> p n g e", g=2, e=DK + 1)

    loaded, zeroed, g_step, fold, fold_mm = (sem(n) for n in ("loaded", "zeroed", "g_step", "fold", "fold_mm"))
    names = """h_copied stats1 var1 ln1 rstd1 x_ready x_turned xT_ready conv_done stats2 var2 ln2 rstd2 hid_ready
               hid_turned hT_ready q_done q_ready k_done k_ready v_done v_ready s_done max1 x1_ready e1_ready
               scan_done recip1 dist1 d_ready ln_d exp_d eff_ready s2_done max2 x2_ready p_ready pt_turned pt_ready pv_done
               recip2 rs_ready att_ready a_turned aT_ready out_done h_written""".split()
    s = {n: sem(n) for n in names}
    consts = [(convw[:], a["a_conv"]), (beta[:], a["a_beta"].partition_broadcast(65)), (wraw[:], a["a_w"]), (lnw[:], a["a_lnw"]),
              (lnb_sel[:], a["a_lnb"]), (wo[:], a["a_wo"]), (gam[:], a["a_gam"].partition_broadcast(128)), (posg[:], a["c_pos"]),
              (cont[:], a["c_cont"].partition_broadcast(128)), (E[:, 0, 0:512], a["c_maskl"]), (E[:, 0, 512:1024], a["c_maskh"]),
              (rowm[:], a["c_rowm"])]

    def parts(ap):
        return (ap[:, 0:SL].rearrange("p (h k) -> p h k", h=H0), ap[:, SL:SA].rearrange("p (h k) -> p h k", h=H0))

    def spread(col, k):
        return col.unsqueeze(2).to_broadcast([128, H0, k])

    with nc.Block() as block:
        @block.sync
        def _(sp):
            for dst, src in consts:
                sp.dma_start(dst, src).then_inc(loaded, 16)

        @block.gpsimd
        def _(pool):
            pool.memset(xT[:], 0.0).then_inc(zeroed, 1)
            pool.wait_ge(zeroed, 1)
            for k, (buf, v) in enumerate(((xT[64:65], 1.0), (hT[64:65], 1.0), (aT[64:65], 1.0), (KT[:], 0.0), (V9[:], 1.0),
                                          (R[:, SA:SA + 1], 0.0), (mv[:], 1.0), (xh[:], 0.0), (hidn[:], 0.0), (att[:], 0.0))):
                pool.memset(buf, v).then_inc(zeroed, 1)
                pool.wait_ge(zeroed, k + 2)

        @block.vector
        def _(dve):
            def carry():
                dve.tensor_copy(scrap[:], ident[:, 0:1])

            dve.wait_ge(loaded, 16 * len(consts))
            dve.wait_ge(zeroed, 11)
            n = [0]

            def link(ins):
                n[0] += 1
                ins.then_inc(fold, 1)
                dve.wait_ge(fold, n[0])
            link(dve.tensor_copy(maskl[:], E[:, 0, 0:512]))
            link(dve.tensor_copy(maskh[:], E[:, 0, 512:1024]))
            link(dve.tensor_copy(identb[:], ident[:]))
            link(dve.tensor_tensor(bsq[:], beta[:], beta[:], ALU.mult))
            link(dve.tensor_scalar(omb[:], bsq[:], -1.0, 1.0, ALU.mult, ALU.add))
            link(dve.tensor_scalar(opb[:], bsq[:], 1.0, None, ALU.add))
            link(dve.tensor_tensor(convw[:], convw[:], omb[:].unsqueeze(1).to_broadcast([65, 5, D]), ALU.mult))
            link(dve.tensor_tensor(diag[:], ident[0:64, 0:64], opb[0:64], ALU.mult))
            link(dve.tensor_tensor(convw[0:64, 4], convw[0:64, 4], diag[:], ALU.add))
            dve.wait_ge(fold_mm, 1)
            link(dve.scalar_tensor_tensor(out=waug[:, 0:512], in0=wraw[:, 0:512], scalar=lnw[:, 0:1], in1=X[0:65, 0:512],
                                          op0=ALU.mult, op1=ALU.add))
            link(dve.scalar_tensor_tensor(out=waug[:, 512:576], in0=wraw[:, 512:576], scalar=lnw[:, 0:1], in1=Y[0:65, 0:64],
                                          op0=ALU.mult, op1=ALU.add))
            link(dve.tensor_scalar(waug[:, 0:256], waug[:, 0:256], float(DK) ** -0.5, None, ALU.mult))
            dve.wait_ge(g_step, 3)
            link(dve.scalar_tensor_tensor(out=gsq[:], in0=gam[:], scalar=0.0, in1=gtmp[:], op0=ALU.max, op1=ALU.add))
            link(dve.tensor_tensor(gsq[:], gsq[:], gsq[:], ALU.mult))
            for ap, k in zip(parts(posg[:]), (HALF, T)):
                link(dve.tensor_tensor(ap, ap, spread(gsq[:], k), ALU.mult))

            def body(t, par, live):
                p0, p1 = par % 2, 1 - par % 2
                if live(4):
                    after(dve, s["pv_done"], t - 3)
                    for g in range(2):
                        r = slice(64 * g, 64 * g + 64)
                        i = dve.reciprocal(rs[r], O[r, :, g, DK])
                    i.then_inc(s["recip2"], 1)
                    after(dve, s["recip2"], t - 3)
                    dve.tensor_tensor(rs[:], rs[:], rowm[:], ALU.mult).then_inc(s["rs_ready"], 1)
                    after(dve, s["rs_ready"], t - 3)
                    for g in range(2):
                        r = slice(64 * g, 64 * g + 64)
                        i = dve.tensor_tensor(att[r, :, 0:D].rearrange("p s (h e) -> p s h e", h=H0), O[r, :, g, 0:DK].rearrange("p (s h) e -> p s h e", s=2),
                                              rs[r].rearrange("p (s h) -> p s h", s=2).unsqueeze(3).to_broadcast([64, 2, H0, DK]), ALU.mult)
                    i.then_inc(s["att_ready"], 1)
                if live(0):
                    dve.tensor_copy(hcur[:], h_all[:, bass.ds(t, 1)].rearrange("p u s d -> p (u s) d")).then_inc(s["h_copied"], 1)
                    after(dve, s["h_copied"], t + 1)
                    for k in range(2):
                        i = dve.bn_stats(stats[:, k], hcur[:, k])
                    i.then_inc(s["stats1"], 1)
                    after_all(dve, carry, (s["stats1"], t + 1))
                    for k in range(2):
                        i = dve.bn_aggr(mv[:, k], stats[:, k])
                    i.then_inc(s["var1"], 1)
                if live(1):
                    after(dve, s["s_done"], t)
                    for k, ap in enumerate(parts(S2[p1])):
                        i = dve.tensor_reduce(mx[:, 0, 8 * k:8 * k + 8], ap, AX_X, ALU.max)
                    i.then_inc(s["max1"], 1)
                if live(0):
                    after(dve, s["rstd1"], t + 1)
                    for k in range(2):
                        i = dve.tensor_scalar(xh[:, k, 0:D], hcur[:, k], mv[:, k, 0:1], rstd[:, k:k + 1], ALU.subtract, ALU.mult)
                    i.then_inc(s["x_ready"], 1)
                if live(1):
                    after(dve, s["max1"], t)
                    after(dve, s["p_ready"], t - 2)
                    for k, (ap, e, w) in enumerate(zip(parts(S2[p1]), parts(E[:, p1]), (HALF, T))):
                        i = dve.tensor_tensor(e, ap, spread(mx[:, 0, 8 * k:8 * k + 8], w), ALU.subtract)
                    i.then_inc(s["x1_ready"], 1)
                if live(2):
                    after(dve, s["eff_ready"], t - 1)
                    dve.scalar_tensor_tensor(out=E[:, p0], in0=E[:, p0], scalar=1e-5, in1=S2[p0], op0=ALU.max, op1=ALU.mult).then_inc(s["s2_done"], 1)
                if live(0):
                    after(dve, s["conv_done"], t + 1)
                    for k in range(2):
                        i = dve.bn_stats(stats[:, 2 + k], X[:, 64 * k:64 * k + 64])
                    i.then_inc(s["stats2"], 1)
                    after_all(dve, carry, (s["stats2"], t + 1))
                    for k in range(2):
                        i = dve.bn_aggr(mv[:, 2 + k], stats[:, 2 + k])
                    i.then_inc(s["var2"], 1)
                if live(2):
                    after(dve, s["s2_done"], t - 1)
                    for k, e in enumerate(parts(E[:, p0])):
                        i = dve.tensor_reduce(mx[:, 1, 8 * k:8 * k + 8], e, AX_X, ALU.max)
                    i.then_inc(s["max2"], 1)
                if live(0):
                    after(dve, s["rstd2"], t + 1)
                    for k in range(2):
                        i = dve.tensor_scalar(hidn[:, k, 0:D], X[:, 64 * k:64 * k + 64], mv[:, 2 + k, 0:1], rstd[:, 2 + k:3 + k], ALU.subtract, ALU.mult)
                    i.then_inc(s["hid_ready"], 1)
                if live(2):
                    after(dve, s["max2"], t - 1)
                    for k, (e, w) in enumerate(zip(parts(E[:, p0]), (HALF, T))):
                        i = dve.tensor_tensor(e, e, spread(mx[:, 1, 8 * k:8 * k + 8], w), ALU.subtract)
                    i.then_inc(s["x2_ready"], 1)
                if live(1):
                    after(dve, s["e1_ready"], t)
                    dve.tensor_tensor_scan(R[:, 0:SA][:, ::-1], cont[:, ::-1], E[:, p1, ::-1], 0.0, ALU.mult, ALU.add).then_inc(s["scan_done"], 1)
                    after(dve, s["scan_done"], t)
                    for k, ap in enumerate(parts(R)):
                        i = dve.reciprocal(rT[:, 8 * k:8 * k + 8], ap[:, :, 0])
                    i.then_inc(s["recip1"], 1)
                if live(4):
                    after(dve, s["out_done"], t - 3)
                    hv = h_all[:, bass.ds(t - 4, 1)].rearrange("p u s d -> p (u s) d")
                    dve.tensor_tensor(hv, X[:, 0:128].rearrange("p (s d) -> p s d", s=2), hv, ALU.add).then_inc(s["h_written"], 1)
                if live(1):
                    dve.tensor_tensor(E[:, p1], R[:, 1:SA + 1], posg[:], ALU.mult).then_inc(s["dist1"], 1)
                    after(dve, s["recip1"], t)
                    after(dve, s["dist1"], t)
                    for k, (e, w) in enumerate(zip(parts(E[:, p1]), (HALF, T))):
                        i = dve.scalar_tensor_tensor(out=e, in0=e, scalar=1e-16, in1=spread(rT[:, 8 * k:8 * k + 8], w), op0=ALU.max, op1=ALU.mult)
                    i.then_inc(s["d_ready"], 1)
            each_pair(dve, 4, body, 4)

        @block.scalar
        def _(act):
            act.preload_act_table_set("natural_log_exp_and_others")
            act.wait_ge(loaded, 16 * len(consts))
            act.wait_ge(zeroed, 11)
            act.activation(gtmp[:], gam[:], ACT.Abs).then_inc(g_step, 1)
            act.wait_ge(g_step, 1)
            act.activation(gtmp[:], gtmp[:], ACT.Exp, scale=-1.0).then_inc(g_step, 1)
            act.wait_ge(g_step, 2)
            act.activation(gtmp[:], gtmp[:], ACT.Ln, bias=1.0).then_inc(g_step, 1)

            def turned(t, r):
                after(act, s["pt_turned"], (t - 3) * 4 + r + 1)
                if r == 0:
                    after(act, s["pv_done"], t - 3)
                if r < 2:
                    act.activation(PTL[:, 4 * r:4 * r + 4].rearrange("p h n -> p (h n)"), Y[0:64], ACT.Copy).then_inc(s["pt_ready"], 1)
                else:
                    act.activation(PTH[:, 4 * r - 8:4 * r - 4].rearrange("p h n -> p (h n)"), Y, ACT.Copy).then_inc(s["pt_ready"], 1)

            def body(t, par, live):
                p0, p1 = par % 2, 1 - par % 2
                if live(2):
                    after(act, s["d_ready"], t - 1)
                    act.activation(E[:, p0], E[:, p0], ACT.Ln).then_inc(s["ln_d"], 1)
                if live(0):
                    after(act, s["var1"], t + 1)
                    act.activation(lnv[:, 0:2], mv[:, 0:2, 1], ACT.Ln, bias=EPS).then_inc(s["ln1"], 1)
                    after(act, s["ln1"], t + 1)
                    act.activation(rstd[:, 0:2], lnv[:, 0:2], ACT.Exp, scale=-0.5).then_inc(s["rstd1"], 1)
                if live(2):
                    after(act, s["ln_d"], t - 1)
                    act.activation(E[:, p0], E[:, p0], ACT.Exp, scale=0.5).then_inc(s["exp_d"], 1)
                if live(0):
                    after(act, s["x_turned"], t + 1)
                    act.activation(xT[0:64, :, 4:4 + T].rearrange("p g (s t) -> p s g t", s=2),
                                   X[0:64, 0:256].rearrange("p (s g t) -> p s g t", s=2, g=2), ACT.Copy).then_inc(s["xT_ready"], 1)
                if live(3):
                    turned(t, 0)
                if live(2):
                    after(act, s["exp_d"], t - 1)
                    act.activation(E[:, p0], E[:, p0], ACT.Exp, scale=-1.0).then_inc(s["eff_ready"], 1)
                if live(3):
                    turned(t, 1)
                if live(1):
                    after(act, s["x1_ready"], t)
                    act.activation(E[:, p1], E[:, p1], ACT.Exp).then_inc(s["e1_ready"], 1)
                if live(0):
                    after(act, s["var2"], t + 1)
                    act.activation(lnv[:, 2:4], mv[:, 2:4, 1], ACT.Ln, bias=1e-12).then_inc(s["ln2"], 1)
                    after(act, s["ln2"], t + 1)
                    act.activation(rstd[:, 2:4], lnv[:, 2:4], ACT.Exp, scale=-0.5).then_inc(s["rstd2"], 1)
                if live(3):
                    turned(t, 2)
                if live(4):
                    after(act, s["a_turned"], t - 3)
                    act.activation(aT[0:64].rearrange("p s n -> p (s n)"), X[0:64, 0:256], ACT.Copy).then_inc(s["aT_ready"], 1)
                if live(3):
                    turned(t, 3)
                if live(0):
                    after(act, s["hid_turned"], t + 1)
                    act.activation(hT[0:64].rearrange("p g (s t) -> p s g t", s=2),
                                   X[0:64, 0:256].rearrange("p (s g t) -> p s g t", s=2, g=2), ACT.Copy).then_inc(s["hT_ready"], 1)
                    after(act, s["q_done"], t + 1)
                    after(act, s["s_done"], t)
                    act.activation(QT[:].rearrange("p s n -> p (s n)"), Y, ACT.Copy).then_inc(s["q_ready"], 1)
                    after(act, s["k_done"], t + 1)
                    for i in range(4):
                        r = slice(32 * i, 32 * i + 32)
                        ins = act.activation(KT[r, :, i], Y[r].rearrange("p (s n) -> p s n", s=2), ACT.Copy)
                    ins.then_inc(s["k_ready"], 1)
                    after(act, s["v_done"], t + 1)
                    act.activation(V9[:, par, :, :, 0:DK], X[:, 0:128].rearrange("p (g h e) -> p g h e", g=2, h=H0), ACT.Copy)\
                       .then_inc(s["v_ready"], 1)
                if live(2):
                    after(act, s["x2_ready"], t - 1)
                    after(act, s["pt_turned"], (t - 2) * 4)
                    act.activation(P[:], E[:, p0], ACT.Exp).then_inc(s["p_ready"], 1)
            each_pair(act, 4, body, 4)

        @block.tensor
        def _(pe):
            pe.wait_ge(loaded, 16 * len(consts))
            pe.wait_ge(zeroed, 11)
            pe.matmul(X[0:65, 0:512], lnb_sel[:], wraw[0:64, 0:512], start=True, stop=True)
            pe.matmul(Y[0:65, 0:64], lnb_sel[:], wraw[0:64, 512:576], start=True, stop=True).then_inc(fold_mm, 1)
            pe.wait_ge(fold, 16)

            def turn(t, r):
                if r == 0:
                    after(pe, s["p_ready"], t - 2)
                    after(pe, s["k_ready"], last(t))
                else:
                    after(pe, s["pt_ready"], (t - 3) * 4 + r)
                for n in range(4):
                    h = 4 * (r % 2) + n
                    base = HALF * h if r < 2 else SL + T * h
                    i = pe.transpose(Y[:, 128 * n:128 * n + 128], P[:, base:base + 128], ident[:])
                i.then_inc(s["pt_turned"], 1)

            def body(t, par, live):
                p0 = par % 2
                if live(0):
                    after(pe, s["x_ready"], t + 1)
                    after(pe, s["att_ready"], t - 3)
                    for k in range(2):
                        i = pe.transpose(X[:, 128 * k:128 * k + 128], xh[:, k], ident[:])
                    i.then_inc(s["x_turned"], 1)
                if live(3):
                    turn(t, 0)
                    turn(t, 1)
                if live(0):
                    after(pe, s["xT_ready"], t + 1)
                    for k in range(2):
                        for g in range(2):
                            for tap in range(5):
                                i = pe.matmul(X[64 * g:64 * g + 64, 64 * k:64 * k + 64], xT[:, g, HALF * k + tap:HALF * k + tap + HALF],
                                              convw[:, tap], start=tap == 0, stop=tap == 4)
                    i.then_inc(s["conv_done"], 1)
                if live(3):
                    turn(t, 2)
                if live(4):
                    after(pe, s["att_ready"], t - 3)
                    after(pe, s["hid_ready"], last(t + 1))
                    for k in range(2):
                        i = pe.transpose(X[:, 128 * k:128 * k + 128], att[:, k], ident[:])
                    i.then_inc(s["a_turned"], 1)
                if live(3):
                    turn(t, 3)
                if live(0):
                    after(pe, s["hid_ready"], t + 1)
                    after(pe, s["aT_ready"], t - 3)
                    for k in range(2):
                        i = pe.transpose(X[:, 128 * k:128 * k + 128], hidn[:, k], ident[:])
                    i.then_inc(s["hid_turned"], 1)
                    after(pe, s["hT_ready"], t + 1)
                    after(pe, s["pt_ready"], (t - 2) * 4)
                    hTf = hT[:].rearrange("p g n -> p (g n)")
                    for k in range(2):
                        i = pe.matmul(Y[:, 256 * k:256 * k + 256], waug[:, 128 * k:128 * k + 128], hTf, start=True, stop=True)
                    i.then_inc(s["q_done"], 1)
                if live(4):
                    after(pe, s["aT_ready"], t - 3)
                    after(pe, s["hT_ready"], last(t + 1))
                    for k in range(2):
                        i = pe.matmul(X[:, 64 * k:64 * k + 64], aT[:, k], wo[:], start=True, stop=True)
                    i.then_inc(s["out_done"], 1)
                if live(0):
                    after(pe, s["q_ready"], t + 1)
                    for k in range(2):
                        i = pe.matmul(Y[:, 256 * k:256 * k + 256], waug[:, 256 + 128 * k:384 + 128 * k], hTf, start=True, stop=True)
                    i.then_inc(s["k_done"], 1)
                    after(pe, s["h_written"], t - 3)
                    for g in range(2):
                        i = pe.matmul(X[:, 64 * g:64 * g + 64], hT[:, g], waug[:, 512:576], start=True, stop=True)
                    i.then_inc(s["v_done"], 1)
                if live(3):
                    after(pe, s["pt_ready"], (t - 2) * 4)
                    after(pe, s["v_ready"], last(t + 1))
                    after(pe, s["h_written"], t - 3)
                    v = V9[:, (par + 1) % 4]
                    for h in range(H0):
                        pe.matmul(O[:, h].rearrange("p g e -> p (g e)"), PTL[:, h], v[0:64, :, h], start=True, stop=True)
                    for h in range(H0):
                        i = pe.matmul(O[:, H0 + h].rearrange("p g e -> p (g e)"), PTH[:, h], v[:, :, h], start=True, stop=True)
                    i.then_inc(s["pv_done"], 1)
                if live(0):
                    after(pe, s["k_ready"], t + 1)
                    after(pe, s["s2_done"], t - 1)
                    S = S2[p0]
                    pe.matmul(S[:, 0:512], identb[:], maskl[:], start=True, stop=False, skip_group_check=True)
                    for b in (1, 2):
                        pe.matmul(S[:, 512 * b:512 * b + 512], identb[:], maskh[:], start=True, stop=False, skip_group_check=True)
                    for h in range(H0):
                        for k, base, w in ((0, HALF * h, HALF), (1, SL + T * h, T)):
                            for g in range(2):
                                i = pe.matmul(S[64 * g:64 * g + 64, base:base + w], QT[:, h // 4, T * g + HALF * k:T * g + HALF * k + HALF],
                                              KT[:, h // 4, h % 4, T * g:T * g + w], start=False, stop=True, skip_group_check=True)
                    i.then_inc(s["s_done"], 1)
            each_pair(pe, 4, body, 4)


def mixture_stage(st, c):
    nc, a, psum, h_all, ident = st.nc, st.a, st.psum, st.h_all, st.ident

    def sb(n, s, dt=F32):
        return st.sb("moe_" + n, s, dt, c)

    def sem(n):
        return st.sem("moe_" + n)

    NP = NEXP // 2
    w1, sel, w2 = sb("w1", [128, NP, 128]), sb("sel", [128, NP, 128]), sb("w2", [128, NP, D])
    b2, router, iota = sb("b2", [128, D]), sb("router", [128, NEXP]), sb("iota", [128, 2, NEXP])
    hcur, hnew = sb("hcur", [128, 2, D]), sb("hnew", [128, 2, D])
    tok = sb("tok", [128, 2, 128])
    tokT, xT = sb("tokT", [128, 2, 2 * T]), sb("xT", [128, 2 * T])
    lg, m8, i8, fi = sb("lg", [128, 2, NEXP]), sb("m8", [128, 2, 8]), sb("i8", [128, 2, 8], mybir.dt.uint32), sb("fi", [128, 2, 8])
    d12, e12, w12 = sb("d12", [128, 2]), sb("e12", [128, 2]), sb("w12", [128, 2, 2])
    den = sb("den", [128, 2])
    eq = sb("eq", [128, 2, 2, NEXP])
    G = sb("G", [128, NP, 2 * T])
    stats, mv, lnv, rstd = sb("stats", [128, 2, 6]), sb("mv", [128, 2, 2]), sb("lnv", [128, 2]), sb("rstd", [128, 2])
    scrap = sb("scrap", [128, 1])
    pX, pW, pH, pC, pY = psum[:, 0], psum[:, 1], psum[:, 2:4], psum[:, 4:6], psum[:, 6]

    names = """h_copied stats1 var1 ln1 rstd1 t_ready t_turned xT_ready logits lg_ready max_done idx_done fi_done d_done e_done
               lg_ready2 den_done w1_done w2_done eq_done c_done w_turned tokT_ready up_done gelu_done cb_done g_ready down_done h_written x_added""".split()
    s = {n: sem(n) for n in names}
    loaded, zeroed = sem("loaded"), sem("zeroed")
    consts = [(w1[:], a["m_w1"]), (sel[:], a["c_sel"]), (w2[:], a["m_w2"]), (b2[:], a["m_b2"]), (router[:], a["m_router"]), (iota[:], a["c_iota"]), (tok[:], a["c_tok"])]

    with nc.Block() as block:
        @block.sync
        def _(sp):
            for dst, src in consts:
                sp.dma_start(dst, src).then_inc(loaded, 16)

        @block.vector
        def _(dve):
            def carry():
                dve.tensor_copy(scrap[:], ident[:, 0:1])

            dve.wait_ge(loaded, 16 * len(consts))

            def body(t, par, live):
                q = 1 - par
                if live(0):
                    dve.tensor_copy(hcur[:], h_all[:, bass.ds(t, 1)].rearrange("p u s d -> p (u s) d")).then_inc(s["h_copied"], 1)
                    after(dve, s["h_copied"], t + 1)
                    for k in range(2):
                        i = dve.bn_stats(stats[:, k], hcur[:, k])
                    i.then_inc(s["stats1"], 1)
                    after_all(dve, carry, (s["stats1"], t + 1))
                    for k in range(2):
                        i = dve.bn_aggr(mv[:, k], stats[:, k])
                    i.then_inc(s["var1"], 1)
                if live(1):
                    after(dve, s["gelu_done"], t)
                    after(dve, s["cb_done"], t)
                    for k in range(2):
                        g = G[:, 2 * k:2 * k + 2].rearrange("p e n -> p (e n)")
                        i = dve.tensor_tensor(g, g, pC[:, k], ALU.mult)
                    i.then_inc(s["g_ready"], 1)
                if live(0):
                    after(dve, s["rstd1"], t + 1)
                    for k in range(2):
                        i = dve.tensor_scalar(tok[:, k, 0:D], hcur[:, k], mv[:, k, 0:1], rstd[:, k:k + 1], ALU.subtract, ALU.mult)
                    i.then_inc(s["t_ready"], 1)
                    after(dve, s["t_ready"], t + 1)
                    dve.tensor_tensor(h_all[:, bass.ds(t, 1)].rearrange("p u s d -> p (u s) d"), hcur[:], tok[:, :, 0:D], ALU.add)\
                       .then_inc(s["x_added"], 1)
                    after(dve, s["logits"], t + 1)
                    dve.tensor_copy(lg[:].rearrange("p k e -> p (k e)"), pX[:, 0:16]).then_inc(s["lg_ready"], 1)
                    after_all(dve, carry, (s["lg_ready"], t + 1))
                    for k in range(2):
                        i = dve.max(m8[:, k], lg[:, k])
                    i.then_inc(s["max_done"], 1)
                    after_all(dve, carry, (s["max_done"], t + 1))
                    for k in range(2):
                        i = dve.max_index(i8[:, k], m8[:, k], lg[:, k])
                    i.then_inc(s["idx_done"], 1)
                    dve.tensor_tensor(d12[:], m8[:, :, 1], m8[:, :, 0], ALU.subtract).then_inc(s["d_done"], 1)
                    after(dve, s["idx_done"], t + 1)
                    dve.tensor_copy(fi[:], i8[:]).then_inc(s["fi_done"], 1)
                    after(dve, s["fi_done"], t + 1)
                    for n in range(2):
                        i = dve.tensor_tensor(eq[:, n], iota[:], fi[:, :, n:n + 1].to_broadcast([128, 2, NEXP]), ALU.is_equal)
                    i.then_inc(s["eq_done"], 1)
                    after(dve, s["e_done"], t + 1)
                    dve.tensor_scalar(den[:], e12[:], 1.0, None, ALU.add).then_inc(s["den_done"], 1)
                    after(dve, s["den_done"], t + 1)
                    dve.reciprocal(w12[:, 0], den[:]).then_inc(s["w1_done"], 1)
                    after(dve, s["w1_done"], t + 1)
                    dve.tensor_tensor(w12[:, 1], w12[:, 0], e12[:], ALU.mult).then_inc(s["w2_done"], 1)
                    after(dve, s["w2_done"], t + 1)
                    after(dve, s["eq_done"], t + 1)
                    for n in range(2):
                        i = dve.tensor_tensor(eq[:, n], eq[:, n], w12[:, n].unsqueeze(2).to_broadcast([128, 2, NEXP]), ALU.mult)
                    i.then_inc(s["c_done"], 1)
                    after(dve, s["c_done"], t + 1)
                    dve.tensor_tensor(tok[:, :, 96:96 + NEXP], eq[:, 0], eq[:, 1], ALU.add).then_inc(s["lg_ready2"], 1)
                if live(1):
                    after(dve, s["down_done"], t)
                    hv = h_all[:, bass.ds(t - 1, 1)].rearrange("p u s d -> p (u s) d")
                    dve.tensor_tensor(hv, pY[:, 0:128].rearrange("p (s d) -> p s d", s=2), hv, ALU.add).then_inc(s["h_written"], 1)
            each_pair(dve, 1, body)

        @block.scalar
        def _(act):
            act.wait_ge(loaded, 16 * len(consts))

            def body(t, par, live):
                q = 1 - par
                if live(0):
                    act.preload_act_table_set("natural_log_exp_and_others")
                    after(act, s["var1"], t + 1)
                    act.activation(lnv[:], mv[:, :, 1], ACT.Ln, bias=EPS).then_inc(s["ln1"], 1)
                    after(act, s["ln1"], t + 1)
                    act.activation(rstd[:], lnv[:], ACT.Exp, scale=-0.5).then_inc(s["rstd1"], 1)
                    after(act, s["t_turned"], t + 1)
                    act.activation(xT[:], pX[:, 0:256], ACT.Copy).then_inc(s["xT_ready"], 1)
                    after(act, s["d_done"], t + 1)
                    act.activation(e12[:], d12[:], ACT.Exp).then_inc(s["e_done"], 1)
                    after(act, s["w_turned"], t + 1)
                    act.activation(tokT[:, par], pW[:, 0:256], ACT.Copy).then_inc(s["tokT_ready"], 1)
                    after(act, s["up_done"], t + 1)
                    after(act, s["down_done"], t)
                    for k in range(2):
                        i = act.activation(G[:, 2 * k:2 * k + 2].rearrange("p e n -> p (e n)"), pH[:, k], ACT.Gelu)
                    i.then_inc(s["gelu_done"], 1)
            each_pair(act, 1, body)

        @block.tensor
        def _(pe):
            pe.wait_ge(loaded, 16 * len(consts))

            def body(t, par, live):
                q = 1 - par
                if live(0):
                    after(pe, s["t_ready"], t + 1)
                    after(pe, s["lg_ready"], t)
                    for k in range(2):
                        i = pe.transpose(pX[:, 128 * k:128 * k + 128], tok[:, k], ident[:])
                    i.then_inc(s["t_turned"], 1)
                if live(1):
                    after(pe, s["g_ready"], t)
                    after(pe, s["h_written"], t - 1)
                    for k in range(2):
                        n = slice(128 * k, 128 * k + 128)
                        pe.matmul(pY[:, 64 * k:64 * k + 64], tokT[:, q, n], b2[:], start=True, stop=False)
                        for e in range(NP):
                            i = pe.matmul(pY[:, 64 * k:64 * k + 64], G[:, e, n], w2[:, e], start=False, stop=e == NP - 1)
                    i.then_inc(s["down_done"], 1)
                if live(0):
                    after(pe, s["xT_ready"], t + 1)
                    for k in range(2):
                        i = pe.matmul(pX[:, 8 * k:8 * k + 8], xT[:, 128 * k:128 * k + 128], router[:], start=True, stop=True)
                    i.then_inc(s["logits"], 1)
                    after(pe, s["lg_ready2"], t + 1)
                    after(pe, s["tokT_ready"], t)
                    for k in range(2):
                        i = pe.transpose(pW[:, 128 * k:128 * k + 128], tok[:, k], ident[:])
                    i.then_inc(s["w_turned"], 1)
                    after(pe, s["tokT_ready"], t + 1)
                    after(pe, s["gelu_done"], t)
                    for e in range(NP):
                        i = pe.matmul(pH[:, e // 2, 256 * (e % 2):256 * (e % 2) + 256], w1[:, e], tokT[:, par], start=True, stop=True)
                    i.then_inc(s["up_done"], 1)
                    for e in range(NP):
                        i = pe.matmul(pC[:, e // 2, 256 * (e % 2):256 * (e % 2) + 256], sel[:, e], tokT[:, par], start=True, stop=True)
                    i.then_inc(s["cb_done"], 1)
            each_pair(pe, 1, body)


def window_attention_stage(st, c):
    nc, a, psum, h_all, ident = st.nc, st.a, st.psum, st.h_all, st.ident

    def sb(n, s, dt=F32):
        return st.sb("wa_" + n, s, dt, c)

    def sem(n):
        return st.sem("wa_" + n)

    NG = NH1 + 2
    W = NG * C1
    PIECES = [(0, 0, 16, 0, 32), (1, 0, 0, 16, 48), (2, 0, 0, 48, 16), (2, 1, 16, 0, 32), (3, 1, 0, 16, 48)]
    wqkv, wn = sb("wqkv", [D, W]), sb("wn", [128, W])
    cosq, sinq = sb("cosq", [128, 2 * NG, 8]), sb("sinq", [128, 2 * NG, 8])
    coso, sino = sb("coso", [128, NBLK, 8]), sb("sino", [128, NBLK, 8])
    mask, identb = sb("mask", [128, NBLK * KW], BF16), sb("identb", [128, 128], BF16)
    wg, wo4 = sb("wg", [C1, NH1, 65]), sb("wo4", [64, 2, D])
    mrow, mw = sb("mrow", [65, NH1, D]), sb("mw", [65, NH1, D])
    hcur, x, xT = sb("hcur", [128, 2, D]), sb("x", [128, 2, 128]), sb("xT", [D, 2 * T])
    sq, ms, lnms, rn = sb("sq", [128, 2, W]), sb("ms", [128, 2 * NG]), sb("lnms", [128, 2 * NG]), sb("rn", [128, 2 * NG])
    qkv = sb("qkv", [128, 4, 2, W + 1])
    rt = [sb(f"rt{i}", [128, 2 * NG, 8]) for i in range(4)]
    ro = [sb(f"ro{i}", [128, NBLK, 8]) for i in range(4)]
    QT, KT = sb("QT", [C1, NBLK, NH1, QB]), sb("KT", [C1, 2, WIN + T])
    mx, P0 = sb("mx", [128, NBLK]), sb("P0", [128, NBLK, KW])
    PZ, PT = sb("PZ", [128, len(PIECES), 2, 192]), sb("PT", [128, len(PIECES) * 2, 128])
    rs, os = sb("rs", [128, NBLK]), sb("os", [128, NBLK * C1 + 64])
    OT = sb("OT", [65, 2, NH1, 128])
    stats, mv, lnv, rstd = sb("stats", [128, 2, 6]), sb("mv", [128, 2, 2]), sb("lnv", [128, 2]), sb("rstd", [128, 2])
    scrap = sb("scrap", [128, 1])
    p0, pQ, p3, pP, pO = psum[:, 0], psum[:, 1:3], psum[:, 3], psum[:, 4:6], psum[:, 6:8]
    osb = os[:, 0:NBLK * C1].rearrange("p (n c) -> p n c", n=NBLK)

    names = """h_copied stats1 var1 ln1 rstd1 x_ready x_turned xT_ready qkv_done raw_ready sq_done ms_done lnms_done rn_done n_done w_done
               r_done rope_ready q_turned k_turned q_ready k_ready s_done max_done p0_ready pz_ready p_turned p_ready pv_done
               rs_done os_done ro_done os_ready o_turned OT_ready out_done h_written""".split()
    s = {n: sem(n) for n in names}
    loaded, zeroed, fold, fold_mm = sem("loaded"), sem("zeroed"), sem("fold"), sem("fold_mm")
    consts = [(wqkv[:], a["w_qkv"]), (wn[:], a["w_norm"].partition_broadcast(128)), (cosq[:], a["c_cosq"]), (sinq[:], a["c_sinq"]),
              (coso[:], a["c_coso"]), (sino[:], a["c_sino"]), (sq[:, 0], a["c_maskw"]),
              (wg[:], a["w_g"]), (wo4[:], a["w_o"]), (mrow[:], a["w_bout"])]

    with nc.Block() as block:
        @block.sync
        def _(sp):
            for dst, src in consts:
                sp.dma_start(dst, src).then_inc(loaded, 16)

        @block.gpsimd
        def _(pool):
            for k, (buf, v) in enumerate(((x[:], 0.0), (qkv[:, :, :, W:W + 1], 1.0), (KT[:], 0.0), (PZ[:], 0.0), (os[:], 0.0), (OT[64:65], 1.0))):
                pool.memset(buf, v).then_inc(zeroed, 1)
                pool.wait_ge(zeroed, k + 1)

        @block.vector
        def _(dve):
            def carry():
                dve.tensor_copy(scrap[:], ident[:, 0:1])

            dve.wait_ge(loaded, 16 * len(consts))
            dve.wait_ge(zeroed, 6)
            dve.tensor_copy(mask[:], sq[:, 0]).then_inc(fold, 1)
            dve.tensor_copy(identb[:], ident[:]).then_inc(fold, 1)
            dve.wait_ge(fold_mm, 1)
            dve.tensor_tensor(mw[:], p0[0:65, 0:256].rearrange("p (h d) -> p h d", h=NH1), mrow[:], ALU.add).then_inc(fold, 1)

            def products(v, cos, sin, tmp):
                x1, x2 = v[:, :, C1 - ROT:C1:2], v[:, :, C1 - ROT + 1:C1:2]
                for o, (u, m) in zip(tmp, ((x1, cos), (x2, sin), (x1, sin), (x2, cos))):
                    i = dve.tensor_tensor(o, u, m, ALU.mult)
                return i

            def body(t, par, live):
                def to(d):
                    return last(t + 1 - d if d < 1 else t - (d - 1) if d > 1 else t)

                v = qkv[:, (par - 1) % 4]
                if live(0):
                    after(dve, s["x_ready"], to(1))
                    dve.tensor_copy(hcur[:], h_all[:, bass.ds(t, 1)].rearrange("p u s d -> p (u s) d")).then_inc(s["h_copied"], 1)
                if live(5):
                    after(dve, s["pv_done"], to(5))
                    for k in range(2):
                        i = dve.reciprocal(rs[:, 4 * k:4 * k + 4], pO[:, k, 0:260].rearrange("p (n e) -> p n e", e=65)[:, :, 64])
                    i.then_inc(s["rs_done"], 1)
                if live(0):
                    after(dve, s["h_copied"], to(0))
                    for k in range(2):
                        i = dve.bn_stats(stats[:, k], hcur[:, k])
                    i.then_inc(s["stats1"], 1)
                if live(5):
                    after(dve, s["rs_done"], to(5))
                    after(dve, s["o_turned"], to(6))
                    for k in range(2):
                        i = dve.tensor_tensor(osb[:, 4 * k:4 * k + 4], pO[:, k, 0:260].rearrange("p (n e) -> p n e", e=65)[:, :, 0:64],
                                              rs[:, 4 * k:4 * k + 4].unsqueeze(2).to_broadcast([128, 4, C1]), ALU.mult)
                    i.then_inc(s["os_done"], 1)
                if live(0):
                    after_all(dve, carry, (s["stats1"], to(0)))
                    for k in range(2):
                        i = dve.bn_aggr(mv[:, k], stats[:, k])
                    i.then_inc(s["var1"], 1)
                if live(1):
                    after(dve, s["sq_done"], to(1))
                    dve.tensor_reduce(ms[:], sq[:].rearrange("p k (g c) -> p (k g) c", c=C1), AX_X, ALU.add).then_inc(s["ms_done"], 1)
                if live(5):
                    after(dve, s["os_done"], to(5))
                    products(osb, coso[:], sino[:], [o[:] for o in ro]).then_inc(s["ro_done"], 1)
                if live(0):
                    after(dve, s["rstd1"], to(0))
                    after(dve, s["x_turned"], to(1))
                    for k in range(2):
                        i = dve.tensor_scalar(x[:, k, 0:D], hcur[:, k], mv[:, k, 0:1], rstd[:, k:k + 1], ALU.subtract, ALU.mult)
                    i.then_inc(s["x_ready"], 1)
                if live(5):
                    after(dve, s["ro_done"], to(5))
                    dve.tensor_tensor(osb[:, :, C1 - ROT:C1:2], ro[0][:], ro[1][:], ALU.add)
                    dve.tensor_tensor(osb[:, :, C1 - ROT + 1:C1:2], ro[3][:], ro[2][:], ALU.subtract).then_inc(s["os_ready"], 1)
                if live(3):
                    after(dve, s["s_done"], to(3))
                    sc = p3[:, 0:NBLK * KW].rearrange("p (n k) -> p n k", n=NBLK)
                    dve.tensor_reduce(mx[:], sc, AX_X, ALU.max).then_inc(s["max_done"], 1)
                if live(1):
                    after(dve, s["rn_done"], to(1))
                    for k in range(2):
                        vk = v[:, k, 0:W].rearrange("p (g c) -> p g c", g=NG)
                        i = dve.tensor_tensor(vk, vk, rn[:, NG * k:NG * k + NG].unsqueeze(2).to_broadcast([128, NG, C1]), ALU.mult)
                    i.then_inc(s["n_done"], 1)
                if live(3):
                    after(dve, s["max_done"], to(3))
                    after(dve, s["pz_ready"], to(4))
                    dve.tensor_tensor(P0[:], sc, mx[:].unsqueeze(2).to_broadcast([128, NBLK, KW]), ALU.subtract).then_inc(s["p0_ready"], 1)
                if live(1):
                    after(dve, s["n_done"], to(1))
                    for k in range(2):
                        i = dve.tensor_tensor(v[:, k, 0:W], v[:, k, 0:W], wn[:], ALU.mult)
                    i.then_inc(s["w_done"], 1)
                    after(dve, s["w_done"], to(1))
                    for k in range(2):
                        g = slice(NG * k, NG * k + NG)
                        i = products(v[:, k, 0:W].rearrange("p (g c) -> p g c", g=NG), cosq[:, g], sinq[:, g], [o[:, g] for o in rt])
                    i.then_inc(s["r_done"], 1)
                if live(6):
                    after(dve, s["out_done"], to(6))
                    hv = h_all[:, bass.ds(t - 6, 1)].rearrange("p u s d -> p (u s) d")
                    dve.tensor_tensor(hv, p0[:, 0:128].rearrange("p (s d) -> p s d", s=2), hv, ALU.add).then_inc(s["h_written"], 1)
                if live(1):
                    after(dve, s["r_done"], to(1))
                    for k in range(2):
                        g = slice(NG * k, NG * k + NG)
                        vk = v[:, k, 0:W].rearrange("p (g c) -> p g c", g=NG)
                        dve.tensor_tensor(vk[:, :, C1 - ROT:C1:2], rt[0][:, g], rt[1][:, g], ALU.subtract)
                        i = dve.tensor_tensor(vk[:, :, C1 - ROT + 1:C1:2], rt[2][:, g], rt[3][:, g], ALU.add)
                    i.then_inc(s["rope_ready"], 1)
            each_pair(dve, 6, body, 4)

        @block.scalar
        def _(act):
            act.preload_act_table_set("natural_log_exp_and_others")
            act.wait_ge(loaded, 16 * len(consts))
            act.wait_ge(zeroed, 6)
            act.wait_ge(fold, 2)

            def body(t, par, live):
                def to(d):
                    return last(t + 1 - d if d < 1 else t - (d - 1) if d > 1 else t)

                if live(1):
                    after(act, s["raw_ready"], to(1))
                    after(act, s["ms_done"], to(2))
                    act.activation(sq[:], qkv[:, (par - 1) % 4, :, 0:W], ACT.Square).then_inc(s["sq_done"], 1)
                if live(0):
                    after(act, s["var1"], to(0))
                    act.activation(lnv[:], mv[:, :, 1], ACT.Ln, bias=EPS).then_inc(s["ln1"], 1)
                    after(act, s["ln1"], to(0))
                    act.activation(rstd[:], lnv[:], ACT.Exp, scale=-0.5).then_inc(s["rstd1"], 1)
                if live(6):
                    after(act, s["o_turned"], to(6))
                    after(act, s["out_done"], to(7))
                    for k in range(2):
                        i = act.activation(OT[0:64, k].rearrange("p h (n q) -> p n h q", n=4), pP[0:64, k].rearrange("p (n h q) -> p n h q", n=4, h=NH1), ACT.Copy)
                    i.then_inc(s["OT_ready"], 1)
                if live(1):
                    after(act, s["ms_done"], to(1))
                    act.activation(lnms[:], ms[:], ACT.Ln, bias=1e-8, scale=1.0 / C1).then_inc(s["lnms_done"], 1)
                if live(0):
                    after(act, s["x_turned"], to(0))
                    act.activation(xT[:], p0[0:64, 0:256], ACT.Copy).then_inc(s["xT_ready"], 1)
                if live(1):
                    after(act, s["lnms_done"], to(1))
                    act.activation(rn[:], lnms[:], ACT.Exp, scale=-0.5).then_inc(s["rn_done"], 1)
                if live(2):
                    after(act, s["q_turned"], to(2))
                    after(act, s["s_done"], to(3))
                    for k in range(2):
                        i = act.activation(QT[:, 4 * k:4 * k + 4].rearrange("p n h q -> p h n q"), pQ[0:64, k].rearrange("p (h n q) -> p h n q", h=NH1, n=4), ACT.Copy)
                    i.then_inc(s["q_ready"], 1)
                    after(act, s["k_turned"], to(2))
                    act.activation(KT[:, :, WIN:].rearrange("p g (k t) -> p k g t", k=2), p0[0:64, 0:256].rearrange("p (k g t) -> p k g t", k=2, g=2), ACT.Copy)\
                       .then_inc(s["k_ready"], 1)
                if live(4):
                    for r in range(3):
                        after(act, s["p_turned"], (t - 4) * 3 + r + 1)
                        n = 4 if r < 2 else 2
                        act.activation(PT[:, 4 * r:4 * r + n].rearrange("p m n -> p (m n)"), pP[:, r % 2, 0:128 * n], ACT.Copy).then_inc(s["p_ready"], 1)
                if live(3):
                    after(act, s["p0_ready"], to(3))
                    after(act, s["p_turned"], (t - 3) * 3)
                    for n, (kind, _, w0, k0, w) in enumerate(PIECES):
                        b = 4 * (kind // 2) + kind % 2
                        i = act.activation(PZ[:, n, :, k0:k0 + w], P0[:, b:b + 3:2, w0:w0 + w], ACT.Exp, scale=C1 ** -0.5)
                    i.then_inc(s["pz_ready"], 1)
                if live(0):
                    after(act, s["qkv_done"], to(0))
                    after(act, s["pv_done"], to(4))
                    act.activation(qkv[:, par, :, 0:W], pQ[:, :, 0:W], ACT.Copy).then_inc(s["raw_ready"], 1)
            each_pair(act, 6, body, 4)

        @block.tensor
        def _(pe):
            pe.wait_ge(loaded, 16 * len(consts))
            pe.wait_ge(zeroed, 6)
            for h in range(NH1):
                i = pe.matmul(p0[0:65, 64 * h:64 * h + 64], wg[:, h], wo4[:, h // 2], start=True, stop=True)
            i.then_inc(fold_mm, 1)
            pe.wait_ge(fold, 3)

            def turn(t, rounds):
                for r in rounds:
                    for m in range(4 * r, min(4 * r + 4, 10)):
                        i = pe.transpose(pP[:, r % 2, 128 * (m % 4):128 * (m % 4) + 128], PZ[:, m // 2].rearrange("p g n -> p (g n)")[:, 128 * (m % 2):128 * (m % 2) + 128], ident[:])
                    i.then_inc(s["p_turned"], 1)

            def body(t, par, live):
                def to(d):
                    return last(t + 1 - d if d < 1 else t - (d - 1) if d > 1 else t)

                if live(6):
                    after(pe, s["os_ready"], to(6))
                    after(pe, s["p_ready"], 3 * to(5))
                    for n in range(NBLK):
                        i = pe.transpose(pP[:, n // 4, 128 * (n % 4):128 * (n % 4) + 128], os[:, C1 * n:C1 * n + 128], ident[:])
                    i.then_inc(s["o_turned"], 1)
                if live(3):
                    after(pe, s["k_ready"], to(3))
                    after(pe, s["p0_ready"], to(4))
                    pe.matmul(p3[:, 0:NBLK * KW], identb[:], mask[:], start=True, stop=False, skip_group_check=True)
                    for n in range(NBLK):
                        k, g, b = n // 4, n // 2 % 2, n % 2
                        i = pe.matmul(p3[:, KW * n:KW * n + KW], QT[:, n].rearrange("p h q -> p (h q)"), KT[:, g, 64 * k + 32 * b:64 * k + 32 * b + KW],
                                      start=False, stop=True, skip_group_check=True)
                    i.then_inc(s["s_done"], 1)
                if live(2):
                    after(pe, s["rope_ready"], to(2))
                    after(pe, s["raw_ready"], to(1))
                    for k in range(2):
                        for h in range(NH1):
                            i = pe.transpose(pQ[:, k, 128 * h:128 * h + 128], qkv[:, (par - 2) % 4, k, 64 * h:64 * h + 128], ident[:])
                    i.then_inc(s["q_turned"], 1)
                if live(0):
                    after(pe, s["x_ready"], to(0))
                    after(pe, s["h_written"], to(7))
                    for k in range(2):
                        i = pe.transpose(p0[:, 128 * k:128 * k + 128], x[:, k], ident[:])
                    i.then_inc(s["x_turned"], 1)
                if live(4):
                    after(pe, s["pz_ready"], to(4))
                    after(pe, s["OT_ready"], to(6))
                    turn(t, (0, 1))
                if live(2):
                    after(pe, s["xT_ready"], to(0))
                    for k in range(2):
                        i = pe.transpose(p0[:, 128 * k:128 * k + 128], qkv[:, (par - 2) % 4, k, 256:384], ident[:])
                    i.then_inc(s["k_turned"], 1)
                if live(0):
                    after(pe, s["xT_ready"], to(0))
                    after(pe, s["q_ready"], to(2))
                    for k in range(2):
                        i = pe.matmul(pQ[:, k, 0:W], xT[:, 128 * k:128 * k + 128], wqkv[:], start=True, stop=True)
                    i.then_inc(s["qkv_done"], 1)
                if live(4):
                    after(pe, s["p_ready"], (t - 4) * 3 + 1)
                    turn(t, (2,))
                if live(6):
                    after(pe, s["OT_ready"], to(6))
                    after(pe, s["k_ready"], to(2))
                    after(pe, s["h_written"], to(7))
                    for k in range(2):
                        for h in range(NH1):
                            i = pe.matmul(p0[:, 64 * k:64 * k + 64], OT[:, k, h], mw[:, h], start=h == 0, stop=h == NH1 - 1)
                    i.then_inc(s["out_done"], 1)
                if live(4):
                    after(pe, s["p_ready"], (t - 4) * 3 + 3)
                    after(pe, s["os_done"], to(5))
                    for n in range(NBLK):
                        kind, g = 2 * (n // 4) + n % 2, n // 2 % 2
                        mine = [(m, p[1]) for m, p in enumerate(PIECES) if p[0] == kind]
                        for j, (m, k) in enumerate(mine):
                            i = pe.matmul(pO[:, n // 4, 65 * (n % 4):65 * (n % 4) + 65], PT[:, 2 * m + g], qkv[:, par, k, 320:385],
                                          start=j == 0, stop=j == len(mine) - 1)
                    i.then_inc(s["pv_done"], 1)
            each_pair(pe, 6, body, 4)


def routed_stage(st, c):
    nc, a, psum, h_all, ident, out = st.nc, st.a, st.psum, st.h_all, st.ident, st.out

    def sb(n, s, dt=F32):
        return st.sb("rf_" + n, s, dt, c)

    def sem(n):
        return st.sem("rf_" + n)

    wi, ws, wo = sb("wi", [D, HID]), sb("ws", [128, 2, HID + 1]), sb("wo", [HID, D])
    bi, bo, ones = sb("bi", [HID, 1]), sb("bo", [1, D]), sb("ones", [1, 128])
    eye = sb("eye", [128, 2, HID + 1])
    ri, rf, rv, rw, rx = sb("ri", [1, PAIRS], I32), sb("rf", [1, PAIRS]), sb("rv", [1, PAIRS]), sb("rw", [1, PAIRS]), sb("rx", [1, PAIRS], I32)
    wsel, weff = sb("wsel", [128, 2, 2, HID + 1]), sb("weff", [128, 2, 2, HID + 1])
    hcur, x, xT = sb("hcur", [128, 2, D]), sb("x", [128, 2, 128]), sb("xT", [D, 2 * T])
    H1, H2, H3 = sb("H1", [HID, 2, 2 * T]), sb("H2", [HID, 2 * T]), sb("H3", [HID, 2 * T])
    fin = sb("fin", [128, 2, 2, D])
    stats, mv, lnv, rstd = sb("stats", [128, 2, 6]), sb("mv", [128, 2, 2]), sb("lnv", [128, 2]), sb("rstd", [128, 2])
    scrap = sb("scrap", [128, 1])
    pX, pA, pB, pC, pO = (psum[:, k] for k in range(5))

    names = """h_copied stats1 var1 ln1 rstd1 x_ready x_turned xT_ready in_done H1_ready l1_done H2_ready l2_done H3_ready
               out_done fin_ready weff_ready""".split()
    s = {n: sem(n) for n in names}
    loaded, zeroed, fold = sem("loaded"), sem("zeroed"), sem("fold")
    w_loaded, stored = [sem("w_loaded0"), sem("w_loaded1")], [sem("stored0"), sem("stored1")]
    consts = [(wi[:], a["r_wi"]), (ws[:], a["r_ws"]), (wo[:], a["r_wo"]), (bi[:], a["r_bi"]), (bo[:], a["r_bo"]), (eye[:], a["c_eye"]), (ri[:], a["r_route"])]

    def count16(t, par):
        return (t // 2 + 1) * 16 if isinstance(t, int) else (t + (2 - par)) * 8

    with nc.Block() as block:
        @block.sync
        def _(sp):
            for dst, src in consts:
                sp.dma_start(dst, src).then_inc(loaded, 16)
            sp.wait_ge(fold, 6)

            def body(t, par, live):
                q = 1 - par
                if live(0):
                    after(sp, s["weff_ready"], t - 1)
                    n = sp.value_load(rx[0:1, bass.ds(t, 1)], min_val=0, max_val=NRT)
                    sp.dma_start(wsel[:, par].rearrange("p l n -> p (l n)"), a["r_wr"][bass.ds(n, 1)].rearrange("e p n -> (e p) n")).then_inc(w_loaded[par], 16)
            each_pair(sp, 0, body)

        @block.gpsimd
        def _(pool):
            for k, (buf, v) in enumerate(((x[:], 0.0), (ones[:], 1.0))):
                pool.memset(buf, v).then_inc(zeroed, 1)
                pool.wait_ge(zeroed, k + 1)
            pool.wait_ge(fold, 7)

            def body(t, par, live):
                after(pool, s["fin_ready"], t + 1)
                for g in range(2):
                    pool.dma_start(out[bass.ds(2 * t + g, 1)].rearrange("b (s t) d -> t (b s) d", s=2), fin[64 * g:64 * g + 64, par]).then_inc(stored[par], 16)
            each_pair(pool, 0, body)
            for k in range(2):
                pool.wait_ge(stored[k], 32 * PAIRS // 2)

        @block.vector
        def _(dve):
            def carry():
                dve.tensor_copy(scrap[:], ident[:, 0:1])

            dve.wait_ge(loaded, 16 * len(consts))
            dve.wait_ge(zeroed, 2)
            n = [0]

            def link(ins):
                n[0] += 1
                ins.then_inc(fold, 1)
                dve.wait_ge(fold, n[0])
            link(dve.tensor_copy(rf[:], ri[:]))
            link(dve.tensor_scalar(rv[:], rf[:], 0.0, None, ALU.is_ge))
            link(dve.tensor_scalar(rw[:], rf[:], float(NRT - 1), None, ALU.is_le))
            link(dve.tensor_tensor(rv[:], rv[:], rw[:], ALU.mult))
            link(dve.scalar_tensor_tensor(out=rf[:], in0=rf[:], scalar=float(-NRT), in1=rv[:], op0=ALU.add, op1=ALU.mult))
            link(dve.tensor_scalar(rx[:], rf[:], float(NRT), None, ALU.add))
            link(dve.tensor_tensor(ws[:], ws[:], eye[:], ALU.add))

            def body(t, par, live):
                q = 1 - par
                if live(0):
                    after(dve, w_loaded[par], count16(t, par))
                    after(dve, s["H3_ready"], t - 1)
                    dve.tensor_tensor(weff[:, par], wsel[:, par], ws[:], ALU.add).then_inc(s["weff_ready"], 1)
                    after(dve, s["x_ready"], t)
                    dve.tensor_copy(hcur[:], h_all[:, bass.ds(t, 1)].rearrange("p u s d -> p (u s) d")).then_inc(s["h_copied"], 1)
                    after(dve, s["h_copied"], t + 1)
                    for k in range(2):
                        i = dve.bn_stats(stats[:, k], hcur[:, k])
                    i.then_inc(s["stats1"], 1)
                    after_all(dve, carry, (s["stats1"], t + 1))
                    for k in range(2):
                        i = dve.bn_aggr(mv[:, k], stats[:, k])
                    i.then_inc(s["var1"], 1)
                    after(dve, s["rstd1"], t + 1)
                    after(dve, s["x_turned"], t)
                    for k in range(2):
                        i = dve.tensor_scalar(x[:, k, 0:D], hcur[:, k], mv[:, k, 0:1], rstd[:, k:k + 1], ALU.subtract, ALU.mult)
                    i.then_inc(s["x_ready"], 1)
                if live(2):
                    after(dve, s["out_done"], t - 1)
                    if not isinstance(t, int) or t >= 4:
                        after(dve, stored[par], count16(t - 4, par) * 2)
                    dve.tensor_tensor(fin[:, par], pO[:, 0:128].rearrange("p (s d) -> p s d", s=2),
                                      h_all[:, bass.ds(t - 2, 1)].rearrange("p u s d -> p (u s) d"), ALU.add).then_inc(s["fin_ready"], 1)
            each_pair(dve, 2, body)

        @block.scalar
        def _(act):
            act.preload_act_table_set("natural_log_exp_and_others")
            act.wait_ge(loaded, 16 * len(consts))

            def body(t, par, live):
                q = 1 - par
                if live(0):
                    after(act, s["var1"], t + 1)
                    act.activation(lnv[:], mv[:, :, 1], ACT.Ln, bias=EPS).then_inc(s["ln1"], 1)
                    after(act, s["ln1"], t + 1)
                    act.activation(rstd[:], lnv[:], ACT.Exp, scale=-0.5).then_inc(s["rstd1"], 1)
                if live(1):
                    after(act, s["l1_done"], t)
                    act.activation(H2[:], pB[:, 0:256], ACT.Relu, bias=weff[:, q, 0, HID:HID + 1]).then_inc(s["H2_ready"], 1)
                if live(0):
                    after(act, s["x_turned"], t + 1)
                    act.activation(xT[:], pX[0:64, 0:256], ACT.Copy).then_inc(s["xT_ready"], 1)
                if live(1):
                    after(act, s["l2_done"], t)
                    after(act, s["out_done"], t - 1)
                    act.activation(H3[:], pC[:, 0:256], ACT.Relu, bias=weff[:, q, 1, HID:HID + 1]).then_inc(s["H3_ready"], 1)
                if live(0):
                    after(act, s["in_done"], t + 1)
                    act.activation(H1[:, par], pA[:, 0:256], ACT.Relu, bias=bi[:]).then_inc(s["H1_ready"], 1)
            each_pair(act, 2, body)

        @block.tensor
        def _(pe):
            pe.wait_ge(loaded, 16 * len(consts))
            pe.wait_ge(zeroed, 2)

            def body(t, par, live):
                q = 1 - par
                if live(1):
                    after(pe, s["H1_ready"], t)
                    after(pe, s["weff_ready"], t)
                    pe.matmul(pB[:, 0:256], weff[:, q, 0, 0:HID], H1[:, q], start=True, stop=True).then_inc(s["l1_done"], 1)
                if live(0):
                    after(pe, s["x_ready"], t + 1)
                    for k in range(2):
                        i = pe.transpose(pX[:, 128 * k:128 * k + 128], x[:, k], ident[:])
                    i.then_inc(s["x_turned"], 1)
                if live(1):
                    after(pe, s["H2_ready"], t)
                    pe.matmul(pC[:, 0:256], weff[:, q, 1, 0:HID], H2[:], start=True, stop=True).then_inc(s["l2_done"], 1)
                if live(0):
                    after(pe, s["xT_ready"], t + 1)
                    pe.matmul(pA[:, 0:256], wi[:], xT[:], start=True, stop=True).then_inc(s["in_done"], 1)
                if live(1):
                    after(pe, s["H3_ready"], t)
                    after(pe, s["fin_ready"], t - 1)
                    for k in range(2):
                        pe.matmul(pO[:, 64 * k:64 * k + 64], H3[:, 128 * k:128 * k + 128], wo[:], start=True, stop=False)
                        i = pe.matmul(pO[:, 64 * k:64 * k + 64], ones[:], bo[:], start=False, stop=True)
                    i.then_inc(s["out_done"], 1)
            each_pair(pe, 2, body)


def _host_constants(i):
    f = {k: np.asarray(v) for k, v in i.items()}
    r = {}
    r["x"] = np.ascontiguousarray(f["x"].reshape(B, T, J * 3))
    r["w1"] = np.ascontiguousarray(f["L0_tok_conv1_w"].transpose(1, 2, 3, 0).reshape(T, 15, T))
    r["w2"] = np.ascontiguousarray(f["L0_tok_conv2_w"].transpose(1, 2, 3, 0).reshape(T, 10, T))
    r["w3"] = np.ascontiguousarray(f["L0_tok_conv3_w"].transpose(1, 2, 3, 0).reshape(T, 10, 2 * T))
    r["conv_bias"] = np.stack([f["L0_tok_conv1_b"], f["L0_tok_conv2_b"], f["L0_tok_conv3_b"][:T], f["L0_tok_conv3_b"][T:]], axis=1)
    r["ln0"] = np.stack([f[k].reshape(J, 3).T for k in ("L0_tok_ln0_g", "L0_tok_ln0_b")])
    r["ln1"] = np.stack([f[k].reshape(J, 2).T for k in ("L0_tok_ln1_g", "L0_tok_ln1_b")])
    r["ln1c"] = np.stack([f["L0_tok_ln1_g"], f["L0_tok_ln1_b"]], axis=1)
    r["out_w"], r["out_b"] = f["L0_tok_out_w"], f["L0_tok_out_b"]
    cw = np.zeros((65, 5, D), np.float32)
    cw[:64] = f["L0_attn_conv_w"].transpose(1, 2, 0)
    cw[64, 4] = f["L0_attn_conv_b"]
    r["a_conv"], r["a_beta"] = cw, f["L0_attn_sqrt_beta"].reshape(D)
    w = np.zeros((65, 576), np.float32)
    for n, k in enumerate("qk"):
        for h in range(H0):
            at = 256 * n + 128 * (h // 4) + 32 * (h % 4)
            w[:64, at:at + DK] = f[f"L0_attn_{k}_w"].T[:, DK * h:DK * h + DK]
            w[64, at:at + DK] = f[f"L0_attn_{k}_b"][DK * h:DK * h + DK]
    w[:64, 512:], w[64, 512:] = f["L0_attn_v_w"].T, f["L0_attn_v_b"]
    r["a_w"] = w
    r["a_lnw"] = np.concatenate([f["L0_attn_ln_w"], np.ones(1, np.float32)])[:, None]
    r["a_lnb"] = np.concatenate([np.zeros((64, 64), np.float32), f["L0_attn_ln_b"][:, None]], axis=1)
    r["a_wo"] = np.concatenate([f["L0_attn_out_w"].T, f["L0_attn_out_b"][None]], axis=0)
    r["a_gam"] = f["L0_attn_gammas"].reshape(H0)
    qh, kk = np.arange(HALF)[:, None], np.arange(T)[None]
    low = np.where(kk[:, :HALF] <= qh, qh - kk[:, :HALF], -1)
    high = np.where(kk <= qh + HALF, qh + HALF - kk, -1)
    both = np.concatenate([np.tile(low, (2, H0)), np.tile(high, (2, H0))], axis=1)
    r["c_pos"] = np.maximum(both, 0).astype(np.float32)
    masked = np.where(both < 0, -1e30, 0.0).astype(np.float32)
    r["c_maskl"], r["c_maskh"] = masked[:, :SL], masked[:, SL:SL + 512]
    cont = np.ones(SA, np.float32)
    cont[HALF - 1:SL:HALF] = 0
    cont[SL + T - 1::T] = 0
    r["c_cont"] = cont
    rowm = np.ones((128, 16), np.float32)
    rowm[0::64, 0:8] = 0
    r["c_rowm"] = rowm
    w1 = np.zeros((128, NEXP // 2, 128), np.float32)
    w2 = np.zeros((128, NEXP // 2, D), np.float32)
    sel = np.zeros((128, NEXP // 2, 128), np.float32)
    for e in range(NEXP):
        w1[:64, e // 2, 64 * (e % 2):64 * (e % 2) + 64] = f["L0_ffn_w1"][e]
        w1[64, e // 2, 64 * (e % 2):64 * (e % 2) + 64] = f["L0_ffn_b1"][e]
        w2[64 * (e % 2):64 * (e % 2) + 64, e // 2] = f["L0_ffn_w2"][e]
        sel[96 + e, e // 2, 64 * (e % 2):64 * (e % 2) + 64] = 1
    r["m_w1"], r["m_w2"], r["c_sel"] = w1, w2, sel
    b2 = np.zeros((128, D), np.float32)
    b2[96:96 + NEXP] = f["L0_ffn_b2"]
    router = np.zeros((128, NEXP), np.float32)
    router[:64] = f["L0_ffn_router_w"].T
    r["m_b2"], r["m_router"] = b2, router
    r["c_iota"] = np.broadcast_to(np.arange(NEXP, dtype=np.float32), (128, 2, NEXP))
    tok = np.zeros((128, 2, 128), np.float32)
    tok[:, :, 64] = 1
    r["c_tok"] = tok
    r["w_qkv"] = np.concatenate([f["L1_attn_W_Q"].T, f["L1_attn_W_K"].T, f["L1_attn_W_V"].T], axis=1)
    r["w_norm"] = np.concatenate([f["L1_attn_wq"].reshape(-1), f["L1_attn_wk"], f["L1_attn_wv"]])
    p = np.arange(128)
    theta = 10000.0 ** (-2.0 * np.arange(ROT // 2) / ROT)
    tq = (p % 64)[:, None] + 64 * np.repeat(np.arange(2), NH1 + 2)[None]
    n = np.arange(NBLK)
    to = (p % QB)[:, None] + (64 * (n // 4) + QB * (n % 2))[None]
    for name, tt in (("q", tq), ("o", to)):
        ang = (tt[:, :, None].astype(np.float32) * theta[None, None].astype(np.float32)).astype(np.float32)
        r["c_cos" + name], r["c_sin" + name] = np.cos(ang).astype(np.float32), np.sin(ang).astype(np.float32)
    key = to[:, :, None] - (p % QB)[:, None, None] - WIN + np.arange(KW)[None, None]
    ok = (key <= to[:, :, None]) & (key >= to[:, :, None] - (WIN - 1)) & (key >= 0)
    r["c_maskw"] = np.where(ok, 0.0, -1e30).reshape(128, NBLK * KW).astype(np.float32)
    wg = np.zeros((C1, NH1, 65), np.float32)
    for h in range(NH1):
        w = f[f"L1_attn_Wg{h // 2}"]
        wg[:, h, :64] = w[:, 64 * (h % 2):64 * (h % 2) + 64]
        if h % 2 == 0:
            wg[:, h, 64] = f[f"L1_attn_bg{h // 2}"]
    r["w_g"] = wg
    r["w_o"] = f["L1_attn_Wout"].T.reshape(2, 64, D).transpose(1, 0, 2)
    bout = np.zeros((65, NH1, D), np.float32)
    bout[64, 0] = f["L1_attn_bout"]
    r["w_bout"] = bout
    wr = np.zeros((NRT + 1, 128, 2, HID + 1), np.float32)
    wr[:NRT, :, :, :HID] = f["L1_ffn_Wr"].transpose(1, 3, 0, 2)
    wr[:NRT, :, :, HID] = f["L1_ffn_br"].transpose(1, 2, 0)
    r["r_wr"] = wr.reshape(NRT + 1, 128, 2 * (HID + 1))
    r["r_ws"] = np.concatenate([f["L1_ffn_Ws"][:, 0].transpose(2, 0, 1), f["L1_ffn_bs"][:, 0].T[:, :, None]], axis=2)
    eye = np.zeros((128, 2, HID + 1), np.float32)
    eye[:, :, :HID] = np.eye(HID)[:, None]
    r["c_eye"] = eye
    r["r_wi"], r["r_bi"] = f["L1_ffn_Wi"].T, f["L1_ffn_bi"][:, None]
    r["r_wo"], r["r_bo"] = f["L1_ffn_Wo"].T, f["L1_ffn_bo"][None]
    r["r_route"] = f["L1_ffn_route_id"][None]
    r["c_ident"] = np.eye(128, dtype=np.float32)
    return {k: np.ascontiguousarray(v) for k, v in r.items()}


def kernel(**inputs):
    import numpy as _np
    import concourse.bacc as _bacc
    from concourse import mybir as _mybir
    from concourse.bass_utils import run_bass_kernel_spmd as _run

    nc = _bacc.Bacc("TRN2", target_bir_lowering=False, num_devices=1)
    host = _host_constants(inputs)
    arrays, args = {}, {}
    for name, v in host.items():
        arrays[f"in_{name}_dram"] = v
        args[name] = nc.dram_tensor(f"in_{name}_dram", v.shape, _mybir.dt.from_np(v.dtype), kind="ExternalInput").ap()
    out = nc.dram_tensor("out_0_dram", (B, T, D), F32, kind="ExternalOutput").ap()
    tower(nc, args, out)
    r = _run(nc, [arrays], core_ids=[0])
    return r.results[0]["out_0_dram"]
```

```python
from contextlib import ExitStack

import concourse.bass as bass
import numpy as np
from concourse import mybir

F32 = mybir.dt.float32
BF16 = mybir.dt.bfloat16
I32 = mybir.dt.int32
ALU = mybir.AluOpType
ACT = mybir.ActivationFunctionType
AX_X = mybir.AxisListType.X

B, T, J, D = 128, 128, 64, 64
PAIRS = B // 2
HALF = T // 2
H0, DK = 8, 8
SL, SH = H0 * HALF, H0 * T
SA = SL + SH
NEXP = 8
NH1, C1, WIN, ROT = 4, 64, 16, 16
QB = 32
NBLK = 2 * T // QB
KW = QB + WIN
HID, NRT = 128, 16
EPS = 1e-5


def after(eng, sem, count):
    if isinstance(count, int) and count <= 0:
        return
    eng.wait_ge(sem, count)


def after_all(eng, carrier, *waits):
    for sem, n in waits:
        after(eng, sem, n)
    if any(not isinstance(n, int) for _, n in waits):
        carrier()


def each_pair(eng, depth, body, unroll=2):
    peel = max(unroll, -(-depth // unroll) * unroll)
    for t in range(peel):
        body(t, t % unroll, lambda d, t=t: 0 <= t - d)
    with eng.Fori(peel, PAIRS - unroll + 1, unroll) as i:
        for k in range(unroll):
            body(i + k if k else i, k, lambda d: True)
    for t in range(PAIRS, PAIRS + depth):
        body(t, t % unroll, lambda d, t=t: t - d < PAIRS)


def last(count):
    return min(count, PAIRS) if isinstance(count, int) else count


def through(t, d):
    return last(t + 1 - d if d < 1 else t - (d - 1) if d > 1 else t)


def tower(nc, a, out):
    ctx = ExitStack()
    with ctx:
        def sb(name, shape, dt=F32, c=ctx):
            return c.enter_context(nc.sbuf_tensor(name, shape, dt))

        stage_sems = []

        def sem(name):
            stage_sems.append(nc.alloc_semaphore(name))
            return stage_sems[-1]

        def end_stage():
            nc.clear_and_free_semaphores(list(stage_sems))
            stage_sems.clear()
            nc.all_engine_barrier()

        psum = ctx.enter_context(nc.psum_tensor("psum", [128, 8, 512], F32))
        h_all = sb("h_all", [128, PAIRS, 2, D])
        ident = sb("ident", [128, 128])
        setup = sem("setup")
        st = Stage(nc, a, out, sb, sem, psum, h_all, ident)
        with nc.Block() as block:
            @block.sync
            def _(sp):
                sp.dma_start(ident[:], a["c_ident"]).then_inc(setup, 16)
                sp.wait_ge(setup, 16)
        with ExitStack() as c:
            token_stage(st, c)
        end_stage()
        with ExitStack() as c:
            distance_attention_stage(st, c)
        end_stage()
        with ExitStack() as c:
            mixture_stage(st, c)
        end_stage()
        with ExitStack() as c:
            window_attention_stage(st, c)
        end_stage()
        with ExitStack() as c:
            routed_stage(st, c)


class Stage:
    def __init__(self, nc, a, out, sb, sem, psum, h_all, ident):
        self.nc, self.a, self.out, self.sb, self.sem = nc, a, out, sb, sem
        self.psum, self.h_all, self.ident = psum, h_all, ident


def token_stage(st, c):
    nc, a, psum, h_all, ident = st.nc, st.a, st.psum, st.h_all, st.ident

    def sb(n, s, dt=F32):
        return st.sb(n, s, dt, c)

    def sem(n):
        return st.sem(n)

    w1 = sb("w1", [128, 15, 128])
    w2 = sb("w2", [128, 10, 128])
    w3 = sb("w3", [128, 10, 256])
    bias = sb("conv_bias", [128, 4])
    ln0 = sb("ln0", [128, 2, 3, J])
    ln1 = sb("ln1", [128, 2, 2, J])
    ln1c = sb("ln1c", [128, 2])
    wout = sb("wout", [128, D])
    woutg = sb("woutg", [128, D])
    beta_rep = sb("beta_rep", [128, 128])
    bias_out = sb("bias_out", [128, D])
    ones = sb("ones_t", [128, 128])
    xin = sb("xin", [128, 2, 2, J * 3])
    cin1 = sb("cin1", [128, 2, 3, 2, J + 4])
    cin2 = sb("cin2", [128, 2, 3, 2, J + 4])
    cin3 = sb("cin3", [128, 2, 2, 2, J + 4])
    y1 = sb("y1", [128, 2, 3, 2, J])
    y2 = sb("y2", [128, 2, 2, 2, J])
    y3 = sb("y3", [128, 2, 2, 2, J])
    s0 = sb("s0", [128, 3, 2, J])
    s1 = sb("s1", [128, 3, 2, J])
    s2 = sb("s2", [128, 2, 2, J])
    resn = sb("resn", [128, 2, 2, 128])
    resT = sb("resT", [128, 2, 256])
    scrap = sb("scrap_t", [128, 1])
    stats = sb("stats_t", [128, 8, 6])
    mv = sb("mv_t", [128, 8, 2])
    lnv = sb("lnv_t", [128, 8])
    rstd = sb("rstd_t", [128, 8])
    p1, p2, p3, pT, pO = (psum[:, k] for k in range(5))
    c1 = p1[:, 0:384].rearrange("p (w g j) -> p w g j", w=3, g=2)
    c2 = p2[:, 0:256].rearrange("p (w g j) -> p w g j", w=2, g=2)
    c3 = p3[:, 0:256].rearrange("p (h g j) -> p h g j", h=2, g=2)

    loaded, zeroed = sem("tok_loaded"), sem("tok_zeroed")
    folded, bias_mm = sem("tok_folded"), sem("tok_bias_mm")
    x_loaded = [sem("x_loaded0"), sem("x_loaded1")]
    stats_done, var_ready, ln_done, rstd_ready = sem("stats_done"), sem("var_ready"), sem("ln_done"), sem("rstd_ready")
    scaled, normed = sem("scaled"), sem("normed")
    conv1_done, conv2_done, conv3_done = sem("conv1_done"), sem("conv2_done"), sem("conv3_done")
    act1, act2, act3 = sem("act1"), sem("act2"), sem("act3")
    res_turned, resT_ready, projected, h_written = sem("res_turned"), sem("resT_ready"), sem("projected"), sem("h_written")
    consts = [(w1[:], a["w1"]), (w2[:], a["w2"]), (w3[:], a["w3"]), (bias[:], a["conv_bias"]),
              (ln0[:], a["ln0"].partition_broadcast(128)), (ln1[:], a["ln1"].partition_broadcast(128)),
              (ln1c[:], a["ln1c"]), (wout[:], a["out_w"]),
              (bias_out[:], a["out_b"].partition_broadcast(128))]

    with nc.Block() as block:
        @block.sync
        def _(sp):
            for dst, src in consts:
                sp.dma_start(dst, src).then_inc(loaded, 16)

            def body(t, par, live):
                if live(0) and not (isinstance(t, int) and t >= PAIRS):
                    after(sp, scaled, t - 1)
                    sp.dma_start(xin[:, par], a["x"][bass.ds(2 * t, 2)].rearrange("g t k -> t g k")).then_inc(x_loaded[par], 16)
            each_pair(sp, 0, body)

        @block.gpsimd
        def _(pool):
            for buf in (cin1, cin2, cin3):
                pool.memset(buf[:], 0.0).then_inc(zeroed, 1)
            pool.memset(mv[:], 1.0).then_inc(zeroed, 1)
            pool.memset(ones[:], 1.0).then_inc(zeroed, 1)

        @block.vector
        def _(dve):
            def carry():
                dve.tensor_copy(scrap[:], ident[:, 0:1])

            dve.wait_ge(loaded, 16 * len(consts))
            dve.wait_ge(zeroed, 5)
            dve.tensor_scalar(woutg[:], wout[:], ln1c[:, 0:1], None, ALU.mult).then_inc(folded, 1)
            dve.tensor_scalar(beta_rep[:], ones[:], ln1c[:, 1:2], None, ALU.mult).then_inc(folded, 1)
            dve.wait_ge(bias_mm, 1)
            dve.tensor_tensor(bias_out[:], pO[:, 0:D], bias_out[:], ALU.add).then_inc(folded, 1)
            dve.wait_ge(folded, 3)

            def body(t, par, live):
                q = 1 - par
                last = None
                if live(0) and not (isinstance(t, int) and t >= PAIRS):
                    after(dve, x_loaded[par], (t // 2 + 1) * 16 if isinstance(t, int) else (t + (2 - par)) * 8)
                    for g in range(2):
                        last = dve.bn_stats(stats[:, g], xin[:, par, g])
                if live(2):
                    after(dve, act1, t - 1)
                    for g in range(2):
                        last = dve.bn_stats(stats[:, 2 + g], y1[:, par, :, g])
                if live(4):
                    after(dve, act2, t - 3)
                    for g in range(2):
                        last = dve.bn_stats(stats[:, 4 + g], y2[:, par, :, g])
                if live(6):
                    after(dve, act3, t - 5)
                    for g in range(2):
                        last = dve.bn_stats(stats[:, 6 + g], y3[:, par, g])
                if last is not None:
                    last.then_inc(stats_done, 1)
                    after_all(dve, carry, (stats_done, t + 1))
                    slots = [k for k in range(4) if live(2 * k) and not (k == 0 and isinstance(t, int) and t >= PAIRS)]
                    for k in slots:
                        for g in (2 * k, 2 * k + 1):
                            last = dve.bn_aggr(mv[:, g], stats[:, g])
                    last.then_inc(var_ready, 1)
                    dve.wait_ge(var_ready, t + 1)
                    last = None
                    for k, (src, dst, gam) in enumerate(((xin[:, par].rearrange("p g (j w) -> p w g j", w=3), s0, ln0),
                                                         (y1[:, par], s1, ln0), (y2[:, par], s2, ln1))):
                        if k in slots:
                            for g in range(2):
                                last = dve.scalar_tensor_tensor(out=dst[:, :, g], in0=src[:, :, g], scalar=mv[:, 2 * k + g, 0:1],
                                                                in1=gam[:, 0], op0=ALU.subtract, op1=ALU.mult)
                    if last is not None:
                        last.then_inc(scaled, 1)
                        dve.wait_ge(scaled, t + 1)
                    dve.wait_ge(rstd_ready, t + 1)
                    if 0 in slots:
                        after(dve, conv1_done, t - 1)
                    if 1 in slots:
                        after(dve, conv2_done, t - 3)
                    if 2 in slots:
                        after(dve, conv3_done, t - 5)
                    for k, (src, dst, gam) in enumerate(((s0, cin1, ln0), (s1, cin2, ln0), (s2, cin3, ln1))):
                        if k in slots:
                            for g in range(2):
                                last = dve.scalar_tensor_tensor(out=dst[:, par, :, g, 2:2 + J], in0=src[:, :, g], scalar=rstd[:, 2 * k + g:2 * k + g + 1],
                                                                in1=gam[:, 1], op0=ALU.mult, op1=ALU.add)
                    if 3 in slots:
                        after(dve, res_turned, t - 7)
                        for g in range(2):
                            last = dve.tensor_scalar(resn[:, par, g], y3[:, par, g].rearrange("p h j -> p (h j)"), mv[:, 6 + g, 0:1], rstd[:, 6 + g:7 + g],
                                                     ALU.subtract, ALU.mult)
                    last.then_inc(normed, 1)
                if live(7):
                    after(dve, projected, t - 6)
                    dve.tensor_tensor(h_all[:, bass.ds(t - 7, 1)].rearrange("p u s d -> p (u s) d"),
                                      pO[:, 0:128].rearrange("p (s d) -> p s d", s=2),
                                      bias_out[:].unsqueeze(1).to_broadcast([128, 2, D]), ALU.add).then_inc(h_written, 1)
            each_pair(dve, 8, body)

        @block.scalar
        def _(act):
            act.preload_act_table_set("natural_log_exp_and_others")
            act.wait_ge(loaded, 16 * len(consts))

            def body(t, par, live):
                q = 1 - par
                if live(6) if isinstance(t, int) and t >= PAIRS else True:
                    act.wait_ge(var_ready, t + 1)
                    act.activation(lnv[:], mv[:, :, 1], ACT.Ln, bias=EPS).then_inc(ln_done, 1)
                    act.wait_ge(ln_done, t + 1)
                    act.activation(rstd[:], lnv[:], ACT.Exp, scale=-0.5).then_inc(rstd_ready, 1)
                if live(1):
                    after(act, conv1_done, t)
                    after(act, normed, t - 0)
                    act.activation(y1[:, q], c1, ACT.Relu, bias=bias[:, 0:1]).then_inc(act1, 1)
                if live(3):
                    after(act, conv2_done, t - 2)
                    act.activation(y2[:, q], c2, ACT.Relu, bias=bias[:, 1:2]).then_inc(act2, 1)
                if live(7):
                    after(act, res_turned, t - 6)
                    after(act, projected, t - 8)
                    act.activation(resT[:, q].rearrange("p (s g t) -> p g s t", s=2, g=2),
                                   pT[:, 0:256].rearrange("p (g s t) -> p g s t", g=2, s=2), ACT.Copy).then_inc(resT_ready, 1)
                if live(5):
                    after(act, conv3_done, t - 4)
                    act.activation(y3[:, q, :, 0], c3[:, 0], ACT.Relu, bias=bias[:, 2:3])
                    act.activation(y3[:, q, :, 1], c3[:, 1], ACT.Relu, bias=bias[:, 3:4]).then_inc(act3, 1)
            each_pair(act, 8, body)

        @block.tensor
        def _(pe):
            pe.wait_ge(loaded, 16 * len(consts))
            pe.wait_ge(folded, 2)
            pe.matmul(pO[:, 0:D], beta_rep[:], wout[:], start=True, stop=True).then_inc(bias_mm, 1)
            pe.wait_ge(folded, 3)
            taps1 = [(kh, kw) for kw in (1, 0, 2) for kh in range(5)]
            taps2 = [(kh, kw) for kw in range(2) for kh in range(5)]

            def body(t, par, live):
                q = 1 - par
                if live(1):
                    pe.wait_ge(normed, t)
                    after(pe, act1, t - 1)
                    for n, (kh, kw) in enumerate(taps1):
                        lo, hi = max(0, 1 - kw), min(3, 4 - kw)
                        mm = pe.matmul(c1[:, lo:hi], w1[:, kh * 3 + kw], cin1[:, q, lo + kw - 1:hi + kw - 1, :, kh:kh + J],
                                       start=n == 0, stop=n == len(taps1) - 1)
                    mm.then_inc(conv1_done, 1)
                if live(3):
                    pe.wait_ge(normed, t)
                    after(pe, act2, t - 3)
                    for n, (kh, kw) in enumerate(taps2):
                        mm = pe.matmul(c2, w2[:, kh * 2 + kw], cin2[:, q, kw:kw + 2, :, kh:kh + J], start=n == 0, stop=n == len(taps2) - 1)
                    mm.then_inc(conv2_done, 1)
                if live(7):
                    pe.wait_ge(normed, t)
                    after(pe, resT_ready, t - 7)
                    for g in range(2):
                        mm = pe.transpose(pT[:, g * 128:(g + 1) * 128], resn[:, q, g], ident[:])
                    mm.then_inc(res_turned, 1)
                if live(5):
                    pe.wait_ge(normed, t)
                    after(pe, act3, t - 5)
                    for m in range(2):
                        for n, (kh, kw) in enumerate(taps2):
                            mm = pe.matmul(c3[:, m], w3[:, kh * 2 + kw, m * 128:(m + 1) * 128], cin3[:, q, kw, :, kh:kh + J],
                                           start=n == 0, stop=n == len(taps2) - 1)
                    mm.then_inc(conv3_done, 1)
                if live(7):
                    after(pe, resT_ready, t - 6)
                    after(pe, h_written, t - 7)
                    for s in range(2):
                        mm = pe.matmul(pO[:, s * D:(s + 1) * D], resT[:, q, s * 128:(s + 1) * 128], woutg[:], start=True, stop=True)
                    mm.then_inc(projected, 1)
            each_pair(pe, 8, body)


def distance_attention_stage(st, c):
    nc, a, psum, h_all, ident = st.nc, st.a, st.psum, st.h_all, st.ident

    def sb(n, s, dt=F32):
        return st.sb("at_" + n, s, dt, c)

    def sem(n):
        return st.sem("at_" + n)

    convw = sb("convw", [65, 5, D])
    beta, bsq, omb, opb = sb("beta", [65, D]), sb("bsq", [65, D]), sb("omb", [65, D]), sb("opb", [65, D])
    diag = sb("diag", [64, D])
    wraw, waug = sb("wraw", [65, 576]), sb("waug", [65, 576])
    lnw, lnb_sel = sb("lnw", [65, 1]), sb("lnb_sel", [64, 65])
    wo = sb("wo", [65, D])
    gam, gtmp, gsq = sb("gam", [128, H0]), sb("gtmp", [128, H0]), sb("gsq", [128, H0])
    posg = sb("posg", [128, SA])
    cont = sb("cont", [128, SA])
    maskl, maskh = sb("maskl", [128, SL], BF16), sb("maskh", [128, 512], BF16)
    identb = sb("identb", [128, 128], BF16)
    rowm = sb("rowm", [128, 16])
    hcur = sb("hcur", [128, 2, D])
    xh = sb("xh", [128, 2, 128])
    xT = sb("xT", [65, 2, 4 + T])
    hidn = sb("hidn", [128, 2, 128])
    hT = sb("hT", [65, 2, T])
    QT = sb("QT", [128, 2, 2 * T])
    KT = sb("KT", [128, 2, 4, 2 * T])
    V9 = sb("V9", [128, 4, 2, H0, DK + 1])
    VL = sb("VL", [128, 4, H0 // 2, 2, 2 * (DK + 1)])
    P = sb("P", [128, SA])
    E = sb("E", [128, 2, SA])
    R = sb("R", [128, SA + 1])
    mx = sb("mx", [128, 2, 16])
    rT = sb("rT", [128, 16])
    PTL, PTH = sb("PTL", [128, H0 // 2, 128]), sb("PTH", [128, H0, 128])
    rs = sb("rs", [128, 16])
    att = sb("att", [128, 2, 128])
    aT = sb("aT", [65, 2, 128])
    scrap = sb("scrap", [128, 1])
    stats, mv, lnv, rstd = sb("stats", [128, 4, 6]), sb("mv", [128, 4, 2]), sb("lnv", [128, 4]), sb("rstd", [128, 4])

    S2 = [psum[:, 3 * p:3 * p + 3].rearrange("p b n -> p (b n)") for p in range(2)]
    X, Y = psum[:, 6], psum[:, 7]
    O = Y[:, 0:288].rearrange("p (n g e) -> p n g e", g=2, e=DK + 1)

    loaded, zeroed, g_step, fold, fold_mm = (sem(n) for n in ("loaded", "zeroed", "g_step", "fold", "fold_mm"))
    names = """h_copied stats1 var1 ln1 rstd1 x_ready x_turned xT_ready conv_done stats2 var2 ln2 rstd2 hid_ready
               hid_turned hT_ready q_done q_ready k_done k_ready v_done v_ready s_done max1 x1_ready e1_ready
               scan_done recip1 dist1 d_ready ln_d exp_d eff_ready s2_done max2 x2_ready p_ready pt_turned pt_ready pv_done
               recip2 rs_ready att_ready a_turned aT_ready out_done h_written""".split()
    s = {n: sem(n) for n in names}
    consts = [(convw[:], a["a_conv"]), (beta[:], a["a_beta"].partition_broadcast(65)), (wraw[:], a["a_w"]), (lnw[:], a["a_lnw"]),
              (lnb_sel[:], a["a_lnb"]), (wo[:], a["a_wo"]), (gam[:], a["a_gam"].partition_broadcast(128)), (posg[:], a["c_pos"]),
              (cont[:], a["c_cont"].partition_broadcast(128)), (E[:, 0, 0:512], a["c_maskl"]), (E[:, 0, 512:1024], a["c_maskh"]),
              (rowm[:], a["c_rowm"])]

    def parts(ap):
        return (ap[:, 0:SL].rearrange("p (h k) -> p h k", h=H0), ap[:, SL:SA].rearrange("p (h k) -> p h k", h=H0))

    def spread(col, k):
        return col.unsqueeze(2).to_broadcast([128, H0, k])

    with nc.Block() as block:
        @block.sync
        def _(sp):
            for dst, src in consts:
                sp.dma_start(dst, src).then_inc(loaded, 16)

        @block.gpsimd
        def _(pool):
            pool.memset(xT[:], 0.0).then_inc(zeroed, 1)
            pool.wait_ge(zeroed, 1)
            for k, (buf, v) in enumerate(((xT[64:65], 1.0), (hT[64:65], 1.0), (aT[64:65], 1.0), (KT[:], 0.0), (V9[:], 1.0), (VL[:], 0.0),
                                          (R[:, SA:SA + 1], 0.0), (mv[:], 1.0), (xh[:], 0.0), (hidn[:], 0.0), (att[:], 0.0),
                                          (VL[0:64].rearrange("p r h s e -> p (r h) s e")[:, :, 0], 1.0),
                                          (VL[64:128].rearrange("p r h s e -> p (r h) s e")[:, :, 1], 1.0))):
                pool.memset(buf, v).then_inc(zeroed, 1)
                pool.wait_ge(zeroed, k + 2)

        @block.vector
        def _(dve):
            def carry():
                dve.tensor_copy(scrap[:], ident[:, 0:1])

            dve.wait_ge(loaded, 16 * len(consts))
            dve.wait_ge(zeroed, 14)
            n = [0]

            def link(ins):
                n[0] += 1
                ins.then_inc(fold, 1)
                dve.wait_ge(fold, n[0])
            link(dve.tensor_copy(maskl[:], E[:, 0, 0:512]))
            link(dve.tensor_copy(maskh[:], E[:, 0, 512:1024]))
            link(dve.tensor_copy(identb[:], ident[:]))
            link(dve.tensor_tensor(bsq[:], beta[:], beta[:], ALU.mult))
            link(dve.tensor_scalar(omb[:], bsq[:], -1.0, 1.0, ALU.mult, ALU.add))
            link(dve.tensor_scalar(opb[:], bsq[:], 1.0, None, ALU.add))
            link(dve.tensor_tensor(convw[:], convw[:], omb[:].unsqueeze(1).to_broadcast([65, 5, D]), ALU.mult))
            link(dve.tensor_tensor(diag[:], ident[0:64, 0:64], opb[0:64], ALU.mult))
            link(dve.tensor_tensor(convw[0:64, 4], convw[0:64, 4], diag[:], ALU.add))
            dve.wait_ge(fold_mm, 1)
            link(dve.scalar_tensor_tensor(out=waug[:, 0:512], in0=wraw[:, 0:512], scalar=lnw[:, 0:1], in1=X[0:65, 0:512],
                                          op0=ALU.mult, op1=ALU.add))
            link(dve.scalar_tensor_tensor(out=waug[:, 512:576], in0=wraw[:, 512:576], scalar=lnw[:, 0:1], in1=Y[0:65, 0:64],
                                          op0=ALU.mult, op1=ALU.add))
            link(dve.tensor_scalar(waug[:, 0:256], waug[:, 0:256], float(DK) ** -0.5, None, ALU.mult))
            dve.wait_ge(g_step, 3)
            link(dve.scalar_tensor_tensor(out=gsq[:], in0=gam[:], scalar=0.0, in1=gtmp[:], op0=ALU.max, op1=ALU.add))
            link(dve.tensor_tensor(gsq[:], gsq[:], gsq[:], ALU.mult))
            for ap, k in zip(parts(posg[:]), (HALF, T)):
                link(dve.tensor_tensor(ap, ap, spread(gsq[:], k), ALU.mult))

            def body(t, par, live):
                p0, p1 = par % 2, 1 - par % 2
                def to(d):
                    return through(t, d)

                if live(0):
                    dve.tensor_copy(hcur[:], h_all[:, bass.ds(t, 1)].rearrange("p u s d -> p (u s) d")).then_inc(s["h_copied"], 1)
                    after(dve, s["h_copied"], to(0))
                    for k in range(2):
                        i = dve.bn_stats(stats[:, k], hcur[:, k])
                    i.then_inc(s["stats1"], 1)
                    after_all(dve, carry, (s["stats1"], to(0)))
                    for k in range(2):
                        i = dve.bn_aggr(mv[:, k], stats[:, k])
                    i.then_inc(s["var1"], 1)
                    after(dve, s["rstd1"], to(0))
                    for k in range(2):
                        i = dve.tensor_scalar(xh[:, k, 0:D], hcur[:, k], mv[:, k, 0:1], rstd[:, k:k + 1], ALU.subtract, ALU.mult)
                    i.then_inc(s["x_ready"], 1)
                if live(2):
                    after(dve, s["s_done"], to(2))
                    for k, ap in enumerate(parts(S2[p0])):
                        i = dve.tensor_reduce(mx[:, 0, 8 * k:8 * k + 8], ap, AX_X, ALU.max)
                    i.then_inc(s["max1"], 1)
                    after(dve, s["max1"], to(2))
                    after(dve, s["p_ready"], to(4))
                    for k, (ap, e, n) in enumerate(zip(parts(S2[p0]), parts(E[:, p0]), (HALF, T))):
                        i = dve.tensor_tensor(e, ap, spread(mx[:, 0, 8 * k:8 * k + 8], n), ALU.subtract)
                    i.then_inc(s["x1_ready"], 1)
                if live(3):
                    after(dve, s["eff_ready"], to(3))
                    dve.scalar_tensor_tensor(out=E[:, p1], in0=E[:, p1], scalar=1e-5, in1=S2[p1], op0=ALU.max, op1=ALU.mult).then_inc(s["s2_done"], 1)
                if live(5):
                    after(dve, s["pv_done"], to(5))
                    for g in range(2):
                        r = slice(64 * g, 64 * g + 64)
                        i = dve.reciprocal(rs[r], O[r, :, g, DK])
                    i.then_inc(s["recip2"], 1)
                    after(dve, s["recip2"], to(5))
                    dve.tensor_tensor(rs[:], rs[:], rowm[:], ALU.mult).then_inc(s["rs_ready"], 1)
                    after(dve, s["rs_ready"], to(5))
                    for g in range(2):
                        r = slice(64 * g, 64 * g + 64)
                        i = dve.tensor_tensor(att[r, :, 0:D].rearrange("p s (h e) -> p s h e", h=H0), O[r, :, g, 0:DK].rearrange("p (s h) e -> p s h e", s=2),
                                              rs[r].rearrange("p (s h) -> p s h", s=2).unsqueeze(3).to_broadcast([64, 2, H0, DK]), ALU.mult)
                    i.then_inc(s["att_ready"], 1)
                if live(3):
                    after(dve, s["s2_done"], to(3))
                    for k, e in enumerate(parts(E[:, p1])):
                        i = dve.tensor_reduce(mx[:, 1, 8 * k:8 * k + 8], e, AX_X, ALU.max)
                    i.then_inc(s["max2"], 1)
                if live(0):
                    after(dve, s["conv_done"], to(0))
                    for k in range(2):
                        i = dve.bn_stats(stats[:, 2 + k], X[:, 64 * k:64 * k + 64])
                    i.then_inc(s["stats2"], 1)
                    after_all(dve, carry, (s["stats2"], to(0)))
                    for k in range(2):
                        i = dve.bn_aggr(mv[:, 2 + k], stats[:, 2 + k])
                    i.then_inc(s["var2"], 1)
                if live(3):
                    after(dve, s["max2"], to(3))
                    for k, (e, n) in enumerate(zip(parts(E[:, p1]), (HALF, T))):
                        i = dve.tensor_tensor(e, e, spread(mx[:, 1, 8 * k:8 * k + 8], n), ALU.subtract)
                    i.then_inc(s["x2_ready"], 1)
                if live(0):
                    after(dve, s["rstd2"], to(0))
                    for k in range(2):
                        i = dve.tensor_scalar(hidn[:, k, 0:D], X[:, 64 * k:64 * k + 64], mv[:, 2 + k, 0:1], rstd[:, 2 + k:3 + k], ALU.subtract, ALU.mult)
                    i.then_inc(s["hid_ready"], 1)
                if live(2):
                    after(dve, s["e1_ready"], to(2))
                    dve.tensor_tensor_scan(R[:, 0:SA][:, ::-1], cont[:, ::-1], E[:, p0, ::-1], 0.0, ALU.mult, ALU.add).then_inc(s["scan_done"], 1)
                if live(2):
                    after(dve, s["scan_done"], to(2))
                    for k, ap in enumerate(parts(R)):
                        i = dve.reciprocal(rT[:, 8 * k:8 * k + 8], ap[:, :, 0])
                    i.then_inc(s["recip1"], 1)
                    dve.tensor_tensor(E[:, p0], R[:, 1:SA + 1], posg[:], ALU.mult).then_inc(s["dist1"], 1)
                    after(dve, s["recip1"], to(2))
                    after(dve, s["dist1"], to(2))
                    for k, (e, n) in enumerate(zip(parts(E[:, p0]), (HALF, T))):
                        i = dve.scalar_tensor_tensor(out=e, in0=e, scalar=1e-16, in1=spread(rT[:, 8 * k:8 * k + 8], n), op0=ALU.max, op1=ALU.mult)
                    i.then_inc(s["d_ready"], 1)
                if live(5):
                    after(dve, s["out_done"], to(5))
                    hv = h_all[:, bass.ds(t - 5, 1)].rearrange("p u s d -> p (u s) d")
                    dve.tensor_tensor(hv, X[:, 0:128].rearrange("p (s d) -> p s d", s=2), hv, ALU.add).then_inc(s["h_written"], 1)
            each_pair(dve, 5, body, 4)

        @block.scalar
        def _(act):
            act.preload_act_table_set("natural_log_exp_and_others")
            act.wait_ge(loaded, 16 * len(consts))
            act.wait_ge(zeroed, 14)
            act.activation(gtmp[:], gam[:], ACT.Abs).then_inc(g_step, 1)
            act.wait_ge(g_step, 1)
            act.activation(gtmp[:], gtmp[:], ACT.Exp, scale=-1.0).then_inc(g_step, 1)
            act.wait_ge(g_step, 2)
            act.activation(gtmp[:], gtmp[:], ACT.Ln, bias=1.0).then_inc(g_step, 1)

            def turned(t, r):
                after(act, s["pt_turned"], (t - 4) * 3 + r + 1)
                if r == 0:
                    after(act, s["pv_done"], t - 4)
                    act.activation(PTL[:].rearrange("p h n -> p (h n)"), Y, ACT.Copy).then_inc(s["pt_ready"], 1)
                else:
                    act.activation(PTH[:, 4 * r - 4:4 * r].rearrange("p h n -> p (h n)"), Y, ACT.Copy).then_inc(s["pt_ready"], 1)

            def body(t, par, live):
                p0, p1 = par % 2, 1 - par % 2
                def to(d):
                    return through(t, d)

                if live(3):
                    after(act, s["d_ready"], to(3))
                    act.activation(E[:, p1], E[:, p1], ACT.Ln).then_inc(s["ln_d"], 1)
                if live(0):
                    after(act, s["var1"], to(0))
                    act.activation(lnv[:, 0:2], mv[:, 0:2, 1], ACT.Ln, bias=EPS).then_inc(s["ln1"], 1)
                if live(0):
                    after(act, s["ln1"], to(0))
                    act.activation(rstd[:, 0:2], lnv[:, 0:2], ACT.Exp, scale=-0.5).then_inc(s["rstd1"], 1)
                if live(3):
                    after(act, s["ln_d"], to(3))
                    act.activation(E[:, p1], E[:, p1], ACT.Exp, scale=0.5).then_inc(s["exp_d"], 1)
                if live(3):
                    after(act, s["exp_d"], to(3))
                    act.activation(E[:, p1], E[:, p1], ACT.Exp, scale=-1.0).then_inc(s["eff_ready"], 1)
                if live(1):
                    after(act, s["hid_turned"], to(1))
                    act.activation(hT[0:64].rearrange("p g (s t) -> p s g t", s=2),
                                   X[0:64, 0:256].rearrange("p (s g t) -> p s g t", s=2, g=2), ACT.Copy).then_inc(s["hT_ready"], 1)
                if live(0):
                    after(act, s["x_turned"], to(0))
                    act.activation(xT[0:64, :, 4:4 + T].rearrange("p g (s t) -> p s g t", s=2),
                                   X[0:64, 0:256].rearrange("p (s g t) -> p s g t", s=2, g=2), ACT.Copy).then_inc(s["xT_ready"], 1)
                if live(2):
                    after(act, s["x1_ready"], to(2))
                    act.activation(E[:, p0], E[:, p0], ACT.Exp).then_inc(s["e1_ready"], 1)
                if live(4):
                    turned(t, 0)
                if live(0):
                    after(act, s["var2"], to(0))
                    act.activation(lnv[:, 2:4], mv[:, 2:4, 1], ACT.Ln, bias=1e-12).then_inc(s["ln2"], 1)
                    after(act, s["ln2"], to(0))
                    act.activation(rstd[:, 2:4], lnv[:, 2:4], ACT.Exp, scale=-0.5).then_inc(s["rstd2"], 1)
                if live(4):
                    turned(t, 1)
                if live(4):
                    turned(t, 2)
                if live(5):
                    after(act, s["a_turned"], to(5))
                    act.activation(aT[0:64].rearrange("p s n -> p (s n)"), X[0:64, 0:256], ACT.Copy).then_inc(s["aT_ready"], 1)
                if live(1):
                    after(act, s["k_done"], to(1))
                    after(act, s["s_done"], to(2))
                    for i in range(4):
                        r = slice(32 * i, 32 * i + 32)
                        ins = act.activation(KT[r, :, i], S2[p1][r, 512:1024].rearrange("p (s n) -> p s n", s=2), ACT.Copy)
                    ins.then_inc(s["k_ready"], 1)
                    after(act, s["v_done"], to(1))
                    after(act, s["pv_done"], to(5))
                    act.activation(V9[:, (par - 1) % 4, :, :, 0:DK], S2[p1][:, 1024:1152].rearrange("p (g h e) -> p g h e", g=2, h=H0), ACT.Copy)
                    for u in range(2):
                        r = slice(64 * u, 64 * u + 64)
                        ins = act.activation(VL[r, (par - 1) % 4, :, u].rearrange("p h (g e) -> p g h e", g=2)[:, :, :, 0:DK],
                                             S2[p1][r, 1024 + 128 * u:1152 + 128 * u].rearrange("p (g h e) -> p g h e", g=2, h=H0)[:, :, u::2], ACT.Copy)
                    ins.then_inc(s["v_ready"], 1)
                if live(1):
                    after(act, s["q_done"], to(1))
                    after(act, s["s_done"], to(2))
                    act.activation(QT[:].rearrange("p s n -> p (s n)"), Y, ACT.Copy).then_inc(s["q_ready"], 1)
                if live(3):
                    after(act, s["x2_ready"], to(3))
                    after(act, s["pt_turned"], (t - 3) * 3)
                    act.activation(P[:], E[:, p1], ACT.Exp).then_inc(s["p_ready"], 1)
            each_pair(act, 5, body, 4)

        @block.tensor
        def _(pe):
            pe.wait_ge(loaded, 16 * len(consts))
            pe.wait_ge(zeroed, 14)
            pe.matmul(X[0:65, 0:512], lnb_sel[:], wraw[0:64, 0:512], start=True, stop=True)
            pe.matmul(Y[0:65, 0:64], lnb_sel[:], wraw[0:64, 512:576], start=True, stop=True).then_inc(fold_mm, 1)
            pe.wait_ge(fold, 16)

            def turn(t, r):
                if r == 0:
                    after(pe, s["p_ready"], t - 3)
                    after(pe, s["q_ready"], last(t - 1))
                    after(pe, s["att_ready"], t - 4)
                else:
                    after(pe, s["pt_ready"], (t - 4) * 3 + r)
                for n in range(4):
                    i = pe.transpose(Y[:, 128 * n:128 * n + 128], P[:, 512 * r + 128 * n:512 * r + 128 * n + 128], ident[:])
                i.then_inc(s["pt_turned"], 1)

            def body(t, par, live):
                p0, p1 = par % 2, 1 - par % 2
                def to(d):
                    return through(t, d)

                if live(1):
                    after(pe, s["hid_ready"], to(1))
                    after(pe, s["h_written"], to(6))
                    for k in range(2):
                        i = pe.transpose(X[:, 128 * k:128 * k + 128], hidn[:, k], ident[:])
                    i.then_inc(s["hid_turned"], 1)
                if live(5):
                    after(pe, s["pt_ready"], 3 * to(5))
                    after(pe, s["q_ready"], to(2))
                    v = V9[:, (par - 1) % 4]
                    for h in range(0, H0, 2):
                        pe.matmul(O[:, h:h + 2].rearrange("p h g e -> p (h g e)"), PTL[:, h // 2], VL[:, (par - 1) % 4, h // 2].rearrange("p s e -> p (s e)"), start=True, stop=True)
                    for h in range(H0):
                        i = pe.matmul(O[:, H0 + h].rearrange("p g e -> p (g e)"), PTH[:, h], v[:, :, h], start=True, stop=True)
                    i.then_inc(s["pv_done"], 1)
                if live(0):
                    after(pe, s["x_ready"], to(0))
                    after(pe, s["hT_ready"], to(1))
                    for k in range(2):
                        i = pe.transpose(X[:, 128 * k:128 * k + 128], xh[:, k], ident[:])
                    i.then_inc(s["x_turned"], 1)
                if live(0):
                    after(pe, s["xT_ready"], to(0))
                    for k in range(2):
                        for g in range(2):
                            for tap in range(5):
                                i = pe.matmul(X[64 * g:64 * g + 64, 64 * k:64 * k + 64], xT[:, g, HALF * k + tap:HALF * k + tap + HALF],
                                              convw[:, tap], start=tap == 0, stop=tap == 4)
                    i.then_inc(s["conv_done"], 1)
                if live(4):
                    turn(t, 0)
                if live(1):
                    after(pe, s["hT_ready"], to(1))
                    after(pe, s["s2_done"], to(3))
                    hTf = hT[:].rearrange("p g n -> p (g n)")
                    for k in range(2):
                        i = pe.matmul(S2[p1][:, 512 + 256 * k:768 + 256 * k], waug[:, 256 + 128 * k:384 + 128 * k], hTf, start=True, stop=True)
                    i.then_inc(s["k_done"], 1)
                if live(4):
                    turn(t, 1)
                if live(1):
                    for g in range(2):
                        i = pe.matmul(S2[p1][:, 1024 + 64 * g:1088 + 64 * g], hT[:, g], waug[:, 512:576], start=True, stop=True)
                    for g in range(2):
                        i = pe.matmul(S2[p1][64:128, 1152 + 64 * g:1216 + 64 * g], hT[:, g, 0:HALF], waug[:, 512:576], start=True, stop=True)
                    i.then_inc(s["v_done"], 1)
                if live(4):
                    turn(t, 2)
                if live(5):
                    after(pe, s["hid_ready"], to(0))
                    after(pe, s["att_ready"], to(5))
                    after(pe, s["h_written"], to(6))
                    for k in range(2):
                        i = pe.transpose(X[:, 128 * k:128 * k + 128], att[:, k], ident[:])
                    i.then_inc(s["a_turned"], 1)
                if live(1):
                    after(pe, s["pt_ready"], 3 * to(4))
                    after(pe, s["q_ready"], to(2))
                    for k in range(2):
                        i = pe.matmul(Y[:, 256 * k:256 * k + 256], waug[:, 128 * k:128 * k + 128], hTf, start=True, stop=True)
                    i.then_inc(s["q_done"], 1)
                if live(5):
                    after(pe, s["aT_ready"], to(5))
                    for k in range(2):
                        i = pe.matmul(X[:, 64 * k:64 * k + 64], aT[:, k], wo[:], start=True, stop=True)
                    i.then_inc(s["out_done"], 1)
                if live(1):
                    after(pe, s["q_ready"], to(1))
                    after(pe, s["v_ready"], to(1))
                    after(pe, s["s2_done"], to(3))
                    S = S2[p1]
                    pe.matmul(S[:, 0:512], identb[:], maskl[:], start=True, stop=False, skip_group_check=True)
                    for b in (1, 2):
                        pe.matmul(S[:, 512 * b:512 * b + 512], identb[:], maskh[:], start=True, stop=False, skip_group_check=True)
                    for h in range(H0):
                        for k, base, n in ((0, HALF * h, HALF), (1, SL + T * h, T)):
                            for g in range(2):
                                i = pe.matmul(S[64 * g:64 * g + 64, base:base + n], QT[:, h // 4, T * g + HALF * k:T * g + HALF * k + HALF],
                                              KT[:, h // 4, h % 4, T * g:T * g + n], start=False, stop=True, skip_group_check=True)
                    i.then_inc(s["s_done"], 1)
            each_pair(pe, 5, body, 4)


def mixture_stage(st, c):
    nc, a, psum, h_all, ident = st.nc, st.a, st.psum, st.h_all, st.ident

    def sb(n, s, dt=F32):
        return st.sb("moe_" + n, s, dt, c)

    def sem(n):
        return st.sem("moe_" + n)

    NP = NEXP // 2
    w1, sel, w2 = sb("w1", [128, NP, 128]), sb("sel", [128, NP, 128]), sb("w2", [128, NP, D])
    b2, router, iota = sb("b2", [128, D]), sb("router", [128, NEXP]), sb("iota", [128, 2, NEXP])
    hcur, hnew = sb("hcur", [128, 2, D]), sb("hnew", [128, 2, D])
    tok = sb("tok", [128, 4, 2, 128])
    tokT, xT = sb("tokT", [128, 2, 2 * T]), sb("xT", [128, 2 * T])
    lg, m8, i8, fi = sb("lg", [128, 2, NEXP]), sb("m8", [128, 2, 8]), sb("i8", [128, 2, 8], mybir.dt.uint32), sb("fi", [128, 2, 8])
    d12, e12, w12 = sb("d12", [128, 2]), sb("e12", [128, 2]), sb("w12", [128, 2, 2])
    den = sb("den", [128, 2])
    eq = sb("eq", [128, 2, 2, NEXP])
    cw, rest = sb("cw", [128, 2, NEXP]), sb("rest", [128, 2, 2, NEXP])
    part, selb = sb("part", [128, 3, 2, NEXP], BF16), sb("selb", [128, NP, 128], BF16)
    tokb = sb("tokb", [128, 2 * T], BF16)
    G = sb("G", [128, 2, NP, 2 * T])
    stats, mv, lnv, rstd = sb("stats", [128, 2, 6]), sb("mv", [128, 2, 2]), sb("lnv", [128, 2]), sb("rstd", [128, 2])
    scrap = sb("scrap", [128, 4])
    column = [0]
    pX, pW, pH, pC, pY = psum[:, 0], psum[:, 1], psum[:, 2:4], psum[:, 4:6], psum[:, 6]

    names = """h_copied stats1 var1 ln1 rstd1 t_ready t_turned xT_ready logits lg_ready max_done idx_done fi_done d_done e_done
               lg_ready2 den_done w1_done w2_done eq_done c_done cw_ready part1 rest1 part2 rest2 part3 tokb_ready w_turned tokT_ready up_done gelu_done cb_done g_ready down_done h_written x_added""".split()
    s = {n: sem(n) for n in names}
    loaded, selected = sem("loaded"), sem("selected")
    consts = [(w1[:], a["m_w1"]), (sel[:], a["c_sel"]), (w2[:], a["m_w2"]), (b2[:], a["m_b2"]), (router[:], a["m_router"]), (iota[:], a["c_iota"]), *[(tok[:, r], a["c_tok"]) for r in range(4)]]

    with nc.Block() as block:
        @block.sync
        def _(sp):
            for dst, src in consts:
                sp.dma_start(dst, src).then_inc(loaded, 16)

        @block.vector
        def _(dve):
            def carry():
                column[0] = (column[0] + 1) % 4
                dve.tensor_copy(scrap[:, column[0]:column[0] + 1], ident[:, 0:1])

            dve.wait_ge(loaded, 16 * len(consts))
            dve.tensor_copy(selb[:], sel[:]).then_inc(selected, 1)

            def body(t, par, live):
                def to(d):
                    return through(t, d)

                x = tok[:, par]
                if live(0):
                    after(dve, s["t_ready"], to(1))
                    after(dve, s["x_added"], to(1))
                    dve.tensor_copy(hcur[:], h_all[:, bass.ds(t, 1)].rearrange("p u s d -> p (u s) d")).then_inc(s["h_copied"], 1)
                if live(3):
                    after(dve, s["gelu_done"], to(3))
                    after(dve, s["cb_done"], to(3))
                    for k in range(2):
                        g = G[:, (par - 3) % 2, 2 * k:2 * k + 2].rearrange("p e n -> p (e n)")
                        i = dve.tensor_tensor(g, g, pC[:, k], ALU.mult)
                    i.then_inc(s["g_ready"], 1)
                if live(0):
                    after(dve, s["h_copied"], to(0))
                    for k in range(2):
                        i = dve.bn_stats(stats[:, k], hcur[:, k])
                    i.then_inc(s["stats1"], 1)
                if live(1):
                    after(dve, s["logits"], to(1))
                    dve.tensor_copy(lg[:].rearrange("p k e -> p (k e)"), pX[:, 0:16]).then_inc(s["lg_ready"], 1)
                if live(0):
                    after_all(dve, carry, (s["stats1"], to(0)))
                    for k in range(2):
                        i = dve.bn_aggr(mv[:, k], stats[:, k])
                    i.then_inc(s["var1"], 1)
                if live(1):
                    after_all(dve, carry, (s["lg_ready"], to(1)))
                    for k in range(2):
                        i = dve.max(m8[:, k], lg[:, k])
                    i.then_inc(s["max_done"], 1)
                    after_all(dve, carry, (s["max_done"], to(1)))
                    dve.tensor_tensor(d12[:], m8[:, :, 1], m8[:, :, 0], ALU.subtract).then_inc(s["d_done"], 1)
                    for k in range(2):
                        i = dve.max_index(i8[:, k], m8[:, k], lg[:, k])
                    i.then_inc(s["idx_done"], 1)
                if live(0):
                    after(dve, s["rstd1"], to(0))
                    for k in range(2):
                        i = dve.tensor_scalar(x[:, k, 0:D], hcur[:, k], mv[:, k, 0:1], rstd[:, k:k + 1], ALU.subtract, ALU.mult)
                    i.then_inc(s["t_ready"], 1)
                if live(1):
                    after(dve, s["idx_done"], to(1))
                    dve.tensor_copy(fi[:], i8[:]).then_inc(s["fi_done"], 1)
                    after(dve, s["e_done"], to(1))
                    dve.tensor_scalar(den[:], e12[:], 1.0, None, ALU.add).then_inc(s["den_done"], 1)
                    after(dve, s["fi_done"], to(1))
                    for n in range(2):
                        i = dve.tensor_tensor(eq[:, n], iota[:], fi[:, :, n:n + 1].to_broadcast([128, 2, NEXP]), ALU.is_equal)
                    i.then_inc(s["eq_done"], 1)
                    after(dve, s["den_done"], to(1))
                    dve.reciprocal(w12[:, 0], den[:]).then_inc(s["w1_done"], 1)
                if live(0):
                    after(dve, s["t_ready"], to(0))
                    dve.tensor_tensor(h_all[:, bass.ds(t, 1)].rearrange("p u s d -> p (u s) d"), hcur[:], x[:, :, 0:D], ALU.add)\
                       .then_inc(s["x_added"], 1)
                if live(1):
                    after(dve, s["w1_done"], to(1))
                    dve.tensor_tensor(w12[:, 1], w12[:, 0], e12[:], ALU.mult).then_inc(s["w2_done"], 1)
                    after(dve, s["w2_done"], to(1))
                    after(dve, s["eq_done"], to(1))
                    for n in range(2):
                        i = dve.tensor_tensor(eq[:, n], eq[:, n], w12[:, n].unsqueeze(2).to_broadcast([128, 2, NEXP]), ALU.mult)
                    i.then_inc(s["c_done"], 1)
                if live(1):
                    after(dve, s["c_done"], to(1))
                    dve.tensor_tensor(cw[:], eq[:, 0], eq[:, 1], ALU.add).then_inc(s["cw_ready"], 1)
                    after(dve, s["cw_ready"], to(1))
                    dve.tensor_copy(part[:, 0], cw[:]).then_inc(s["part1"], 1)
                    after(dve, s["part1"], to(1))
                    dve.tensor_tensor(rest[:, 0], cw[:], part[:, 0], ALU.subtract).then_inc(s["rest1"], 1)
                    after(dve, s["rest1"], to(1))
                    dve.tensor_copy(part[:, 1], rest[:, 0]).then_inc(s["part2"], 1)
                    after(dve, s["part2"], to(1))
                    dve.tensor_tensor(rest[:, 1], rest[:, 0], part[:, 1], ALU.subtract).then_inc(s["rest2"], 1)
                    after(dve, s["rest2"], to(1))
                    dve.tensor_copy(part[:, 2], rest[:, 1]).then_inc(s["part3"], 1)
                    after(dve, s["part3"], to(1))
                    for n in range(3):
                        i = dve.tensor_copy(tok[:, (par - 1) % 4, :, 96 + NEXP * n:96 + NEXP * n + NEXP], part[:, n])
                    i.then_inc(s["lg_ready2"], 1)
                if live(3):
                    after(dve, s["down_done"], to(3))
                    hv = h_all[:, bass.ds(t - 3, 1)].rearrange("p u s d -> p (u s) d")
                    dve.tensor_tensor(hv, pY[:, 0:128].rearrange("p (s d) -> p s d", s=2), hv, ALU.add).then_inc(s["h_written"], 1)
            each_pair(dve, 3, body, 4)

        @block.scalar
        def _(act):
            act.wait_ge(loaded, 16 * len(consts))

            def body(t, par, live):
                def to(d):
                    return through(t, d)

                if live(2):
                    after(act, s["w_turned"], to(2))
                    act.activation(tokT[:, par % 2], pW[:, 0:256], ACT.Copy).then_inc(s["tokT_ready"], 1)
                    after(act, s["cb_done"], to(3))
                    act.activation(tokb[:], pW[:, 0:256], ACT.Copy).then_inc(s["tokb_ready"], 1)
                if live(0) or live(1):
                    act.preload_act_table_set("natural_log_exp_and_others")
                if live(0):
                    after(act, s["var1"], to(0))
                    act.activation(lnv[:], mv[:, :, 1], ACT.Ln, bias=EPS).then_inc(s["ln1"], 1)
                    after(act, s["ln1"], to(0))
                    act.activation(rstd[:], lnv[:], ACT.Exp, scale=-0.5).then_inc(s["rstd1"], 1)
                if live(1):
                    after(act, s["d_done"], to(1))
                    act.activation(e12[:], d12[:], ACT.Exp).then_inc(s["e_done"], 1)
                if live(0):
                    after(act, s["t_turned"], to(0))
                    act.activation(xT[:], pX[:, 0:256], ACT.Copy).then_inc(s["xT_ready"], 1)
                if live(2):
                    after(act, s["up_done"], to(2))
                    after(act, s["down_done"], to(4))
                    for k in range(2):
                        i = act.activation(G[:, par % 2, 2 * k:2 * k + 2].rearrange("p e n -> p (e n)"), pH[:, k], ACT.Gelu)
                    i.then_inc(s["gelu_done"], 1)
            each_pair(act, 3, body, 4)

        @block.tensor
        def _(pe):
            pe.wait_ge(loaded, 16 * len(consts))
            pe.wait_ge(selected, 1)

            def body(t, par, live):
                def to(d):
                    return through(t, d)

                if live(2):
                    after(pe, s["lg_ready2"], to(2))
                    after(pe, s["tokb_ready"], to(3))
                    for k in range(2):
                        i = pe.transpose(pW[:, 128 * k:128 * k + 128], tok[:, (par - 2) % 4, k], ident[:])
                    i.then_inc(s["w_turned"], 1)
                if live(2):
                    after(pe, s["tokT_ready"], to(2))
                    after(pe, s["gelu_done"], to(3))
                    for e in range(NP):
                        i = pe.matmul(pH[:, e // 2, 256 * (e % 2):256 * (e % 2) + 256], w1[:, e], tokT[:, par % 2], start=True, stop=True)
                    i.then_inc(s["up_done"], 1)
                if live(0):
                    after(pe, s["t_ready"], to(0))
                    after(pe, s["lg_ready"], to(1))
                    for k in range(2):
                        i = pe.transpose(pX[:, 128 * k:128 * k + 128], tok[:, par, k], ident[:])
                    i.then_inc(s["t_turned"], 1)
                if live(3):
                    after(pe, s["g_ready"], to(3))
                    after(pe, s["h_written"], to(4))
                    for k in range(2):
                        n = slice(128 * k, 128 * k + 128)
                        pe.matmul(pY[:, 64 * k:64 * k + 64], tokT[:, (par - 3) % 2, n], b2[:], start=True, stop=False)
                        for e in range(NP):
                            i = pe.matmul(pY[:, 64 * k:64 * k + 64], G[:, (par - 3) % 2, e, n], w2[:, e], start=False, stop=e == NP - 1)
                    i.then_inc(s["down_done"], 1)
                if live(2):
                    after(pe, s["tokb_ready"], to(2))
                    after(pe, s["g_ready"], to(3))
                    for e in range(NP):
                        i = pe.matmul(pC[:, e // 2, 256 * (e % 2):256 * (e % 2) + 256], selb[:, e], tokb[:], start=True, stop=True)
                    i.then_inc(s["cb_done"], 1)
                if live(0):
                    after(pe, s["xT_ready"], to(0))
                    for k in range(2):
                        i = pe.matmul(pX[:, 8 * k:8 * k + 8], xT[:, 128 * k:128 * k + 128], router[:], start=True, stop=True)
                    i.then_inc(s["logits"], 1)
            each_pair(pe, 3, body, 4)


def window_attention_stage(st, c):
    nc, a, psum, h_all, ident = st.nc, st.a, st.psum, st.h_all, st.ident

    def sb(n, s, dt=F32):
        return st.sb("wa_" + n, s, dt, c)

    def sem(n):
        return st.sem("wa_" + n)

    NG = NH1 + 2
    W = NG * C1
    PIECES = [(0, 0, 16, 0, 32), (1, 0, 0, 16, 48), (2, 0, 0, 48, 16), (2, 1, 16, 0, 32), (3, 1, 0, 16, 48)]
    wqkv, wn = sb("wqkv", [D, W]), sb("wn", [128, W])
    cosq, sinq = sb("cosq", [128, 2 * NG, 8]), sb("sinq", [128, 2 * NG, 8])
    coso, sino = sb("coso", [128, NBLK, 8]), sb("sino", [128, NBLK, 8])
    mask, identb = sb("mask", [128, NBLK * KW], BF16), sb("identb", [128, 128], BF16)
    wg, wo4 = sb("wg", [C1, NH1, 65]), sb("wo4", [64, 2, D])
    mrow, mw = sb("mrow", [65, NH1, D]), sb("mw", [65, NH1, D])
    hcur, x, xT = sb("hcur", [128, 2, D]), sb("x", [128, 2, 128]), sb("xT", [D, 2 * T])
    sq, ms, lnms, rn = sb("sq", [128, 2, W]), sb("ms", [128, 2 * NG]), sb("lnms", [128, 2 * NG]), sb("rn", [128, 2 * NG])
    qkv = sb("qkv", [128, 4, 2, W + 1])
    rt = [sb(f"rt{i}", [128, 2 * NG, 8]) for i in range(4)]
    ro = [sb(f"ro{i}", [128, NBLK, 8]) for i in range(4)]
    QT, KT = sb("QT", [C1, NBLK, NH1, QB]), sb("KT", [C1, 2, WIN + T])
    mx, P0 = sb("mx", [128, NBLK]), sb("P0", [128, NBLK, KW])
    PZ, PT = sb("PZ", [128, len(PIECES), 2, 192]), sb("PT", [128, len(PIECES) * 2, 128])
    rs, os = sb("rs", [128, NBLK]), sb("os", [128, NBLK * C1 + 64])
    OT = sb("OT", [65, 2, NH1, 128])
    stats, mv, lnv, rstd = sb("stats", [128, 2, 6]), sb("mv", [128, 2, 2]), sb("lnv", [128, 2]), sb("rstd", [128, 2])
    scrap = sb("scrap", [128, 1])
    p0, pQ, p3, pP, pO = psum[:, 0], psum[:, 1:3], psum[:, 3], psum[:, 4:6], psum[:, 6:8]
    osb = os[:, 0:NBLK * C1].rearrange("p (n c) -> p n c", n=NBLK)

    names = """h_copied stats1 var1 ln1 rstd1 x_ready x_turned xT_ready qkv_done raw_ready sq_done ms_done lnms_done rn_done n_done w_done
               r_done rope_ready q_turned k_turned q_ready k_ready s_done max_done p0_ready pz_ready p_turned p_ready pv_done
               rs_done os_done ro_done os_ready o_turned OT_ready out_done h_written""".split()
    s = {n: sem(n) for n in names}
    loaded, zeroed, fold, fold_mm = sem("loaded"), sem("zeroed"), sem("fold"), sem("fold_mm")
    consts = [(wqkv[:], a["w_qkv"]), (wn[:], a["w_norm"].partition_broadcast(128)), (cosq[:], a["c_cosq"]), (sinq[:], a["c_sinq"]),
              (coso[:], a["c_coso"]), (sino[:], a["c_sino"]), (sq[:, 0], a["c_maskw"]),
              (wg[:], a["w_g"]), (wo4[:], a["w_o"]), (mrow[:], a["w_bout"])]

    with nc.Block() as block:
        @block.sync
        def _(sp):
            for dst, src in consts:
                sp.dma_start(dst, src).then_inc(loaded, 16)

        @block.gpsimd
        def _(pool):
            for k, (buf, v) in enumerate(((x[:], 0.0), (qkv[:, :, :, W:W + 1], 1.0), (KT[:], 0.0), (PZ[:], 0.0), (os[:], 0.0), (OT[64:65], 1.0))):
                pool.memset(buf, v).then_inc(zeroed, 1)
                pool.wait_ge(zeroed, k + 1)

        @block.vector
        def _(dve):
            def carry():
                dve.tensor_copy(scrap[:], ident[:, 0:1])

            dve.wait_ge(loaded, 16 * len(consts))
            dve.wait_ge(zeroed, 6)
            dve.tensor_copy(mask[:], sq[:, 0]).then_inc(fold, 1)
            dve.tensor_copy(identb[:], ident[:]).then_inc(fold, 1)
            dve.wait_ge(fold_mm, 1)
            dve.tensor_tensor(mw[:], p0[0:65, 0:256].rearrange("p (h d) -> p h d", h=NH1), mrow[:], ALU.add).then_inc(fold, 1)

            def products(v, cos, sin, tmp):
                x1, x2 = v[:, :, C1 - ROT:C1:2], v[:, :, C1 - ROT + 1:C1:2]
                for o, (u, m) in zip(tmp, ((x1, cos), (x2, sin), (x1, sin), (x2, cos))):
                    i = dve.tensor_tensor(o, u, m, ALU.mult)
                return i

            def body(t, par, live):
                def to(d):
                    return through(t, d)

                v = qkv[:, (par - 1) % 4]
                if live(0):
                    after(dve, s["x_ready"], to(1))
                    dve.tensor_copy(hcur[:], h_all[:, bass.ds(t, 1)].rearrange("p u s d -> p (u s) d")).then_inc(s["h_copied"], 1)
                if live(5):
                    after(dve, s["pv_done"], to(5))
                    for k in range(2):
                        i = dve.reciprocal(rs[:, 4 * k:4 * k + 4], pO[:, k, 0:260].rearrange("p (n e) -> p n e", e=65)[:, :, 64])
                    i.then_inc(s["rs_done"], 1)
                if live(0):
                    after(dve, s["h_copied"], to(0))
                    for k in range(2):
                        i = dve.bn_stats(stats[:, k], hcur[:, k])
                    i.then_inc(s["stats1"], 1)
                if live(5):
                    after(dve, s["rs_done"], to(5))
                    after(dve, s["o_turned"], to(6))
                    for k in range(2):
                        i = dve.tensor_tensor(osb[:, 4 * k:4 * k + 4], pO[:, k, 0:260].rearrange("p (n e) -> p n e", e=65)[:, :, 0:64],
                                              rs[:, 4 * k:4 * k + 4].unsqueeze(2).to_broadcast([128, 4, C1]), ALU.mult)
                    i.then_inc(s["os_done"], 1)
                if live(0):
                    after_all(dve, carry, (s["stats1"], to(0)))
                    for k in range(2):
                        i = dve.bn_aggr(mv[:, k], stats[:, k])
                    i.then_inc(s["var1"], 1)
                if live(1):
                    after(dve, s["sq_done"], to(1))
                    dve.tensor_reduce(ms[:], sq[:].rearrange("p k (g c) -> p (k g) c", c=C1), AX_X, ALU.add).then_inc(s["ms_done"], 1)
                if live(5):
                    after(dve, s["os_done"], to(5))
                    products(osb, coso[:], sino[:], [o[:] for o in ro]).then_inc(s["ro_done"], 1)
                if live(0):
                    after(dve, s["rstd1"], to(0))
                    after(dve, s["x_turned"], to(1))
                    for k in range(2):
                        i = dve.tensor_scalar(x[:, k, 0:D], hcur[:, k], mv[:, k, 0:1], rstd[:, k:k + 1], ALU.subtract, ALU.mult)
                    i.then_inc(s["x_ready"], 1)
                if live(5):
                    after(dve, s["ro_done"], to(5))
                    dve.tensor_tensor(osb[:, :, C1 - ROT:C1:2], ro[0][:], ro[1][:], ALU.add)
                    dve.tensor_tensor(osb[:, :, C1 - ROT + 1:C1:2], ro[3][:], ro[2][:], ALU.subtract).then_inc(s["os_ready"], 1)
                if live(3):
                    after(dve, s["s_done"], to(3))
                    sc = p3[:, 0:NBLK * KW].rearrange("p (n k) -> p n k", n=NBLK)
                    dve.tensor_reduce(mx[:], sc, AX_X, ALU.max).then_inc(s["max_done"], 1)
                if live(1):
                    after(dve, s["rn_done"], to(1))
                    for k in range(2):
                        vk = v[:, k, 0:W].rearrange("p (g c) -> p g c", g=NG)
                        i = dve.tensor_tensor(vk, vk, rn[:, NG * k:NG * k + NG].unsqueeze(2).to_broadcast([128, NG, C1]), ALU.mult)
                    i.then_inc(s["n_done"], 1)
                if live(3):
                    after(dve, s["max_done"], to(3))
                    after(dve, s["pz_ready"], to(4))
                    dve.tensor_tensor(P0[:], sc, mx[:].unsqueeze(2).to_broadcast([128, NBLK, KW]), ALU.subtract).then_inc(s["p0_ready"], 1)
                if live(1):
                    after(dve, s["n_done"], to(1))
                    for k in range(2):
                        i = dve.tensor_tensor(v[:, k, 0:W], v[:, k, 0:W], wn[:], ALU.mult)
                    i.then_inc(s["w_done"], 1)
                    after(dve, s["w_done"], to(1))
                    for k in range(2):
                        g = slice(NG * k, NG * k + NG)
                        i = products(v[:, k, 0:W].rearrange("p (g c) -> p g c", g=NG), cosq[:, g], sinq[:, g], [o[:, g] for o in rt])
                    i.then_inc(s["r_done"], 1)
                if live(6):
                    after(dve, s["out_done"], to(6))
                    hv = h_all[:, bass.ds(t - 6, 1)].rearrange("p u s d -> p (u s) d")
                    dve.tensor_tensor(hv, p0[:, 0:128].rearrange("p (s d) -> p s d", s=2), hv, ALU.add).then_inc(s["h_written"], 1)
                if live(1):
                    after(dve, s["r_done"], to(1))
                    for k in range(2):
                        g = slice(NG * k, NG * k + NG)
                        vk = v[:, k, 0:W].rearrange("p (g c) -> p g c", g=NG)
                        dve.tensor_tensor(vk[:, :, C1 - ROT:C1:2], rt[0][:, g], rt[1][:, g], ALU.subtract)
                        i = dve.tensor_tensor(vk[:, :, C1 - ROT + 1:C1:2], rt[2][:, g], rt[3][:, g], ALU.add)
                    i.then_inc(s["rope_ready"], 1)
            each_pair(dve, 6, body, 4)

        @block.scalar
        def _(act):
            act.preload_act_table_set("natural_log_exp_and_others")
            act.wait_ge(loaded, 16 * len(consts))
            act.wait_ge(zeroed, 6)
            act.wait_ge(fold, 2)

            def body(t, par, live):
                def to(d):
                    return through(t, d)

                if live(1):
                    after(act, s["raw_ready"], to(1))
                    after(act, s["ms_done"], to(2))
                    act.activation(sq[:], qkv[:, (par - 1) % 4, :, 0:W], ACT.Square).then_inc(s["sq_done"], 1)
                if live(0):
                    after(act, s["var1"], to(0))
                    act.activation(lnv[:], mv[:, :, 1], ACT.Ln, bias=EPS).then_inc(s["ln1"], 1)
                    after(act, s["ln1"], to(0))
                    act.activation(rstd[:], lnv[:], ACT.Exp, scale=-0.5).then_inc(s["rstd1"], 1)
                if live(6):
                    after(act, s["o_turned"], to(6))
                    after(act, s["out_done"], to(7))
                    for k in range(2):
                        i = act.activation(OT[0:64, k].rearrange("p h (n q) -> p n h q", n=4), pP[0:64, k].rearrange("p (n h q) -> p n h q", n=4, h=NH1), ACT.Copy)
                    i.then_inc(s["OT_ready"], 1)
                if live(1):
                    after(act, s["ms_done"], to(1))
                    act.activation(lnms[:], ms[:], ACT.Ln, bias=1e-8, scale=1.0 / C1).then_inc(s["lnms_done"], 1)
                if live(1):
                    after(act, s["lnms_done"], to(1))
                    act.activation(rn[:], lnms[:], ACT.Exp, scale=-0.5).then_inc(s["rn_done"], 1)
                if live(2):
                    after(act, s["q_turned"], to(2))
                    after(act, s["s_done"], to(3))
                    for k in range(2):
                        i = act.activation(QT[:, 4 * k:4 * k + 4].rearrange("p n h q -> p h n q"), pQ[0:64, k].rearrange("p (h n q) -> p h n q", h=NH1, n=4), ACT.Copy)
                    i.then_inc(s["q_ready"], 1)
                if live(0):
                    after(act, s["x_turned"], to(0))
                    act.activation(xT[:], p0[0:64, 0:256], ACT.Copy).then_inc(s["xT_ready"], 1)
                if live(2):
                    after(act, s["k_turned"], to(2))
                    act.activation(KT[:, :, WIN:].rearrange("p g (k t) -> p k g t", k=2), p0[0:64, 0:256].rearrange("p (k g t) -> p k g t", k=2, g=2), ACT.Copy)\
                       .then_inc(s["k_ready"], 1)
                if live(4):
                    for r in range(3):
                        after(act, s["p_turned"], (t - 4) * 3 + r + 1)
                        n = 4 if r < 2 else 2
                        act.activation(PT[:, 4 * r:4 * r + n].rearrange("p m n -> p (m n)"), pP[:, r % 2, 0:128 * n], ACT.Copy).then_inc(s["p_ready"], 1)
                if live(3):
                    after(act, s["p0_ready"], to(3))
                    after(act, s["p_turned"], (t - 3) * 3)
                    for n, (kind, _, w0, k0, w) in enumerate(PIECES):
                        b = 4 * (kind // 2) + kind % 2
                        i = act.activation(PZ[:, n, :, k0:k0 + w], P0[:, b:b + 3:2, w0:w0 + w], ACT.Exp, scale=C1 ** -0.5)
                    i.then_inc(s["pz_ready"], 1)
                if live(0):
                    after(act, s["qkv_done"], to(0))
                    after(act, s["pv_done"], to(4))
                    act.activation(qkv[:, par, :, 0:W], pQ[:, :, 0:W], ACT.Copy).then_inc(s["raw_ready"], 1)
            each_pair(act, 6, body, 4)

        @block.tensor
        def _(pe):
            pe.wait_ge(loaded, 16 * len(consts))
            pe.wait_ge(zeroed, 6)
            for h in range(NH1):
                i = pe.matmul(p0[0:65, 64 * h:64 * h + 64], wg[:, h], wo4[:, h // 2], start=True, stop=True)
            i.then_inc(fold_mm, 1)
            pe.wait_ge(fold, 3)

            def turn(t, rounds):
                for r in rounds:
                    for m in range(4 * r, min(4 * r + 4, 10)):
                        i = pe.transpose(pP[:, r % 2, 128 * (m % 4):128 * (m % 4) + 128], PZ[:, m // 2].rearrange("p g n -> p (g n)")[:, 128 * (m % 2):128 * (m % 2) + 128], ident[:])
                    i.then_inc(s["p_turned"], 1)

            def body(t, par, live):
                def to(d):
                    return through(t, d)

                if live(6):
                    after(pe, s["os_ready"], to(6))
                    after(pe, s["p_ready"], 3 * to(5))
                    for n in range(NBLK):
                        i = pe.transpose(pP[:, n // 4, 128 * (n % 4):128 * (n % 4) + 128], os[:, C1 * n:C1 * n + 128], ident[:])
                    i.then_inc(s["o_turned"], 1)
                if live(3):
                    after(pe, s["k_ready"], to(3))
                    after(pe, s["p0_ready"], to(4))
                    pe.matmul(p3[:, 0:NBLK * KW], identb[:], mask[:], start=True, stop=False, skip_group_check=True)
                    for n in range(NBLK):
                        k, g, b = n // 4, n // 2 % 2, n % 2
                        i = pe.matmul(p3[:, KW * n:KW * n + KW], QT[:, n].rearrange("p h q -> p (h q)"), KT[:, g, 64 * k + 32 * b:64 * k + 32 * b + KW],
                                      start=False, stop=True, skip_group_check=True)
                    i.then_inc(s["s_done"], 1)
                if live(2):
                    after(pe, s["rope_ready"], to(2))
                    after(pe, s["raw_ready"], to(1))
                    for k in range(2):
                        for h in range(NH1):
                            i = pe.transpose(pQ[:, k, 128 * h:128 * h + 128], qkv[:, (par - 2) % 4, k, 64 * h:64 * h + 128], ident[:])
                    i.then_inc(s["q_turned"], 1)
                if live(4):
                    after(pe, s["pz_ready"], to(4))
                    after(pe, s["OT_ready"], to(6))
                    turn(t, (0, 1))
                if live(0):
                    after(pe, s["x_ready"], to(0))
                    after(pe, s["h_written"], to(7))
                    for k in range(2):
                        i = pe.transpose(p0[:, 128 * k:128 * k + 128], x[:, k], ident[:])
                    i.then_inc(s["x_turned"], 1)
                if live(2):
                    after(pe, s["xT_ready"], to(0))
                    for k in range(2):
                        i = pe.transpose(p0[:, 128 * k:128 * k + 128], qkv[:, (par - 2) % 4, k, 256:384], ident[:])
                    i.then_inc(s["k_turned"], 1)
                if live(0):
                    after(pe, s["xT_ready"], to(0))
                    after(pe, s["q_ready"], to(2))
                    for k in range(2):
                        i = pe.matmul(pQ[:, k, 0:W], xT[:, 128 * k:128 * k + 128], wqkv[:], start=True, stop=True)
                    i.then_inc(s["qkv_done"], 1)
                if live(4):
                    after(pe, s["p_ready"], (t - 4) * 3 + 1)
                    turn(t, (2,))
                if live(6):
                    after(pe, s["OT_ready"], to(6))
                    after(pe, s["k_ready"], to(2))
                    after(pe, s["h_written"], to(7))
                    for k in range(2):
                        for h in range(NH1):
                            i = pe.matmul(p0[:, 64 * k:64 * k + 64], OT[:, k, h], mw[:, h], start=h == 0, stop=h == NH1 - 1)
                    i.then_inc(s["out_done"], 1)
                if live(4):
                    after(pe, s["p_ready"], (t - 4) * 3 + 3)
                    after(pe, s["os_done"], to(5))
                    for n in range(NBLK):
                        kind, g = 2 * (n // 4) + n % 2, n // 2 % 2
                        mine = [(m, p[1]) for m, p in enumerate(PIECES) if p[0] == kind]
                        for j, (m, k) in enumerate(mine):
                            i = pe.matmul(pO[:, n // 4, 65 * (n % 4):65 * (n % 4) + 65], PT[:, 2 * m + g], qkv[:, par, k, 320:385],
                                          start=j == 0, stop=j == len(mine) - 1)
                    i.then_inc(s["pv_done"], 1)
            each_pair(pe, 6, body, 4)


def routed_stage(st, c):
    nc, a, psum, h_all, ident, out = st.nc, st.a, st.psum, st.h_all, st.ident, st.out

    def sb(n, s, dt=F32):
        return st.sb("rf_" + n, s, dt, c)

    def sem(n):
        return st.sem("rf_" + n)

    wi, ws, wo = sb("wi", [D, HID]), sb("ws", [128, 2, HID + 1]), sb("wo", [HID, D])
    bi, bo, ones = sb("bi", [HID, 1]), sb("bo", [1, D]), sb("ones", [1, 128])
    eye = sb("eye", [128, 2, HID + 1])
    ri, rf, rv, rw, rx = sb("ri", [1, PAIRS], I32), sb("rf", [1, PAIRS]), sb("rv", [1, PAIRS]), sb("rw", [1, PAIRS]), sb("rx", [1, PAIRS], I32)
    wsel, weff = sb("wsel", [128, 2, 2, HID + 1]), sb("weff", [128, 2, 2, HID + 1])
    hcur, x, xT = sb("hcur", [128, 2, D]), sb("x", [128, 2, 128]), sb("xT", [D, 2 * T])
    H1, H2, H3 = sb("H1", [HID, 2, 2 * T]), sb("H2", [HID, 2 * T]), sb("H3", [HID, 2 * T])
    fin = sb("fin", [128, 2, 2, D])
    stats, mv, lnv, rstd = sb("stats", [128, 2, 6]), sb("mv", [128, 2, 2]), sb("lnv", [128, 2]), sb("rstd", [128, 2])
    scrap = sb("scrap", [128, 1])
    pX, pA, pB, pC, pO = (psum[:, k] for k in range(5))

    names = """h_copied stats1 var1 ln1 rstd1 x_ready x_turned xT_ready in_done H1_ready l1_done H2_ready l2_done H3_ready
               out_done fin_ready weff_ready""".split()
    s = {n: sem(n) for n in names}
    loaded, zeroed, fold = sem("loaded"), sem("zeroed"), sem("fold")
    w_loaded, stored = [sem("w_loaded0"), sem("w_loaded1")], [sem("stored0"), sem("stored1")]
    consts = [(wi[:], a["r_wi"]), (ws[:], a["r_ws"]), (wo[:], a["r_wo"]), (bi[:], a["r_bi"]), (bo[:], a["r_bo"]), (eye[:], a["c_eye"]), (ri[:], a["r_route"])]

    def count16(t, par):
        return (t // 2 + 1) * 16 if isinstance(t, int) else (t + (2 - par)) * 8

    with nc.Block() as block:
        @block.sync
        def _(sp):
            for dst, src in consts:
                sp.dma_start(dst, src).then_inc(loaded, 16)
            sp.wait_ge(fold, 6)

            def body(t, par, live):
                q = 1 - par
                if live(0):
                    after(sp, s["weff_ready"], t - 1)
                    n = sp.value_load(rx[0:1, bass.ds(t, 1)], min_val=0, max_val=NRT)
                    sp.dma_start(wsel[:, par].rearrange("p l n -> p (l n)"), a["r_wr"][bass.ds(n, 1)].rearrange("e p n -> (e p) n")).then_inc(w_loaded[par], 16)
            each_pair(sp, 0, body)

        @block.gpsimd
        def _(pool):
            for k, (buf, v) in enumerate(((x[:], 0.0), (ones[:], 1.0))):
                pool.memset(buf, v).then_inc(zeroed, 1)
                pool.wait_ge(zeroed, k + 1)
            pool.wait_ge(fold, 7)

            def body(t, par, live):
                after(pool, s["fin_ready"], t + 1)
                for g in range(2):
                    pool.dma_start(out[bass.ds(2 * t + g, 1)].rearrange("b (s t) d -> t (b s) d", s=2), fin[64 * g:64 * g + 64, par]).then_inc(stored[par], 16)
            each_pair(pool, 0, body)
            for k in range(2):
                pool.wait_ge(stored[k], 32 * PAIRS // 2)

        @block.vector
        def _(dve):
            def carry():
                dve.tensor_copy(scrap[:], ident[:, 0:1])

            dve.wait_ge(loaded, 16 * len(consts))
            dve.wait_ge(zeroed, 2)
            n = [0]

            def link(ins):
                n[0] += 1
                ins.then_inc(fold, 1)
                dve.wait_ge(fold, n[0])
            link(dve.tensor_copy(rf[:], ri[:]))
            link(dve.tensor_scalar(rv[:], rf[:], 0.0, None, ALU.is_ge))
            link(dve.tensor_scalar(rw[:], rf[:], float(NRT - 1), None, ALU.is_le))
            link(dve.tensor_tensor(rv[:], rv[:], rw[:], ALU.mult))
            link(dve.scalar_tensor_tensor(out=rf[:], in0=rf[:], scalar=float(-NRT), in1=rv[:], op0=ALU.add, op1=ALU.mult))
            link(dve.tensor_scalar(rx[:], rf[:], float(NRT), None, ALU.add))
            link(dve.tensor_tensor(ws[:], ws[:], eye[:], ALU.add))

            def body(t, par, live):
                q = 1 - par
                if live(0):
                    after(dve, w_loaded[par], count16(t, par))
                    after(dve, s["H3_ready"], t - 1)
                    dve.tensor_tensor(weff[:, par], wsel[:, par], ws[:], ALU.add).then_inc(s["weff_ready"], 1)
                    after(dve, s["x_ready"], t)
                    dve.tensor_copy(hcur[:], h_all[:, bass.ds(t, 1)].rearrange("p u s d -> p (u s) d")).then_inc(s["h_copied"], 1)
                    after(dve, s["h_copied"], t + 1)
                    for k in range(2):
                        i = dve.bn_stats(stats[:, k], hcur[:, k])
                    i.then_inc(s["stats1"], 1)
                    after_all(dve, carry, (s["stats1"], t + 1))
                    for k in range(2):
                        i = dve.bn_aggr(mv[:, k], stats[:, k])
                    i.then_inc(s["var1"], 1)
                    after(dve, s["rstd1"], t + 1)
                    after(dve, s["x_turned"], t)
                    for k in range(2):
                        i = dve.tensor_scalar(x[:, k, 0:D], hcur[:, k], mv[:, k, 0:1], rstd[:, k:k + 1], ALU.subtract, ALU.mult)
                    i.then_inc(s["x_ready"], 1)
                if live(2):
                    after(dve, s["out_done"], t - 1)
                    if not isinstance(t, int) or t >= 4:
                        after(dve, stored[par], count16(t - 4, par) * 2)
                    dve.tensor_tensor(fin[:, par], pO[:, 0:128].rearrange("p (s d) -> p s d", s=2),
                                      h_all[:, bass.ds(t - 2, 1)].rearrange("p u s d -> p (u s) d"), ALU.add).then_inc(s["fin_ready"], 1)
            each_pair(dve, 2, body)

        @block.scalar
        def _(act):
            act.preload_act_table_set("natural_log_exp_and_others")
            act.wait_ge(loaded, 16 * len(consts))

            def body(t, par, live):
                q = 1 - par
                if live(0):
                    after(act, s["var1"], t + 1)
                    act.activation(lnv[:], mv[:, :, 1], ACT.Ln, bias=EPS).then_inc(s["ln1"], 1)
                    after(act, s["ln1"], t + 1)
                    act.activation(rstd[:], lnv[:], ACT.Exp, scale=-0.5).then_inc(s["rstd1"], 1)
                if live(1):
                    after(act, s["l1_done"], t)
                    act.activation(H2[:], pB[:, 0:256], ACT.Relu, bias=weff[:, q, 0, HID:HID + 1]).then_inc(s["H2_ready"], 1)
                if live(0):
                    after(act, s["x_turned"], t + 1)
                    act.activation(xT[:], pX[0:64, 0:256], ACT.Copy).then_inc(s["xT_ready"], 1)
                if live(1):
                    after(act, s["l2_done"], t)
                    after(act, s["out_done"], t - 1)
                    act.activation(H3[:], pC[:, 0:256], ACT.Relu, bias=weff[:, q, 1, HID:HID + 1]).then_inc(s["H3_ready"], 1)
                if live(0):
                    after(act, s["in_done"], t + 1)
                    act.activation(H1[:, par], pA[:, 0:256], ACT.Relu, bias=bi[:]).then_inc(s["H1_ready"], 1)
            each_pair(act, 2, body)

        @block.tensor
        def _(pe):
            pe.wait_ge(loaded, 16 * len(consts))
            pe.wait_ge(zeroed, 2)

            def body(t, par, live):
                q = 1 - par
                if live(1):
                    after(pe, s["H1_ready"], t)
                    after(pe, s["weff_ready"], t)
                    pe.matmul(pB[:, 0:256], weff[:, q, 0, 0:HID], H1[:, q], start=True, stop=True).then_inc(s["l1_done"], 1)
                if live(0):
                    after(pe, s["x_ready"], t + 1)
                    for k in range(2):
                        i = pe.transpose(pX[:, 128 * k:128 * k + 128], x[:, k], ident[:])
                    i.then_inc(s["x_turned"], 1)
                if live(1):
                    after(pe, s["H2_ready"], t)
                    pe.matmul(pC[:, 0:256], weff[:, q, 1, 0:HID], H2[:], start=True, stop=True).then_inc(s["l2_done"], 1)
                if live(0):
                    after(pe, s["xT_ready"], t + 1)
                    pe.matmul(pA[:, 0:256], wi[:], xT[:], start=True, stop=True).then_inc(s["in_done"], 1)
                if live(1):
                    after(pe, s["H3_ready"], t)
                    after(pe, s["fin_ready"], t - 1)
                    for k in range(2):
                        pe.matmul(pO[:, 64 * k:64 * k + 64], H3[:, 128 * k:128 * k + 128], wo[:], start=True, stop=False)
                        i = pe.matmul(pO[:, 64 * k:64 * k + 64], ones[:], bo[:], start=False, stop=True)
                    i.then_inc(s["out_done"], 1)
            each_pair(pe, 2, body)


def _host_constants(i):
    f = {k: np.asarray(v) for k, v in i.items()}
    r = {}
    r["x"] = np.ascontiguousarray(f["x"].reshape(B, T, J * 3))
    r["w1"] = np.ascontiguousarray(f["L0_tok_conv1_w"].transpose(1, 2, 3, 0).reshape(T, 15, T))
    r["w2"] = np.ascontiguousarray(f["L0_tok_conv2_w"].transpose(1, 2, 3, 0).reshape(T, 10, T))
    r["w3"] = np.ascontiguousarray(f["L0_tok_conv3_w"].transpose(1, 2, 3, 0).reshape(T, 10, 2 * T))
    r["conv_bias"] = np.stack([f["L0_tok_conv1_b"], f["L0_tok_conv2_b"], f["L0_tok_conv3_b"][:T], f["L0_tok_conv3_b"][T:]], axis=1)
    r["ln0"] = np.stack([f[k].reshape(J, 3).T for k in ("L0_tok_ln0_g", "L0_tok_ln0_b")])
    r["ln1"] = np.stack([f[k].reshape(J, 2).T for k in ("L0_tok_ln1_g", "L0_tok_ln1_b")])
    r["ln1c"] = np.stack([f["L0_tok_ln1_g"], f["L0_tok_ln1_b"]], axis=1)
    r["out_w"], r["out_b"] = f["L0_tok_out_w"], f["L0_tok_out_b"]
    cw = np.zeros((65, 5, D), np.float32)
    cw[:64] = f["L0_attn_conv_w"].transpose(1, 2, 0)
    cw[64, 4] = f["L0_attn_conv_b"]
    r["a_conv"], r["a_beta"] = cw, f["L0_attn_sqrt_beta"].reshape(D)
    w = np.zeros((65, 576), np.float32)
    for n, k in enumerate("qk"):
        for h in range(H0):
            at = 256 * n + 128 * (h // 4) + 32 * (h % 4)
            w[:64, at:at + DK] = f[f"L0_attn_{k}_w"].T[:, DK * h:DK * h + DK]
            w[64, at:at + DK] = f[f"L0_attn_{k}_b"][DK * h:DK * h + DK]
    w[:64, 512:], w[64, 512:] = f["L0_attn_v_w"].T, f["L0_attn_v_b"]
    r["a_w"] = w
    r["a_lnw"] = np.concatenate([f["L0_attn_ln_w"], np.ones(1, np.float32)])[:, None]
    r["a_lnb"] = np.concatenate([np.zeros((64, 64), np.float32), f["L0_attn_ln_b"][:, None]], axis=1)
    r["a_wo"] = np.concatenate([f["L0_attn_out_w"].T, f["L0_attn_out_b"][None]], axis=0)
    r["a_gam"] = f["L0_attn_gammas"].reshape(H0)
    qh, kk = np.arange(HALF)[:, None], np.arange(T)[None]
    low = np.where(kk[:, :HALF] <= qh, qh - kk[:, :HALF], -1)
    high = np.where(kk <= qh + HALF, qh + HALF - kk, -1)
    both = np.concatenate([np.tile(low, (2, H0)), np.tile(high, (2, H0))], axis=1)
    r["c_pos"] = np.maximum(both, 0).astype(np.float32)
    masked = np.where(both < 0, -1e30, 0.0).astype(np.float32)
    r["c_maskl"], r["c_maskh"] = masked[:, :SL], masked[:, SL:SL + 512]
    cont = np.ones(SA, np.float32)
    cont[HALF - 1:SL:HALF] = 0
    cont[SL + T - 1::T] = 0
    r["c_cont"] = cont
    rowm = np.ones((128, 16), np.float32)
    rowm[0::64, 0:8] = 0
    r["c_rowm"] = rowm
    w1 = np.zeros((128, NEXP // 2, 128), np.float32)
    w2 = np.zeros((128, NEXP // 2, D), np.float32)
    sel = np.zeros((128, NEXP // 2, 128), np.float32)
    for e in range(NEXP):
        w1[:64, e // 2, 64 * (e % 2):64 * (e % 2) + 64] = f["L0_ffn_w1"][e]
        w1[64, e // 2, 64 * (e % 2):64 * (e % 2) + 64] = f["L0_ffn_b1"][e]
        w2[64 * (e % 2):64 * (e % 2) + 64, e // 2] = f["L0_ffn_w2"][e]
        for n in range(3):
            sel[96 + NEXP * n + e, e // 2, 64 * (e % 2):64 * (e % 2) + 64] = 1
    r["m_w1"], r["m_w2"], r["c_sel"] = w1, w2, sel
    b2 = np.zeros((128, D), np.float32)
    for n in range(3):
        b2[96 + NEXP * n:96 + NEXP * n + NEXP] = f["L0_ffn_b2"]
    router = np.zeros((128, NEXP), np.float32)
    router[:64] = f["L0_ffn_router_w"].T
    r["m_b2"], r["m_router"] = b2, router
    r["c_iota"] = np.broadcast_to(np.arange(NEXP, dtype=np.float32), (128, 2, NEXP))
    tok = np.zeros((128, 2, 128), np.float32)
    tok[:, :, 64] = 1
    r["c_tok"] = tok
    r["w_qkv"] = np.concatenate([f["L1_attn_W_Q"].T, f["L1_attn_W_K"].T, f["L1_attn_W_V"].T], axis=1)
    r["w_norm"] = np.concatenate([f["L1_attn_wq"].reshape(-1), f["L1_attn_wk"], f["L1_attn_wv"]])
    p = np.arange(128)
    theta = 10000.0 ** (-2.0 * np.arange(ROT // 2) / ROT)
    tq = (p % 64)[:, None] + 64 * np.repeat(np.arange(2), NH1 + 2)[None]
    n = np.arange(NBLK)
    to = (p % QB)[:, None] + (64 * (n // 4) + QB * (n % 2))[None]
    for name, tt in (("q", tq), ("o", to)):
        ang = (tt[:, :, None].astype(np.float32) * theta[None, None].astype(np.float32)).astype(np.float32)
        r["c_cos" + name], r["c_sin" + name] = np.cos(ang).astype(np.float32), np.sin(ang).astype(np.float32)
    key = to[:, :, None] - (p % QB)[:, None, None] - WIN + np.arange(KW)[None, None]
    ok = (key <= to[:, :, None]) & (key >= to[:, :, None] - (WIN - 1)) & (key >= 0)
    r["c_maskw"] = np.where(ok, 0.0, -1e30).reshape(128, NBLK * KW).astype(np.float32)
    wg = np.zeros((C1, NH1, 65), np.float32)
    for h in range(NH1):
        w = f[f"L1_attn_Wg{h // 2}"]
        wg[:, h, :64] = w[:, 64 * (h % 2):64 * (h % 2) + 64]
        if h % 2 == 0:
            wg[:, h, 64] = f[f"L1_attn_bg{h // 2}"]
    r["w_g"] = wg
    r["w_o"] = f["L1_attn_Wout"].T.reshape(2, 64, D).transpose(1, 0, 2)
    bout = np.zeros((65, NH1, D), np.float32)
    bout[64, 0] = f["L1_attn_bout"]
    r["w_bout"] = bout
    wr = np.zeros((NRT + 1, 128, 2, HID + 1), np.float32)
    wr[:NRT, :, :, :HID] = f["L1_ffn_Wr"].transpose(1, 3, 0, 2)
    wr[:NRT, :, :, HID] = f["L1_ffn_br"].transpose(1, 2, 0)
    r["r_wr"] = wr.reshape(NRT + 1, 128, 2 * (HID + 1))
    r["r_ws"] = np.concatenate([f["L1_ffn_Ws"][:, 0].transpose(2, 0, 1), f["L1_ffn_bs"][:, 0].T[:, :, None]], axis=2)
    eye = np.zeros((128, 2, HID + 1), np.float32)
    eye[:, :, :HID] = np.eye(HID)[:, None]
    r["c_eye"] = eye
    r["r_wi"], r["r_bi"] = f["L1_ffn_Wi"].T, f["L1_ffn_bi"][:, None]
    r["r_wo"], r["r_bo"] = f["L1_ffn_Wo"].T, f["L1_ffn_bo"][None]
    r["r_route"] = f["L1_ffn_route_id"][None]
    r["c_ident"] = np.eye(128, dtype=np.float32)
    return {k: np.ascontiguousarray(v) for k, v in r.items()}


def kernel(**inputs):
    import numpy as _np
    import concourse.bacc as _bacc
    from concourse import mybir as _mybir
    from concourse.bass_utils import run_bass_kernel_spmd as _run

    nc = _bacc.Bacc("TRN2", target_bir_lowering=False, num_devices=1)
    host = _host_constants(inputs)
    arrays, args = {}, {}
    for name, v in host.items():
        arrays[f"in_{name}_dram"] = v
        args[name] = nc.dram_tensor(f"in_{name}_dram", v.shape, _mybir.dt.from_np(v.dtype), kind="ExternalInput").ap()
    out = nc.dram_tensor("out_0_dram", (B, T, D), F32, kind="ExternalOutput").ap()
    tower(nc, args, out)
    r = _run(nc, [arrays], core_ids=[0])
    return r.results[0]["out_0_dram"]
```
